# Optimizing a Trainium2 kernel written in Bass

```python
import numpy as np
import jax
import jax.numpy as jnp

def _softmax(x, axis=-1):
    return jax.nn.softmax(x, axis=axis)

def _gelu(x):
    return jax.nn.gelu(x, approximate=True)

def _silu(x):
    return jax.nn.silu(x)

def _sigmoid(x):
    return jax.nn.sigmoid(x)

def _layernorm(x, axis=-1, eps=1e-05):
    m = jnp.mean(x, axis=axis, keepdims=True)
    v = jnp.var(x, axis=axis, keepdims=True)
    return (x - m) / jnp.sqrt(v + eps)

def _scatter_add(tgt, idx, src, axis=0):
    return tgt.at[idx].add(src)

def _segment_sum(src, seg, n):
    return jax.ops.segment_sum(src, seg, n)
kernel_name = 'mk_xattn_ffn_d1_seqx_r4_eaa9a5'

def setup_inputs(seed: int=0):
    np.random.seed(seed)
    _w = jnp.asarray

    def _rec_inputs():
        import jax
        import jax.numpy as jnp
        _rk = jax.random.key(seed)
        x = 0.002226 + 0.9996 * jax.random.normal(jax.random.fold_in(_rk, 1), (16, 128, 256), jnp.float32)
        _lenS = 128 - jax.random.randint(jax.random.fold_in(_rk, 7), (16,), 0, max(1, 128 // 4) + 1, jnp.int32)
        _lenS2 = 128 - jax.random.randint(jax.random.fold_in(_rk, 8), (16,), 0, max(1, 128 // 4) + 1, jnp.int32)
        _ctx_1024P = jax.random.normal(jax.random.fold_in(_rk, 11), (16, 16, 256), jnp.float32)
        _ctx_1024c = jax.random.dirichlet(jax.random.fold_in(_rk, 511), 0.3 * jnp.ones((16,), jnp.float32), (16, 128))
        _ctx_1024t = jnp.einsum('bsk,bkd->bsd', _ctx_1024c, _ctx_1024P)
        _ctx_1024t = _ctx_1024t * jax.lax.rsqrt(jnp.mean(jnp.square(_ctx_1024t)) + 1e-12) * 0.953939
        ctx_1024 = -7.10856e-05 + 0.999911 * (_ctx_1024t + 0.3 * jax.random.normal(jax.random.fold_in(_rk, 611), (16, 128, 256), jnp.float32))
        return (x, ctx_1024)
    x, ctx_1024 = _rec_inputs()

    def _L0_xattn_setup():
        import jax, jax.numpy as jnp
        import numpy as np
        DIM = 256
        HEAD_DIM = 64
        NUM_HEADS = 8
        INNER = HEAD_DIM * NUM_HEADS
        ROT_DIM = HEAD_DIM
        ROPE_BASE = 10000.0
        EPS = 1e-05

        def layer_norm(x, g, b):
            mu = jnp.mean(x, axis=-1, keepdims=True)
            var = jnp.var(x, axis=-1, keepdims=True)
            return (x - mu) * jax.lax.rsqrt(var + EPS) * g + b

        def rope_rotate_k(k):
            n = k.shape[1]
            half = ROT_DIM // 2
            inv_freq = 1.0 / ROPE_BASE ** (jnp.arange(0, ROT_DIM, 2, dtype=jnp.float32) / ROT_DIM)
            theta = jnp.arange(n, dtype=jnp.float32)[:, None] * inv_freq[None, :]
            angles = jnp.concatenate([theta, theta], axis=-1)
            cos = jnp.cos(angles)[None, :, None, :].astype(k.dtype)
            sin = jnp.sin(angles)[None, :, None, :].astype(k.dtype)
            k_rope, k_pass = (k[..., :ROT_DIM], k[..., ROT_DIM:])
            neg_half = jnp.concatenate([-k_rope[..., half:], k_rope[..., :half]], axis=-1)
            k_rope = k_rope * cos + neg_half * sin
            return jnp.concatenate([k_rope, k_pass], axis=-1)
        key = jax.random.key(seed)
        ks = jax.random.split(key, 5)
        b, n, m = (8, 2048, 64)
        s = 1.0 / np.sqrt(DIM)
        return {'x': jax.random.normal(ks[0], (b, n, DIM), jnp.float32), 'latents': jax.random.normal(ks[1], (b, m, DIM), jnp.float32), 'gamma_x': jnp.ones((DIM,), jnp.float32), 'beta_x': jnp.zeros((DIM,), jnp.float32), 'gamma_l': jnp.ones((DIM,), jnp.float32), 'beta_l': jnp.zeros((DIM,), jnp.float32), 'Wq': jax.random.normal(ks[2], (DIM, INNER), jnp.float32) * s, 'Wkv': jax.random.normal(ks[3], (DIM, 2 * INNER), jnp.float32) * s, 'Wo': jax.random.normal(ks[4], (INNER, DIM), jnp.float32) * (1.0 / np.sqrt(INNER))}
    _L0_xattn_all = _L0_xattn_setup()
    _L0_xattn_in = {k: v for k, v in _L0_xattn_all.items() if k in ('gamma_x', 'beta_x', 'gamma_l', 'beta_l', 'Wq', 'Wkv', 'Wo')}
    del _L0_xattn_all

    def _L0_ffn_setup():
        import jax, jax.numpy as jnp
        import numpy as np
        B, S, D, F, E = (8, 256, 256, 1024, 8)
        EPS = 1e-05
        key = jax.random.key(seed)
        ks = jax.random.split(key, 4)
        s = 0.02
        return {'input_features': jax.random.normal(ks[0], (B, S, D), jnp.float32), 'centroids': jax.random.normal(ks[1], (E, D), jnp.float32) * 0.1, 'ln_g': jnp.ones((E, D), jnp.float32), 'ln_b': jnp.zeros((E, D), jnp.float32), 'w1': jax.random.normal(ks[2], (E, D, F), jnp.float32) * s, 'b1': jnp.zeros((E, F), jnp.float32), 'w2': jax.random.normal(ks[3], (E, F, D), jnp.float32) * s, 'b2': jnp.zeros((E, D), jnp.float32)}
    _L0_ffn_all = _L0_ffn_setup()
    _L0_ffn_in = {k: v for k, v in _L0_ffn_all.items() if k in ('centroids', 'ln_g', 'ln_b', 'w1', 'b1', 'w2', 'b2')}
    del _L0_ffn_all
    return {'x': x, 'ctx_1024': ctx_1024, 'L0_xattn_gamma_x': _L0_xattn_in['gamma_x'], 'L0_xattn_beta_x': _L0_xattn_in['beta_x'], 'L0_xattn_gamma_l': _L0_xattn_in['gamma_l'], 'L0_xattn_beta_l': _L0_xattn_in['beta_l'], 'L0_xattn_Wq': _L0_xattn_in['Wq'], 'L0_xattn_Wkv': _L0_xattn_in['Wkv'], 'L0_xattn_Wo': _L0_xattn_in['Wo'], 'L0_ffn_centroids': _L0_ffn_in['centroids'], 'L0_ffn_ln_g': _L0_ffn_in['ln_g'], 'L0_ffn_ln_b': _L0_ffn_in['ln_b'], 'L0_ffn_w1': _L0_ffn_in['w1'], 'L0_ffn_b1': _L0_ffn_in['b1'], 'L0_ffn_w2': _L0_ffn_in['w2'], 'L0_ffn_b2': _L0_ffn_in['b2']}

def reference(x, ctx_1024, L0_xattn_gamma_x, L0_xattn_beta_x, L0_xattn_gamma_l, L0_xattn_beta_l, L0_xattn_Wq, L0_xattn_Wkv, L0_xattn_Wo, L0_ffn_centroids, L0_ffn_ln_g, L0_ffn_ln_b, L0_ffn_w1, L0_ffn_b1, L0_ffn_w2, L0_ffn_b2):
    import jax
    import jax.numpy as jnp

    def _L0_xattn_ref(x, latents, gamma_x, beta_x, gamma_l, beta_l, Wq, Wkv, Wo):
        import jax, jax.numpy as jnp
        import numpy as np
        DIM = 256
        HEAD_DIM = 64
        NUM_HEADS = 8
        INNER = HEAD_DIM * NUM_HEADS
        ROT_DIM = HEAD_DIM
        ROPE_BASE = 10000.0
        EPS = 1e-05

        def layer_norm(x, g, b):
            mu = jnp.mean(x, axis=-1, keepdims=True)
            var = jnp.var(x, axis=-1, keepdims=True)
            return (x - mu) * jax.lax.rsqrt(var + EPS) * g + b

        def rope_rotate_k(k):
            n = k.shape[1]
            half = ROT_DIM // 2
            inv_freq = 1.0 / ROPE_BASE ** (jnp.arange(0, ROT_DIM, 2, dtype=jnp.float32) / ROT_DIM)
            theta = jnp.arange(n, dtype=jnp.float32)[:, None] * inv_freq[None, :]
            angles = jnp.concatenate([theta, theta], axis=-1)
            cos = jnp.cos(angles)[None, :, None, :].astype(k.dtype)
            sin = jnp.sin(angles)[None, :, None, :].astype(k.dtype)
            k_rope, k_pass = (k[..., :ROT_DIM], k[..., ROT_DIM:])
            neg_half = jnp.concatenate([-k_rope[..., half:], k_rope[..., :half]], axis=-1)
            k_rope = k_rope * cos + neg_half * sin
            return jnp.concatenate([k_rope, k_pass], axis=-1)
        b, n, _ = x.shape
        m = latents.shape[1]
        h, d = (NUM_HEADS, HEAD_DIM)
        scale = d ** (-0.5)
        xn = layer_norm(x, gamma_x, beta_x)
        ln = layer_norm(latents, gamma_l, beta_l)
        q = (ln @ Wq).reshape(b, m, h, d)
        kv_x = xn @ Wkv
        k_x, v_x = (kv_x[..., :INNER], kv_x[..., INNER:])
        kv_l = ln @ Wkv
        k_l, v_l = (kv_l[..., :INNER], kv_l[..., INNER:])
        k_x = k_x.reshape(b, n, h, d)
        v_x = v_x.reshape(b, n, h, d)
        k_x = rope_rotate_k(k_x)
        q = jnp.transpose(q, (0, 2, 1, 3)) * scale
        k_x = jnp.transpose(k_x, (0, 2, 1, 3))
        v_x = jnp.transpose(v_x, (0, 2, 1, 3))
        k_l = jnp.transpose(k_l.reshape(b, m, h, d), (0, 2, 1, 3))
        v_l = jnp.transpose(v_l.reshape(b, m, h, d), (0, 2, 1, 3))
        k = jnp.concatenate([k_x, k_l], axis=2)
        v = jnp.concatenate([v_x, v_l], axis=2)
        sim = jnp.einsum('bhid,bhjd->bhij', q, k)
        attn = jax.nn.softmax(sim, axis=-1)
        out = jnp.einsum('bhij,bhjd->bhid', attn, v)
        out = jnp.transpose(out, (0, 2, 1, 3)).reshape(b, m, INNER)
        return out @ Wo

    def _L0_ffn_ref(input_features, centroids, ln_g, ln_b, w1, b1, w2, b2):
        import jax, jax.numpy as jnp
        import numpy as np
        B, S, D, F, E = (8, 256, 256, 1024, 8)
        EPS = 1e-05
        x = input_features.reshape(-1, D)
        aff = jax.lax.stop_gradient(x @ centroids.T)
        eid = jnp.argmax(aff, axis=-1)
        alpha = jax.nn.sigmoid(jnp.sum(x * centroids[eid], axis=-1, keepdims=True))
        mu = jnp.mean(x, axis=-1, keepdims=True)
        var = jnp.mean((x - mu) ** 2, axis=-1, keepdims=True)
        xn = (x - mu) * jax.lax.rsqrt(var + EPS)
        xln = xn * ln_g[eid] + ln_b[eid]
        onehot = jax.nn.one_hot(eid, E, dtype=x.dtype)
        ffn = jnp.zeros_like(x)
        for e in range(E):
            h = jax.nn.relu(xln @ w1[e] + b1[e])
            ffn = ffn + onehot[:, e:e + 1] * (h @ w2[e] + b2[e])
        out = x + alpha * ffn
        return out.reshape(input_features.shape)
    x = x + _L0_xattn_ref(ctx_1024, _layernorm(x, axis=-1), L0_xattn_gamma_x, L0_xattn_beta_x, L0_xattn_gamma_l, L0_xattn_beta_l, L0_xattn_Wq, L0_xattn_Wkv, L0_xattn_Wo)
    x = x + _L0_ffn_ref(_layernorm(x, axis=-1), L0_ffn_centroids, L0_ffn_ln_g, L0_ffn_ln_b, L0_ffn_w1, L0_ffn_b1, L0_ffn_w2, L0_ffn_b2)
    return x

_drawn_inputs = setup_inputs


def setup_inputs(seed=0):
    import zlib

    import numpy as np

    out = dict(_drawn_inputs(seed))
    spreads = {'L0_xattn_gamma_x': (1.0, 0.2),
     'L0_xattn_beta_x': (0.0, 0.1),
     'L0_xattn_gamma_l': (1.0, 0.2),
     'L0_xattn_beta_l': (0.0, 0.1),
     'L0_ffn_ln_g': (1.0, 0.6),
     'L0_ffn_ln_b': (0.0, 0.8),
     'L0_ffn_b1': (0.0, 0.406),
     'L0_ffn_b2': (0.0, 0.1)}
    factors = {}
    for name, (base, spread) in spreads.items():
        noise = np.random.default_rng([zlib.crc32(name.encode()), seed]).standard_normal(out[name].shape)
        drawn = base * np.exp(spread * noise) if base else spread * noise
        out[name] = jnp.asarray(drawn.astype(out[name].dtype))
    for name, factor in factors.items():
        out[name] = (out[name] * factor).astype(out[name].dtype)
    return out
```

```python
from contextlib import ExitStack

import concourse.bass as bass
from concourse import mybir

F32 = mybir.dt.float32
F16 = mybir.dt.float16
I32 = mybir.dt.int32
U32 = mybir.dt.uint32
ALU = mybir.AluOpType
ACT = mybir.ActivationFunctionType
AX_X = mybir.AxisListType.X

P = 128
EPS = 1e-5
W_SCALE = 64.0
W_INV = 1.0 / W_SCALE


class Step:

    def __init__(self, s, batches, it=None):
        self.s, self.batches, self.it = s, batches, it

    def has(self, lag):
        return self.it is not None or 0 <= self.s - lag < self.batches

    def par(self, lag):
        return (self.s - lag) % 2

    def batch(self, lag):
        b = self.s - lag
        return b if self.it is None else b + self.it * 2

    def n(self, lag, per=1, k=None, ring=1):
        v = per * ((self.s - lag) // ring) + (per if k is None else k)
        return v if self.it is None else v + self.it * (2 // ring * per)


def xattn_moe_kernel(nc, x, ctx_in, gamma_x, beta_x, gamma_l, beta_l, wq, wkv, wo, cent, ln_g, ln_b,
                     w1, b1, w2, b2, rope_cos, rope_sin, ident_c, tri_c, cols_c, tabs_c, basee_c, ids_c, empty_c, out):
    B, T, D = x.shape
    INNER = wq.shape[1]
    DH = 64
    H = INNER // DH
    E, _, FF = w1.shape
    KD = D // P
    NB = INNER // P
    FB = FF // P
    TOK = B * T
    TILES = TOK // P + E - 1
    NT = TILES + 1
    REGION = TOK
    TABLE = (E * REGION // P + NT) * P
    REC = 2 * D + 4
    ALPHA, INV2 = 2 * D, 2 * D + 1
    OOB = 2 * TOK
    assert T == P and KD == 2 and NB == 4 and H == 8 and FB == 8 and B == 2 * E

    L, PJ, AT, WR, RT, SC = -1, 0, 1, 2, 3, 4
    LOOP_FROM, LOOP_TO = 4, 14
    T_FROM, T_TO = 6, TILES - 1
    assert (T_TO - T_FROM) % 4 == 0

    xf = x.rearrange("b t d -> (b t) d")
    cf = ctx_in.rearrange("b t d -> (b t) d")
    outf = out.rearrange("b t d -> (b t) d")
    x_b = xf.rearrange("(b p) d -> b p d", p=P)
    c_b = cf.rearrange("(b p) d -> b p d", p=P)
    w1_g = w1.rearrange("e (k p) f -> (e k) p f", p=P)
    w2_g = w2.rearrange("e (h f p) d -> (e h) p f d", h=2, p=P)
    GRP = FF

    with ExitStack() as es:
        def sb(name, shape, dt):
            return es.enter_context(nc.sbuf_tensor(name, shape, dt))

        def pb(name):
            return es.enter_context(nc.psum_tensor(name, [P, 512], F32))

        def sem(name):
            return es.enter_context(nc.semaphore(name))

        rec_dram = nc.dram_tensor("rec_dram", [TOK, REC], F32).ap()
        ids_dram = nc.dram_tensor("ids_dram", [TABLE, 1], I32).ap()
        rec_b = rec_dram.rearrange("(b p) r -> b p r", p=P)

        w1h = sb("w1h", [P, E, KD * FF], F16)
        w1l = sb("w1l", [P, E, KD * FF], F16)
        w2h = sb("w2h", [P, E, FB * D], F16)
        w2l = sb("w2l", [P, E, FB * D], F16)
        KV = 2 * INNER
        AW = KD * INNER + KD * KV + KD * INNER + NB * D
        aw = [sb("awh", [P, AW], F16), sb("awl", [P, AW], F16)]
        o_q, o_kv, o_rot, o_wo = 0, KD * INNER, KD * (INNER + KV), KD * (INNER + KV + INNER)
        wq_s = [a[:, o_q:o_kv].rearrange("p (k n) -> p k n", k=KD) for a in aw]
        wkv_s = [a[:, o_kv:o_rot].rearrange("p (k n) -> p k n", k=KD) for a in aw]
        rot_s = [a[:, o_rot:o_wo].rearrange("p (k n) -> p k n", k=KD) for a in aw]
        wo_s = [a[:, o_wo:AW].rearrange("p (k n) -> p k n", k=NB) for a in aw]
        stage = [sb(f"stage{i}", [P, GRP], F32) for i in range(2)]
        xc = [sb(f"xc{i}", [P, 2, D], F32) for i in range(2)]
        lnT = [sb(f"lnT{h}", [P, KD, 2 * P], F16) for h in "hl"]
        qT = [sb(f"qT{h}", [P, NB, P], F16) for h in "hl"]
        kT_all = sb("kT", [P, 4, NB * 2 * P], F16)
        kT = [[kT_all[:, 2 * h + i, :].rearrange("p (n s t) -> p n s t", n=NB, s=2) for i in range(2)]
              for h in range(2)]
        v = [[sb(f"v{h}{i}", [P, 2, INNER], F16) for i in range(2)] for h in "hl"]
        k_cos = sb("k_cos", [P, NB, P], F32)
        k_sin = sb("k_sin", [P, NB, P], F32)
        lnT32 = k_sin[:, :, :].rearrange("p b t -> p (b t)")
        cos_t = sb("cos_t", [P, P], F32)
        sin_t = sb("sin_t", [P, P], F32)
        probs = [sb(f"probs{i}", [P, 2, 2 * P], F32) for i in range(2)]
        pT = [[sb(f"pT{h}{i}", [P, 4 * P], F16) for i in range(2)] for h in "hl"]
        attn = sb("attn", [P, INNER], F32)
        aT = [sb(f"aT{h}", [P, NB, P], F16) for h in "hl"]
        rec = [sb(f"rec{i}", [P, REC], F32) for i in range(2)]
        x1 = [r[:, D:2 * D] for r in rec]
        fT = sb("fT", [P, D], F32)
        ident = sb("ident", [P, P], F32)
        tri = sb("tri", [P, 2, P], F16)
        cols = sb("cols", [P, 16], F32)
        tabs = stage[1][:, 0:16 + E * E + 1]
        b1_r = stage[0][0:E, 0:FF]
        lngb_r = stage[1][0:E, 128:128 + 2 * D]
        b2_r = stage[1][0:E, 128 + 2 * D:128 + 3 * D]
        basee = sb("basee", [P, 2, E], F32)
        rowt = attn[0:8 + E * KD, 0:P]
        colt = sb("colt", [P, 8 + E * KD], F32)
        small = sb("small", [P, 120], F32)
        at = [0]

        def few(n):
            a = small[:, at[0]:at[0] + n]
            at[0] += n
            return a

        nmax = [few(2) for _ in range(2)]
        rsum = [few(H) for _ in range(2)]
        rinv = few(H)
        lst = few(12).rearrange("p (a b) -> p a b", a=2)
        mv = few(6).rearrange("p (a b) -> p a b", a=3)
        norms = few(24)
        fst, top8, eidf = few(6), few(8), few(1)
        place, placef, ealpha = few(2 * E).rearrange("p (a e) -> p a e", a=2), few(1), few(2)
        nmean, r1, r2, s2 = norms[:, 0:3], norms[:, 3:6], norms[:, 6:9], norms[:, 9:12]
        nv, nu, ninv2 = norms[:, 12:15], norms[:, 15:18], norms[:, 18:19]
        idx8 = sb("idx8", [P, 8], U32)
        oneh = sb("oneh", [P, E], F16)
        ohcum = [sb(f"ohcum{i}", [P, E], F16) for i in range(2)]
        placei = sb("placei", [P, 1], I32)
        tokid = sb("tokid", [P, 1], I32)
        oob = attn[:, P:P + TABLE // P].bitcast(I32)
        tile_e = sb("tile_e", [1, P], I32)
        tile_r = sb("tile_r", [P, 1], I32)
        idt = sb("idt", [P, NT], I32)

        def over(t, lo, n):
            return t[:, lo:lo + n].bitcast(F32)
        W1 = KD * FF
        w1c = [[kT_all[:, 0:2, :].rearrange("p a n -> p (a n)"), kT_all[:, 2:4, :].rearrange("p a n -> p (a n)")],
               [aw[0][:, 0:W1], aw[1][:, 0:W1]]]
        g_rec = [over(aw[i // 2], W1 + (i % 2) * 2 * REC, 2 * REC) for i in range(4)]
        yout = [over(aw[i], W1 + 4 * REC, 2 * D) for i in range(2)]
        xg, ybase = attn[:, 0:D], attn[:, D:2 * D]
        hid32 = [k_cos, k_sin]
        xgT = [lnT[i][:, 0, :].rearrange("p (k t) -> p k t", k=KD) for i in range(2)]
        hid = [[v[i][j][:, :, :].rearrange("p a (c t) -> p (a c) t", t=P) for j in range(2)] for i in range(2)]
        NCOL = 2 * KD + FB
        tile_c = probs[0][:, :, :].rearrange("p a b -> p (a b)")[:, 0:NCOL * NT].rearrange("p (c t) -> p c t", c=NCOL)
        oh_t = probs[1][:, 0, 0:E]
        oh_e = probs[1][0:E, 0, 128:256]
        oh_eh = pT[0][0][0:E, 0:P]
        ef_t = probs[1][:, 0, 16:17]
        ids_t = probs[1][0:NT, 1, 0:P].bitcast(I32)
        ids_f = probs[1][0:NT, 1, P:2 * P]
        b2_s = [pT[1][i][0:E, 0:D] for i in range(2)]
        rt = attn[:, :]

        ps_s = es.enter_context(nc.psum_tensor("ps_s", [P, 2, 512], F32))
        ps_t = [pb(f"ps_t{i}") for i in range(2)]
        ps_u = [pb(f"ps_u{i}") for i in range(3)]
        ps_o = pb("ps_o")
        ps_h = [[ps_s[:, i, :] for i in range(2)], [t[:, :] for t in ps_t]]

        consts_in = sem("consts_in")
        first_in = sem("first_in")
        xc_in = [sem(f"xc_in{i}") for i in range(2)]
        x1_in = [sem(f"x1_in{i}") for i in range(2)]
        stage_in = [sem(f"stage_in{i}") for i in range(2)]
        rowt_in = sem("rowt_in")
        table_init = sem("table_init")
        rec_stored = sem("rec_stored")
        ids_scattered = sem("ids_scattered")
        aw_high = sem("aw_high")
        aw_split = sem("aw_split")
        rot_made = sem("rot_made")
        w_high = sem("w_high")
        w_scaled = sem("w_scaled")
        w_split = sem("w_split")
        setup_dve = sem("setup_dve")
        colt_ps = sem("colt_ps")
        colt_ready = sem("colt_ready")
        in_bn = sem("in_bn")
        in_stats = sem("in_stats")
        norm_seq = sem("norm_seq")
        xn_ready = sem("xn_ready")
        lnT_ready = sem("lnT_ready")
        lnT_affine = sem("lnT_affine")
        lnT_high = sem("lnT_high")
        lnT_split = sem("lnT_split")
        kx_ready, kx_cos = sem("kx_ready"), sem("kx_cos")
        rot_ready, rot_sin = sem("rot_ready"), sem("rot_sin")
        kx_sum, kx_high, kx_split = sem("kx_sum"), sem("kx_high"), sem("kx_split")
        kl_ready, kl_high, kl_split = sem("kl_ready"), sem("kl_high"), sem("kl_split")
        vx_ready, vx_high, vx_split = sem("vx_ready"), sem("vx_high"), sem("vx_split")
        vl_ready, vl_high, vl_split = sem("vl_ready"), sem("vl_high"), sem("vl_split")
        q_ready, q_high, q_split = sem("q_ready"), sem("q_high"), sem("q_split")
        scores_ready = sem("scores_ready")
        nmax_ready = sem("nmax_ready")
        probs_ready = sem("probs_ready")
        pT_ready, pT_high, pT_split = sem("pT_ready"), sem("pT_high"), sem("pT_split")
        pv_done = sem("pv_done")
        rinv_ready = sem("rinv_ready")
        attn_ready = sem("attn_ready")
        aT_ready, aT_high, aT_split = sem("aT_ready"), sem("aT_high"), sem("aT_split")
        y_ready = sem("y_ready")
        x1_ready, x1_bn, x1_stats = sem("x1_ready"), sem("x1_bn"), sem("x1_stats")
        f2_ready = sem("f2_ready")
        fT_ready, fT_copied = sem("fT_ready"), sem("fT_copied")
        aff_ready = sem("aff_ready")
        route_seq = sem("route_seq")
        ealpha_ready = sem("ealpha_ready")
        alpha_seq = sem("alpha_seq")
        pref_ready = sem("pref_ready")
        place_seq = sem("place_seq")
        counts_ps = sem("counts_ps")
        tabs_in = sem("tabs_in")
        tile_seq = sem("tile_seq")
        tiles_ready = sem("tiles_ready")
        turned_ps = sem("turned_ps")
        turned = sem("turned")
        ids_in = sem("ids_in")
        idf_ready = sem("idf_ready")
        idt_ps = sem("idt_ps")
        idt_ready = sem("idt_ready")
        cols_ps = sem("cols_ps")
        cols_ready = sem("cols_ready")
        b2_high = sem("b2_high")
        b2_split = sem("b2_split")
        buffers_clear = sem("buffers_clear")
        w1c_in = [sem(f"w1c_in{i}") for i in range(2)]
        g_in = [sem(f"g_in{i}") for i in range(4)]
        xgT_ps, xg_ready, xgT_high, xgT_split = sem("xgT_ps"), sem("xg_ready"), sem("xgT_high"), sem("xgT_split")
        hid_ps, hid_biased, hid_high, hid_split = sem("hid_ps"), sem("hid_biased"), sem("hid_high"), sem("hid_split")
        y2_ps, y2_base, y2_out = sem("y2_ps"), sem("y2_base"), sem("y2_out")
        out_stored = [sem(f"out_stored{i}") for i in range(4)]

        NO_N, RO_N, PL_N, AL_N = 9, 6, 5, 2
        N_FIRST, N_CONST = 16 * 2, 16 * 6

        UNITS = [("kx", PJ, kx_cos, 1), ("rot", PJ, rot_sin, 1), ("kl", PJ, kl_split, 1), ("fT", RT, fT_copied, 1),
                 ("vx", PJ, vx_split, 1), ("aff", RT, route_seq, RO_N), ("vl", PJ, vl_split, 1),
                 ("aT", WR, aT_split, 1), ("q", PJ, q_split, 1), ("lnT", L, lnT_split, 1),
                 ("y", WR, x1_ready, 1), ("pref", RT, place_seq, PL_N)]
        ORDER = [u[0] for u in UNITS]

        def bank(name):
            return ps_u[ORDER.index(name) % 3]

        def wait_alone(eng, s, n):
            eng.wait_ge(s, n)
            eng.nop(nofuse=True)

        def pipeline(eng, step, last=B + RT):
            for s in range(-1, LOOP_FROM):
                step(Step(s, B))
            with eng.Fori(0, (LOOP_TO - LOOP_FROM) // 2) as it:
                for u in range(2):
                    step(Step(LOOP_FROM + u, B, it))
            for s in range(LOOP_TO, last):
                step(Step(s, B))

        block = es.enter_context(nc.Block())

        @block.sync
        def _(sp):
            def load_xc(b, par):
                sp.dma_start(xc[par][:, 0, :], c_b[b]).then_inc(xc_in[par], 16)
                sp.dma_start(xc[par][:, 1, :], x_b[b]).then_inc(xc_in[par], 16)

            load_xc(0, 0)
            sp.dma_start(cols[:, :], cols_c).then_inc(first_in, 16)
            sp.dma_start(ident[:, :], ident_c).then_inc(first_in, 16)
            for i, g in enumerate((gamma_x, gamma_l, beta_x, beta_l)):
                sp.dma_start(rowt[2 * i:2 * i + 2, :], g.rearrange("(k p) -> k p", p=P)).then_inc(rowt_in, 16)
            sp.dma_start(rowt[8:8 + E * KD, :], cent.rearrange("e (k p) -> (e k) p", p=P)).then_inc(rowt_in, 16)
            for k in range(KD):
                sp.dma_start(stage[k][:, :], wkv[k * P:(k + 1) * P, :]).then_inc(stage_in[k], 16)
            sp.dma_start(cos_t[:, :], rope_cos).then_inc(consts_in, 16)
            sp.dma_start(sin_t[:, :], rope_sin).then_inc(consts_in, 16)
            sp.dma_start(tri[:, :, :], tri_c).then_inc(consts_in, 16)
            sp.dma_start(basee[:, :, :], basee_c.partition_broadcast(P)).then_inc(consts_in, 16)
            sp.dma_start(tokid[:, :], ids_c).then_inc(consts_in, 16)
            sp.dma_start(oob[:, :], empty_c).then_inc(consts_in, 16)
            for i, src in enumerate((wq, wo)):
                src = src.rearrange("(k p) n -> p k n", p=P)
                sp.wait_ge(aw_split, i + 1)
                sp.dma_start(stage[i][:, :].rearrange("p (k n) -> p k n", k=src.shape[1]), src)\
                    .then_inc(stage_in[i], 16)
            sp.wait_ge(consts_in, N_CONST)
            sp.dma_start(ids_dram.rearrange("(p c) o -> p (c o)", p=P), oob[:, :]).then_inc(table_init, 16)

            def step(st):
                if st.has(L - 1):
                    if st.has(PJ):
                        wait_alone(sp, lnT_ready, st.n(PJ))
                    load_xc(st.batch(L - 1), st.par(L - 1))
                if st.has(PJ):
                    g = st.batch(PJ)
                    if st.has(PJ + 1):
                        wait_alone(sp, w_split, st.n(PJ + 1, 2, 1))
                    else:
                        wait_alone(sp, aw_split, 3)
                    sp.dma_start(stage[0][:, :], w1_g[g]).then_inc(stage_in[0], 16)
                    if st.has(PJ + 1):
                        wait_alone(sp, w_split, st.n(PJ + 1, 2, 2))
                    else:
                        wait_alone(sp, aw_split, 4)
                    sp.dma_start(stage[1][:, :].rearrange("p (f d) -> p f d", d=D), w2_g[g]).then_inc(stage_in[1], 16)
                if st.has(WR):
                    if st.has(WR + 2):
                        wait_alone(sp, rec_stored, st.n(WR + 2, 16))
                    sp.dma_start(x1[st.par(WR)], x_b[st.batch(WR)]).then_inc(x1_in[st.par(WR)], 16)
                if st.has(RT):
                    wait_alone(sp, f2_ready, st.n(RT))
                    wait_alone(sp, alpha_seq, st.n(RT, AL_N))
                    sp.dma_start(rec_b[st.batch(RT)], rec[st.par(RT)][:, :]).then_inc(rec_stored, 16)

            pipeline(sp, step)

            sp.wait_ge(w_split, 2 * B)
            sp.dma_start(tabs, tabs_c.partition_broadcast(P)).then_inc(tabs_in, 16)
            sp.dma_start(b1_r, b1).then_inc(tabs_in, 16)
            sp.dma_start(lngb_r[:, 0:D], ln_g).then_inc(tabs_in, 16)
            sp.dma_start(lngb_r[:, D:2 * D], ln_b).then_inc(tabs_in, 16)
            sp.dma_start(b2_r, b2).then_inc(tabs_in, 16)

            sp.wait_ge(tiles_ready, 1)

            def copy_w1(t, par, free):
                e = sp.value_load(tile_e[0:1, bass.ds(t, 1)], min_val=0, max_val=E - 1)
                if free is not None:
                    wait_alone(sp, hid_ps, free)
                for i, w in enumerate((w1h, w1l)):
                    sp.dma_start(w1c[par][i], w[:, bass.ds(e, 1), :].rearrange("p a n -> p (a n)"))\
                        .then_inc(w1c_in[par], 16)

            for t in range(3):
                copy_w1(t, t % 2, 2 * (t - 1) if t >= 2 else None)
            with sp.Fori(0, (TILES - 3) // 2) as it:
                for t in (3, 4):
                    copy_w1(it * 2 + t, t % 2, it * 4 + 2 * (t - 1))
            for ring in range(4):
                sp.wait_ge(out_stored[ring], 16 * len(range(ring, TILES, 4)))

        @block.scalar
        def _(act):
            dsts = [wkv_s[0][:, 0, :], wkv_s[0][:, 1, :], wq_s[0], wo_s[0]]
            for i, dst in enumerate(dsts):
                act.wait_ge(stage_in[i % 2], 16 * (i // 2 + 1))
                src = stage[i % 2][:, :]
                if i >= 2:
                    src = src.rearrange("p (k n) -> p k n", k=dst.shape[1])
                act.activation(dst, src, ACT.Copy, scale=W_SCALE).then_inc(aw_high, 1)

            def high(ready, n, dst, src, scale, done):
                act.wait_ge(ready, n)
                act.activation(dst, src, ACT.Copy, scale=scale).then_inc(done, 1)

            def exp_pair(st, j):
                if st.has(AT):
                    act.wait_ge(nmax_ready, st.n(AT, 4, j + 1))
                    for i in range(2):
                        h = 2 * j + i
                        ins = act.activation(probs[j % 2][:, i, :], ps_s[:, i, 0:2 * P], ACT.Exp,
                                             bias=nmax[j % 2][:, i:i + 1],
                                             accum_out=rsum[st.par(AT)][:, h:h + 1])
                    ins.then_inc(probs_ready, 1)

            def pT_pair(st, lag, j):
                if st.has(lag):
                    high(pT_ready, st.n(lag, 4, j + 1), pT[0][j % 2][:, :], ps_t[j % 2][:, :], 1.0, pT_high)

            def w_group(st, i):
                if st.has(PJ):
                    g = st.batch(PJ)
                    wait_alone(act, stage_in[i], st.n(PJ, 16) + 32)
                    w = (w1h, w2h)[i][:, :, :].rearrange("p e (h n) -> p (e h) n", h=2)
                    act.activation(w[:, g, :], stage[i][:, :], ACT.Copy, scale=W_SCALE).then_inc(w_high, 1)

            def step(st):
                exp_pair(st, 0)
                w_group(st, 0)
                pT_pair(st, WR, 3)
                exp_pair(st, 1)
                if st.has(PJ):
                    high(kl_ready, st.n(PJ), kT[0][st.par(PJ)][:, :, 1, :],
                         bank("kl")[:, :].rearrange("p (b t) -> p b t", b=NB), W_INV, kl_high)
                if st.has(RT):
                    high(fT_ready, st.n(RT), fT[:, :], bank("fT")[:, 0:D], 1.0, fT_copied)
                pT_pair(st, AT, 0)
                if st.has(PJ):
                    high(vx_ready, st.n(PJ), v[0][st.par(PJ)][:, 0, :], bank("vx")[:, :], W_INV, vx_high)
                exp_pair(st, 2)
                if st.has(PJ):
                    high(vl_ready, st.n(PJ), v[0][st.par(PJ)][:, 1, :], bank("vl")[:, :], W_INV, vl_high)
                pT_pair(st, AT, 1)
                if st.has(WR):
                    high(aT_ready, st.n(WR), aT[0][:, :, :],
                         bank("aT")[:, :].rearrange("p (b t) -> p b t", b=NB), 1.0, aT_high)
                exp_pair(st, 3)
                if st.has(PJ):
                    high(q_ready, st.n(PJ), qT[0][:, :, :], bank("q")[:, :].rearrange("p (b t) -> p b t", b=NB),
                         W_INV * DH ** -0.5, q_high)
                if st.has(L):
                    if st.has(PJ):
                        act.wait_ge(kx_sum, st.n(PJ))
                    else:
                        act.wait_ge(colt_ready, 1)
                    act.wait_ge(lnT_ready, st.n(L))
                    for c in range(2 * KD):
                        k, src = c // 2, c % 2
                        g, b = colt[:, 2 * src + k:2 * src + k + 1], colt[:, 4 + 2 * src + k:4 + 2 * src + k + 1]
                        ins = act.activation(lnT32[:, c * P:(c + 1) * P], bank("lnT")[:, c * P:(c + 1) * P],
                                             ACT.Identity, bias=b, scale=g)
                    ins.then_inc(lnT_affine, 1)
                    high(lnT_affine, st.n(L), lnT[0][:, :, :], lnT32.rearrange("p (k t) -> p k t", k=KD), 1.0, lnT_high)
                if st.has(RT):
                    act.wait_ge(route_seq, st.n(RT, RO_N, 2))
                    act.wait_ge(norm_seq, st.n(L, NO_N))
                    act.activation(ealpha[:, 0:1], top8[:, 0:1], ACT.Exp, scale=ninv2).then_inc(ealpha_ready, 1)
                pT_pair(st, AT, 2)
                w_group(st, 1)

            pipeline(act, step)

            act.wait_ge(tabs_in, 80)
            act.activation(b2_s[0], b2_r, ACT.Copy, scale=W_SCALE).then_inc(b2_high, 1)

            def x_high(n):
                act.wait_ge(xg_ready, n)
                act.activation(xgT[0], xg.rearrange("p (k t) -> p k t", k=KD), ACT.Copy).then_inc(xgT_high, 1)

            def h_high(n, par):
                for hf in range(2):
                    act.wait_ge(hid_biased, n + hf)
                    act.activation(hid[0][par][:, 4 * hf:4 * hf + 4, :],
                                   hid32[hf][:, :, :], ACT.Relu).then_inc(hid_high, 1)

            x_high(1)
            for t in range(T_FROM):
                h_high(2 * t + 1, t % 2)
                x_high(t + 2)
            with act.Fori(0, (T_TO - T_FROM) // 4) as it:
                for t in range(T_FROM, T_FROM + 4):
                    h_high(it * 8 + (2 * t + 1), t % 2)
                    x_high(it * 4 + (t + 2))
            for t in range(T_TO, TILES):
                h_high(2 * t + 1, t % 2)
                if t + 1 < TILES:
                    x_high(t + 2)

        @block.gpsimd
        def _(pool):
            pool.wait_ge(first_in, N_FIRST)
            eps, mhalf, half, mone = (cols[:, i:i + 3] for i in (0, 3, 6, 9))

            def norm_scales(st):
                k = [0]

                def done(ins):
                    k[0] += 1
                    ins.then_inc(norm_seq, 1)

                def former():
                    pool.wait_ge(norm_seq, st.n(L, NO_N, k[0]))

                if st.has(L):
                    pool.wait_ge(in_stats, st.n(L, 2))
                if st.has(RT):
                    pool.wait_ge(x1_stats, st.n(RT))
                if st.has(RT + 1):
                    pool.wait_ge(ealpha_ready, st.n(RT + 1))
                done(pool.tensor_tensor(nv, mv[:, :, 1], eps, ALU.add))
                done(pool.tensor_tensor(nmean, mv[:, :, 0], mone, ALU.mult))
                former()
                done(pool.tensor_tensor(r1, nv, mhalf, ALU.pow))
                former()
                done(pool.tensor_tensor(nu[:, 1:3], mv[:, 1:3, 1], r1[:, 1:3], ALU.mult))
                former()
                done(pool.tensor_tensor(nv[:, 1:3], nu[:, 1:3], r1[:, 1:3], ALU.mult))
                former()
                done(pool.tensor_tensor(nu[:, 1:3], nv[:, 1:3], eps[:, 1:3], ALU.add))
                former()
                done(pool.tensor_tensor(r2[:, 1:3], nu[:, 1:3], mhalf[:, 1:3], ALU.pow))
                former()
                done(pool.tensor_tensor(s2[:, 1:3], r1[:, 1:3], r2[:, 1:3], ALU.mult))
                if st.has(RT):
                    pool.tensor_tensor(rec[st.par(RT)][:, INV2:INV2 + 1], nu[:, 2:3], half[:, 2:3], ALU.pow)
                wait_alone(pool, norm_seq, st.n(L, NO_N, k[0]))
                if st.has(RT):
                    r = rec[st.par(RT)]
                    pool.tensor_scalar(r[:, 0:D], x1[st.par(RT)], nmean[:, 2:3], s2[:, 2:3], ALU.add, ALU.mult)\
                        .then_inc(f2_ready, 1)
                    pool.wait_ge(f2_ready, st.n(RT))
                    done(pool.tensor_tensor(ninv2, r[:, INV2:INV2 + 1], mone[:, 0:1], ALU.mult))
                else:
                    done(pool.tensor_tensor(ninv2, mone[:, 0:1], mone[:, 0:1], ALU.mult))
                assert k[0] == NO_N

            def rope(st):
                if not st.has(PJ):
                    return
                pool.wait_ge(rot_sin, st.n(PJ))
                pool.tensor_tensor(k_cos[:, :, :], k_cos[:, :, :], k_sin[:, :, :], ALU.add).then_inc(kx_sum, 1)
                wait_alone(pool, kx_sum, st.n(PJ))
                pool.tensor_scalar(kT[0][st.par(PJ)][:, :, 0, :], k_cos[:, :, :], 1.0, 0.0, ALU.mult, ALU.add)\
                    .then_inc(kx_high, 1)

            def norm_inputs(st):
                if st.has(L):
                    c = xc[st.par(L)]
                    pool.tensor_scalar(c[:, 0, :], c[:, 0, :], nmean[:, 0:1], r1[:, 0:1], ALU.add, ALU.mult)
                    pool.tensor_scalar(c[:, 1, :], c[:, 1, :], nmean[:, 1:2], s2[:, 1:2], ALU.add, ALU.mult)\
                        .then_inc(xn_ready, 1)

            def w_low(st, i):
                if not st.has(PJ):
                    return
                g = st.batch(PJ)
                wh = (w1h, w2h)[i][:, :, :].rearrange("p e (h n) -> p (e h) n", h=2)
                wl = (w1l, w2l)[i][:, :, :].rearrange("p e (h n) -> p (e h) n", h=2)
                wait_alone(pool, w_high, st.n(PJ, 2, i + 1))
                pool.tensor_scalar(stage[i][:, :], stage[i][:, :], W_SCALE, 0.0, ALU.mult, ALU.add).then_inc(w_scaled, 1)
                wait_alone(pool, w_scaled, st.n(PJ, 2, i + 1))
                pool.tensor_tensor(wl[:, g, :], stage[i][:, :], wh[:, g, :], ALU.subtract).then_inc(w_split, 1)

            def scatter_ids(st):
                if not st.has(SC):
                    return
                if st.it is None and st.s - SC == 0:
                    pool.wait_ge(table_init, 16)
                wait_alone(pool, place_seq, st.n(SC, PL_N))
                pool.indirect_dma_start(ids_dram, bass.IndirectOffsetOnAxis(ap=placei[:, 0:1], axis=0),
                                        tokid[:, :], None).then_inc(ids_scattered, 16)

            def step(st):
                scatter_ids(st)
                norm_scales(st)
                rope(st)
                norm_inputs(st)
                w_low(st, 0)
                w_low(st, 1)

            pipeline(pool, step, B + SC)

            pool.wait_ge(tiles_ready, 1)
            pool.wait_ge(ids_scattered, 16 * B)
            pool.indirect_dma_start(ids_t, None, ids_dram.rearrange("(r c) o -> r (c o)", c=P),
                                    bass.IndirectOffsetOnAxis(ap=tile_r[0:NT, 0:1], axis=0)).then_inc(ids_in, 16)

            pool.wait_ge(idt_ready, 1)
            pool.wait_ge(buffers_clear, 1)
            pool.wait_ge(rec_stored, 16 * B)

            def gather(t):
                pool.indirect_dma_start(g_rec[t % 4], None, rec_dram,
                                        bass.IndirectOffsetOnAxis(ap=idt[:, t:t + 1], axis=0),
                                        bounds_check=TOK - 1, oob_is_err=False).then_inc(g_in[t % 4], 16)

            def scatter(t):
                pool.wait_ge(y2_out, t + 1)
                pool.indirect_dma_start(outf, bass.IndirectOffsetOnAxis(ap=idt[:, t:t + 1], axis=0),
                                        yout[t % 2], None,
                                        bounds_check=TOK - 1, oob_is_err=False).then_inc(out_stored[t % 4], 16)

            for t in range(4):
                gather(t)
            for t in range(TILES):
                scatter(t)
                if t + 4 < TILES:
                    gather(t + 4)

        @block.vector
        def _(dve):
            dve.memset(mv, 1.0).then_inc(setup_dve, 1)
            dve.memset(ohcum[0][:, :], 0.0).then_inc(setup_dve, 1)
            for r in rec:
                ins = dve.memset(r[:, 2 * D:REC], 0.0)
            ins.then_inc(setup_dve, 1)

            def low(ready, n, dst, src, scale, high, done):
                dve.wait_ge(ready, n)
                dve.scalar_tensor_tensor(dst, src, scale, high, ALU.mult, ALU.subtract).then_inc(done, 1)

            srcs = [wkv_s, wkv_s, wq_s, wo_s]

            def aw_low(i):
                d = srcs[i]
                hi, lo = (d[0][:, i, :], d[1][:, i, :]) if i < 2 else (d[0], d[1])
                src = stage[i % 2][:, :]
                if i >= 2:
                    src = src.rearrange("p (k n) -> p k n", k=hi.shape[1])
                low(aw_high, i + 1, lo, src, W_SCALE, hi, aw_split)

            def stats(st):
                if st.has(L - 1):
                    par = st.par(L - 1)
                    dve.wait_ge(xc_in[par], st.n(L - 1, 32, ring=2))
                    for i in range(2):
                        ins = dve.bn_stats(lst[:, i, :], xc[par][:, i, :])
                    ins.then_inc(in_bn, 1)
                    if st.has(L):
                        dve.wait_ge(xn_ready, st.n(L))
                    wait_alone(dve, in_bn, st.n(L - 1))
                    for i in range(2):
                        dve.bn_aggr(mv[:, i, :], lst[:, i, :]).then_inc(in_stats, 1)

            def row_max(st, j):
                if st.has(AT):
                    dve.wait_ge(scores_ready, st.n(AT, 4, j + 1))
                    dve.tensor_reduce(nmax[j % 2][:, :], ps_s[:, :, 0:2 * P],
                                      AX_X, ALU.max, negate=True).then_inc(nmax_ready, 1)

            def pT_pair(st, lag, j):
                if st.has(lag):
                    low(pT_high, st.n(lag, 4, j + 1), pT[1][j % 2][:, :], ps_t[j % 2][:, :], 1.0,
                        pT[0][j % 2][:, :], pT_split)

            def blocks(t):
                return t[:, :].rearrange("p (b t) -> p b t", b=NB)

            def attn_norm(st):
                if st.has(WR):
                    dve.wait_ge(probs_ready, st.n(WR, 4))
                    dve.reciprocal(rinv[:, :], rsum[st.par(WR)][:, :]).then_inc(rinv_ready, 1)
                    dve.wait_ge(pv_done, st.n(WR, 4))
                    dve.wait_ge(rinv_ready, st.n(WR))
                    if st.it is None and st.s == WR:
                        dve.wait_ge(table_init, 16)
                    dve.tensor_tensor(attn[:, :].rearrange("p (h d) -> p h d", h=H),
                                      ps_o[:, :].rearrange("p (h d) -> p h d", h=H),
                                      rinv[:, :].unsqueeze(2).broadcast_to([P, H, DH]), ALU.mult).then_inc(attn_ready, 1)

            def route(st):
                if not st.has(RT):
                    return
                par = st.par(RT)
                aff = bank("aff")[:, 0:E]
                dve.wait_ge(aff_ready, st.n(RT))
                dve.max(top8[:, :], aff).then_inc(route_seq, 2)
                wait_alone(dve, route_seq, st.n(RT, RO_N, 2))
                dve.max_index(idx8[:, :], top8[:, :], aff).then_inc(route_seq, 1)
                dve.wait_ge(route_seq, st.n(RT, RO_N, 3))
                dve.tensor_copy(eidf[:, :], idx8[:, 0:1]).then_inc(route_seq, 1)
                dve.wait_ge(route_seq, st.n(RT, RO_N, 4))
                dve.tensor_scalar(oneh[:, :], basee[:, 1, :], eidf[:, 0:1], None, ALU.is_equal).then_inc(route_seq, 1)
                dve.wait_ge(route_seq, st.n(RT, RO_N, 5))
                dve.tensor_tensor(ohcum[1 - par][:, :], ohcum[par][:, :], oneh[:, :], ALU.add).then_inc(route_seq, 1)

            def alpha(st):
                if st.has(RT):
                    dve.wait_ge(ealpha_ready, st.n(RT))
                    dve.tensor_scalar(ealpha[:, 1:2], ealpha[:, 0:1], 1.0, W_SCALE, ALU.add, ALU.mult)\
                        .then_inc(alpha_seq, 1)
                    dve.wait_ge(alpha_seq, st.n(RT, AL_N, 1))
                    dve.reciprocal(rec[st.par(RT)][:, ALPHA:ALPHA + 1], ealpha[:, 1:2]).then_inc(alpha_seq, 1)

            def places(st):
                if not st.has(RT):
                    return
                dve.wait_ge(pref_ready, st.n(RT))
                dve.tensor_tensor(place[:, 0, :], bank("pref")[:, 0:E], basee[:, 0, :], ALU.add).then_inc(place_seq, 1)
                dve.wait_ge(place_seq, st.n(RT, PL_N, 1))
                dve.tensor_tensor(place[:, 1, :], place[:, 0, :], oneh[:, :], ALU.mult).then_inc(place_seq, 1)
                dve.wait_ge(place_seq, st.n(RT, PL_N, 2))
                first = not st.has(RT + 1)
                dve.tensor_reduce(placef[:, :], place[:, 1, :], AX_X, ALU.add).then_inc(place_seq, 2 if first else 1)
                if not first:
                    dve.wait_ge(ids_scattered, st.n(RT + 1, 16))
                    dve.tensor_scalar(tokid[:, :], tokid[:, :], float(P), None, ALU.add).then_inc(place_seq, 1)
                dve.wait_ge(place_seq, st.n(RT, PL_N, 4))
                dve.tensor_copy(placei[:, :], placef[:, :]).then_inc(place_seq, 1)

            def step(st):
                row_max(st, 0)
                if st.has(PJ):
                    if st.has(PJ + 1):
                        dve.wait_ge(kx_split, st.n(PJ + 1))
                        dve.wait_ge(kx_high, st.n(PJ + 1))
                    else:
                        dve.wait_ge(consts_in, N_CONST)
                    dve.wait_ge(kx_ready, st.n(PJ))
                    dve.tensor_tensor(k_cos[:, :, :], blocks(bank("kx")),
                                      cos_t[:, :].unsqueeze(1).broadcast_to([P, NB, P]), ALU.mult).then_inc(kx_cos, 1)
                    dve.wait_ge(rot_ready, st.n(PJ))
                    dve.tensor_tensor(k_sin[:, :, :], blocks(bank("rot")),
                                      sin_t[:, :].unsqueeze(1).broadcast_to([P, NB, P]), ALU.mult).then_inc(rot_sin, 1)
                if st.s == -1:
                    for i in range(2):
                        aw_low(i)
                    dve.wait_ge(aw_split, 2)
                    for hl, k in ((0, 0), (0, 1), (1, 0), (1, 1)):
                        k4 = wkv_s[hl][:, k, 0:INNER].rearrange("p (h a d) -> p h a d", a=2, d=DH // 2)
                        r4 = rot_s[hl][:, k, :].rearrange("p (h a d) -> p h a d", a=2, d=DH // 2)
                        dve.tensor_scalar(r4[:, :, 0, :], k4[:, :, 1, :], -1.0, None, ALU.mult).then_inc(rot_made, 1)
                        dve.tensor_copy(r4[:, :, 1, :], k4[:, :, 0, :]).then_inc(rot_made, 1)
                pT_pair(st, WR, 3)
                row_max(st, 1)
                if st.has(PJ):
                    low(kl_high, st.n(PJ), kT[1][st.par(PJ)][:, :, 1, :], blocks(bank("kl")), W_INV,
                        kT[0][st.par(PJ)][:, :, 1, :], kl_split)
                pT_pair(st, AT, 0)
                attn_norm(st)
                if st.has(PJ):
                    low(vx_high, st.n(PJ), v[1][st.par(PJ)][:, 0, :], bank("vx")[:, :], W_INV,
                        v[0][st.par(PJ)][:, 0, :], vx_split)
                row_max(st, 2)
                if st.has(PJ):
                    dve.wait_ge(kx_high, st.n(PJ))
                    dve.tensor_tensor(kT[1][st.par(PJ)][:, :, 0, :], k_cos[:, :, :], kT[0][st.par(PJ)][:, :, 0, :],
                                      ALU.subtract).then_inc(kx_split, 1)
                route(st)
                if st.has(PJ):
                    low(vl_high, st.n(PJ), v[1][st.par(PJ)][:, 1, :], bank("vl")[:, :], W_INV,
                        v[0][st.par(PJ)][:, 1, :], vl_split)
                pT_pair(st, AT, 1)
                if st.has(WR):
                    low(aT_high, st.n(WR), aT[1][:, :, :], blocks(bank("aT")), 1.0, aT[0][:, :, :], aT_split)
                row_max(st, 3)
                if st.has(PJ):
                    low(q_high, st.n(PJ), qT[1][:, :, :], blocks(bank("q")), W_INV * DH ** -0.5, qT[0][:, :, :], q_split)
                if st.has(L):
                    low(lnT_high, st.n(L), lnT[1][:, :, :], lnT32.rearrange("p (k t) -> p k t", k=KD), 1.0,
                        lnT[0][:, :, :], lnT_split)
                if st.s == -1:
                    aw_low(2)
                    aw_low(3)
                alpha(st)
                pT_pair(st, AT, 2)
                if st.has(WR):
                    xt = x1[st.par(WR)]
                    dve.wait_ge(x1_in[st.par(WR)], st.n(WR, 16, ring=2))
                    dve.wait_ge(y_ready, st.n(WR))
                    dve.scalar_tensor_tensor(xt, bank("y")[:, 0:D], W_INV, xt, ALU.mult, ALU.add).then_inc(x1_ready, 1)
                    dve.wait_ge(x1_ready, st.n(WR))
                    dve.bn_stats(fst[:, :], xt).then_inc(x1_bn, 1)
                    if st.has(WR + 1):
                        dve.wait_ge(f2_ready, st.n(WR + 1))
                    wait_alone(dve, x1_bn, st.n(WR))
                    dve.bn_aggr(mv[:, 2, :], fst[:, :]).then_inc(x1_stats, 1)
                stats(st)
                places(st)

            stats(Step(-2, B))
            dve.wait_ge(colt_ps, 1)
            dve.tensor_copy(colt[:, :], ps_o[:, 0:8 + E * KD]).then_inc(colt_ready, 1)
            pipeline(dve, step)

            pos = [0]

            def piece(n):
                a = rt[:, pos[0]:pos[0] + n]
                pos[0] += n
                return a

            seq = [0]

            def link(ins):
                seq[0] += 1
                ins.then_inc(tile_seq, 1)
                dve.wait_ge(tile_seq, seq[0])

            cnt, ntile, cum, past, gone = (piece(E) for _ in range(5))
            more = piece(16 * E).rearrange("p (e k) -> p e k", e=E)
            upto = piece(E * E).rearrange("p (a b) -> p a b", a=E)
            n_e, n_gone, rest, rowf = (piece(1) for _ in range(4))
            thr = tabs[:, 0:16].unsqueeze(1).broadcast_to([P, E, 16])
            mask = tabs[:, 16:16 + E * E].rearrange("p (a b) -> p a b", a=E)
            tcol = cols[:, 12:13]
            dve.wait_ge(tabs_in, 80)
            dve.wait_ge(counts_ps, 1)
            link(dve.tensor_copy(cnt, ps_o[:, 0:E]))
            link(dve.tensor_tensor(more, cnt.unsqueeze(2).broadcast_to([P, E, 16]), thr, ALU.is_gt))
            link(dve.tensor_reduce(ntile, more, AX_X, ALU.add))
            link(dve.tensor_tensor(upto, mask, ntile.unsqueeze(1).broadcast_to([P, E, E]), ALU.mult))
            link(dve.tensor_reduce(cum, upto, AX_X, ALU.add))
            link(dve.tensor_scalar(past, cum, tcol, None, ALU.is_le))
            link(dve.tensor_tensor(gone, past, ntile, ALU.mult))
            dve.tensor_reduce(n_e, past, AX_X, ALU.add)
            link(dve.tensor_reduce(n_gone, gone, AX_X, ALU.add))
            dve.tensor_scalar(ef_t, n_e, float(E - 1), None, ALU.min)
            link(dve.tensor_tensor(rest, tcol, n_gone, ALU.subtract))
            dve.tensor_scalar(oh_t, basee[:, 1, :], ef_t, None, ALU.is_equal).then_inc(tile_seq, 1)
            dve.scalar_tensor_tensor(rowf, n_e, float(REGION // P), rest, ALU.mult, ALU.add).then_inc(tile_seq, 1)
            dve.wait_ge(tile_seq, seq[0] + 2)
            dve.tensor_copy(tile_r[:, :], rowf).then_inc(tile_seq, 1)
            dve.wait_ge(turned_ps, 1)
            dve.tensor_copy(tile_e[:, :], ps_o[0:1, 0:P])
            dve.tensor_copy(oh_e, ps_t[0][0:E, 0:P])
            dve.tensor_copy(oh_eh, ps_t[0][0:E, 0:P]).then_inc(tiles_ready, 1)
            for g in g_rec:
                ins = dve.memset(g, 0.0)
            ins.then_inc(buffers_clear, 1)
            low(b2_high, 1, b2_s[1], b2_r, W_SCALE, b2_s[0], b2_split)
            dve.wait_ge(cols_ps, 1)
            dve.tensor_copy(tile_c, ps_s[:, 0, 0:NCOL * NT].rearrange("p (c t) -> p c t", c=NCOL)).then_inc(cols_ready, 1)
            dve.wait_ge(ids_in, 16)
            dve.tensor_copy(ids_f, ids_t).then_inc(idf_ready, 1)
            dve.wait_ge(idt_ps, 1)
            dve.tensor_copy(idt[:, :], ps_t[1][:, 0:NT]).then_inc(idt_ready, 1)
            dve.wait_ge(cols_ready, 1)

            def column(c, t):
                return tile_c[:, c, bass.ds(t, 1)]

            def x_split(t, n):
                if not (isinstance(n, int) and n == 1):
                    dve.wait_ge(xgT_split, n - 1)
                dve.wait_ge(xgT_ps, n)
                for k in range(KD):
                    ins = dve.tensor_scalar(xg[:, k * P:(k + 1) * P], ps_u[2][:, k * P:(k + 1) * P],
                                            column(k, t), column(KD + k, t), ALU.mult, ALU.add)
                ins.then_inc(xg_ready, 1)
                dve.wait_ge(xgT_high, n)
                dve.tensor_tensor(xgT[1], xg.rearrange("p (k t) -> p k t", k=KD), xgT[0], ALU.subtract)\
                    .then_inc(xgT_split, 1)

            def h_split(t, n, par):
                for hf in range(2):
                    h3 = hid32[hf][:, :, :]
                    if not (isinstance(n, int) and n == 1):
                        dve.wait_ge(hid_split, n + hf - 2)
                    dve.wait_ge(hid_ps, n + hf)
                    c = 2 * KD + 4 * hf
                    bias = tile_c[:, c:c + 4, bass.ds(t, 1)]
                    dve.scalar_tensor_tensor(h3, ps_h[par][hf].rearrange("p (f t) -> p f t", t=P), W_INV,
                                             bias.broadcast_to([P, 4, P]), ALU.mult, ALU.add).then_inc(hid_biased, 1)
                    dve.wait_ge(hid_high, n + hf)
                    dve.scalar_tensor_tensor(hid[1][par][:, 4 * hf:4 * hf + 4, :], h3, 0.0,
                                             hid[0][par][:, 4 * hf:4 * hf + 4, :], ALU.max, ALU.subtract)\
                        .then_inc(hid_split, 1)

            def y_out(n, par, ring, free, first):
                r = g_rec[ring]
                if not (isinstance(n, int) and n == 1):
                    dve.wait_ge(y2_out, n - 1)
                dve.scalar_tensor_tensor(ybase, r[:, 0:D], r[:, INV2:INV2 + 1], r[:, D:2 * D], ALU.mult, ALU.add)\
                    .then_inc(y2_base, 1)
                if not first:
                    dve.wait_ge(out_stored[(ring + 2) % 4], free)
                dve.wait_ge(y2_base, n)
                dve.wait_ge(y2_ps, n)
                dve.scalar_tensor_tensor(yout[par], ps_u[par][:, 0:D], r[:, ALPHA:ALPHA + 1], ybase,
                                         ALU.mult, ALU.add).then_inc(y2_out, 1)

            def tile_step(t, it=None):
                r = 0 if it is None else it
                if t < TILES:
                    h_split(r * 4 + t, r * 8 + (2 * t + 1), t % 2)
                if t + 1 < TILES:
                    x_split(r * 4 + (t + 1), r * 4 + (t + 2))
                if t >= 1:
                    y_out(r * 4 + t, (t - 1) % 2, (t - 1) % 4, r * 16 + 16 * ((t - 3) // 4 + 1), t < 3)

            x_split(0, 1)
            for t in range(T_FROM):
                tile_step(t)
            with dve.Fori(0, (T_TO - T_FROM) // 4) as it:
                for t in range(T_FROM, T_FROM + 4):
                    tile_step(t, it)
            for t in range(T_TO, TILES + 1):
                tile_step(t)

        @block.tensor
        def _(pe):
            PAIRS = ((0, 0), (0, 1), (1, 0))

            def split_mm(out, lhs, rhs):
                n = len(lhs) * len(PAIRS)
                c = 0
                for k in range(len(lhs)):
                    for a, b in PAIRS:
                        ins = pe.matmul(out, lhs[k][a], rhs[k][b], start=(c == 0), stop=(c == n - 1))
                        c += 1
                return ins

            def unit(st, name):
                k = ORDER.index(name)
                for m in range(k - 3, -24, -3):
                    i, off = m % 12, -(m // 12)
                    _, lag, evac, per = UNITS[i]
                    if st.has(lag + off):
                        pe.wait_ge(evac, st.n(lag + off, per))
                        break
                return bank(name)

            def scores(st, j):
                if not st.has(AT):
                    return
                if j == 0:
                    pe.wait_ge(q_split, st.n(AT))
                    pe.wait_ge(kx_split, st.n(AT))
                    pe.wait_ge(kl_split, st.n(AT))
                    if st.has(AT + 1):
                        pe.wait_ge(probs_ready, st.n(AT + 1, 4))
                else:
                    pe.wait_ge(probs_ready, st.n(AT, 4, j))
                par = st.par(AT)
                for c, (a, b) in enumerate(PAIRS):
                    for i in range(2):
                        r = slice(64 * i, 64 * i + 64)
                        ins = pe.matmul(ps_s[:, i, 0:2 * P], qT[a][r, j, :],
                                        kT[b][par][r, j, :, :].rearrange("p s t -> p (s t)"),
                                        start=(c == 0), stop=(c == 2))
                ins.then_inc(scores_ready, 1)

            def turn_probs(st, lag, j):
                if st.has(lag):
                    pe.wait_ge(probs_ready, st.n(lag, 4, j + 1))
                    for c in range(4):
                        ins = pe.transpose(ps_t[j % 2][:, c * P:(c + 1) * P],
                                           probs[j % 2][:, c // 2, (c % 2) * P:(c % 2 + 1) * P], ident[:, :])
                    ins.then_inc(pT_ready, 1)

            def values(st, lag, j):
                if not st.has(lag):
                    return
                if j == 0:
                    pe.wait_ge(vx_split, st.n(lag))
                    pe.wait_ge(vl_split, st.n(lag))
                    if st.has(lag + 1):
                        pe.wait_ge(attn_ready, st.n(lag + 1))
                pe.wait_ge(pT_split, st.n(lag, 4, j + 1))
                par = st.par(lag)
                for i in range(2):
                    h = 2 * j + i
                    ins = split_mm(ps_o[:, h * DH:(h + 1) * DH],
                                   [[pT[a][j % 2][:, (2 * i + c) * P:(2 * i + c + 1) * P] for a in range(2)]
                                    for c in range(2)],
                                   [[v[a][par][:, c, h * DH:(h + 1) * DH] for a in range(2)] for c in range(2)])
                ins.then_inc(pv_done, 1)

            def project_T(st, name, w, col0, src, ready):
                if not st.has(PJ):
                    return
                bk = unit(st, name)
                for n in range(NB):
                    ins = split_mm(bk[:, n * P:(n + 1) * P],
                                   [[w[a][:, k, col0 + n * P:col0 + (n + 1) * P] for a in range(2)] for k in range(KD)],
                                   [[lnT[a][:, k, src * P:(src + 1) * P] for a in range(2)] for k in range(KD)])
                ins.then_inc(ready, 1)

            def project_v(st, name, src, ready):
                if not st.has(PJ):
                    return
                bk = unit(st, name)
                split_mm(bk[:, :],
                         [[lnT[a][:, k, src * P:(src + 1) * P] for a in range(2)] for k in range(KD)],
                         [[wkv_s[a][:, k, INNER:2 * INNER] for a in range(2)] for k in range(KD)]).then_inc(ready, 1)

            def step(st):
                scores(st, 0)
                if st.has(PJ):
                    pe.wait_ge(lnT_split, st.n(PJ))
                    if st.s == 0 and st.it is None:
                        pe.wait_ge(aw_split, 3)
                        pe.wait_ge(rot_made, 8)
                project_T(st, "kx", wkv_s, 0, 0, kx_ready)
                values(st, WR, 2)
                project_T(st, "rot", rot_s, 0, 0, rot_ready)
                turn_probs(st, WR, 3)
                scores(st, 1)
                project_T(st, "kl", wkv_s, 0, 1, kl_ready)
                if st.has(RT):
                    bk = unit(st, "fT")
                    pe.wait_ge(f2_ready, st.n(RT))
                    for k in range(KD):
                        ins = pe.transpose(bk[:, k * P:(k + 1) * P], rec[st.par(RT)][:, k * P:(k + 1) * P], ident[:, :])
                    ins.then_inc(fT_ready, 1)
                turn_probs(st, AT, 0)
                values(st, WR, 3)
                project_v(st, "vx", 0, vx_ready)
                scores(st, 2)
                if st.has(RT):
                    bk = unit(st, "aff")
                    pe.wait_ge(fT_copied, st.n(RT))
                    ck = colt[:, 8:8 + E * KD].rearrange("p (e k) -> p k e", k=KD)
                    for k in range(KD):
                        ins = pe.matmul(bk[:, 0:E], fT[:, k * P:(k + 1) * P], ck[:, k, :], start=(k == 0), stop=(k == KD - 1))
                    ins.then_inc(aff_ready, 1)
                project_v(st, "vl", 1, vl_ready)
                turn_probs(st, AT, 1)
                values(st, AT, 0)
                if st.has(WR):
                    bk = unit(st, "aT")
                    pe.wait_ge(attn_ready, st.n(WR))
                    for n in range(NB):
                        ins = pe.transpose(bk[:, n * P:(n + 1) * P], attn[:, n * P:(n + 1) * P], ident[:, :])
                    ins.then_inc(aT_ready, 1)
                scores(st, 3)
                project_T(st, "q", wq_s, 0, 1, q_ready)
                if st.has(L):
                    bk = unit(st, "lnT")
                    pe.wait_ge(xn_ready, st.n(L))
                    for k in range(KD):
                        for s in range(2):
                            c = 2 * k + s
                            ins = pe.transpose(bk[:, c * P:(c + 1) * P], xc[st.par(L)][:, s, k * P:(k + 1) * P],
                                               ident[:, :])
                    ins.then_inc(lnT_ready, 1)
                turn_probs(st, AT, 2)
                values(st, AT, 1)
                if st.has(WR):
                    bk = unit(st, "y")
                    pe.wait_ge(aT_split, st.n(WR))
                    if st.it is None and st.s == WR:
                        pe.wait_ge(aw_split, 4)
                    split_mm(bk[:, 0:D], [[aT[a][:, n, :] for a in range(2)] for n in range(NB)],
                             [[wo_s[a][:, n, :] for a in range(2)] for n in range(NB)]).then_inc(y_ready, 1)
                if st.has(RT):
                    bk = unit(st, "pref")
                    pe.wait_ge(route_seq, st.n(RT, RO_N))
                    pe.matmul(bk[:, 0:E], tri[:, 0, :], oneh[:, :], start=True, stop=False)
                    pe.matmul(bk[:, 0:E], tri[:, 1, :], ohcum[st.par(RT)][:, :], start=False, stop=True)\
                        .then_inc(pref_ready, 1)

            pe.wait_ge(first_in, N_FIRST)
            pe.wait_ge(rowt_in, 80)
            n = 8 + E * KD
            pe.transpose(ps_o[:, 0:n], rowt, ident[0:n, 0:n]).then_inc(colt_ps, 1)
            pipeline(pe, step)

            pe.wait_ge(route_seq, RO_N * B)
            pe.matmul(ps_o[:, 0:E], tri[:, 1, :], ohcum[0][:, :], start=True, stop=True).then_inc(counts_ps, 1)
            pe.wait_ge(tile_seq, 12)
            pe.matmul(ps_o[0:1, 0:P], ef_t, ident[:, :], start=True, stop=True)
            pe.transpose(ps_t[0][0:E, 0:P], oh_t, ident[:, :]).then_inc(turned_ps, 1)
            pe.wait_ge(tiles_ready, 1)
            srcs = [lngb_r[:, k * P:(k + 1) * P] for k in range(2 * KD)] + [b1_r[:, f * P:(f + 1) * P] for f in range(FB)]
            for c, src in enumerate(srcs):
                ins = pe.matmul(ps_s[:, 0, c * NT:(c + 1) * NT], src, oh_e[:, 0:NT], start=True, stop=True)
            ins.then_inc(cols_ps, 1)
            pe.wait_ge(idf_ready, 1)
            pe.transpose(ps_t[1][:, 0:NT], ids_f, ident[0:NT, 0:NT]).then_inc(idt_ps, 1)
            pe.wait_ge(b2_split, 1)
            pe.wait_ge(cols_ready, 1)
            pe.wait_ge(idt_ready, 1)

            pe.wait_ge(w_split, 2 * B)

            def expert(t):
                return pe.value_load(tile_e[0:1, bass.ds(t, 1)], min_val=0, max_val=E - 1)

            def x_turn(ring, n, n_rec):
                pe.wait_ge(g_in[ring], n_rec)
                if not (isinstance(n, int) and n == 0):
                    pe.wait_ge(xg_ready, n)
                for k in range(KD):
                    ins = pe.transpose(ps_u[2][:, k * P:(k + 1) * P], g_rec[ring][:, k * P:(k + 1) * P], ident[:, :])
                ins.then_inc(xgT_ps, 1)

            def hidden(n, n_w1, par):
                pe.wait_ge(w1c_in[par], n_w1)
                pe.wait_ge(xgT_split, n)
                for f in range(FB):
                    ins = split_mm(ps_h[par][f // 4][:, (f % 4) * P:(f % 4 + 1) * P],
                                   [[w[:, k * FF + f * P:k * FF + (f + 1) * P] for w in w1c[par]] for k in range(KD)],
                                   [[xgT[a][:, k, :] for a in range(2)] for k in range(KD)])
                    if f % 4 == 3:
                        ins.then_inc(hid_ps, 1)

            def project_out(t, n, par, free):
                e = expert(t)
                if free is not None:
                    pe.wait_ge(y2_out, free)
                pe.wait_ge(hid_split, n)
                oh = oh_eh[:, bass.ds(t, 1)].broadcast_to([E, P])
                for i in range(2):
                    pe.matmul(ps_u[par][:, 0:D], oh, b2_s[i], start=(i == 0), stop=False)
                split = [(f, a, b) for f in range(FB) for a, b in PAIRS]
                for f, a, b in split:
                    ins = pe.matmul(ps_u[par][:, 0:D], hid[a][par][:, f, :], (w2h, w2l)[b][:, e, f * D:(f + 1) * D],
                                    start=False, stop=((f, a, b) == split[-1]))
                ins.then_inc(y2_ps, 1)

            def tile_step(t, it=None):
                r = 0 if it is None else it
                if t < TILES:
                    hidden(r * 4 + (t + 1), r * 64 + 32 * (t // 2 + 1), t % 2)
                if t + 1 < TILES:
                    x_turn((t + 1) % 4, r * 4 + (t + 1), r * 16 + 16 * ((t + 1) // 4 + 1))
                if t >= 1:
                    project_out(r * 4 + (t - 1), r * 8 + 2 * t, (t - 1) % 2, r * 4 + (t - 2) if t > 2 else None)

            x_turn(0, 0, 16)
            for t in range(T_FROM):
                tile_step(t)
            with pe.Fori(0, (T_TO - T_FROM) // 4) as it:
                for t in range(T_FROM, T_FROM + 4):
                    tile_step(t, it)
            for t in range(T_TO, TILES + 1):
                tile_step(t)


_INS = ['x', 'ctx_1024', 'L0_xattn_gamma_x', 'L0_xattn_beta_x', 'L0_xattn_gamma_l', 'L0_xattn_beta_l',
        'L0_xattn_Wq', 'L0_xattn_Wkv', 'L0_xattn_Wo', 'L0_ffn_centroids', 'L0_ffn_ln_g', 'L0_ffn_ln_b',
        'L0_ffn_w1', 'L0_ffn_b1', 'L0_ffn_w2', 'L0_ffn_b2']


def _constants(tokens, experts):
    import numpy as np
    p = 128
    dh, base = 64, 10000.0
    inv = (np.float32(1.0) / np.float32(base) ** (np.arange(0, dh, 2, dtype=np.float32) / np.float32(dh)))
    ang = np.arange(p, dtype=np.float32)[:, None] * inv[None, :].astype(np.float32)
    ang = np.concatenate([ang, ang, ang, ang], axis=1)
    cos = (np.cos(ang).T / 64.0).astype(np.float32)
    sin = (np.sin(ang).T / 64.0).astype(np.float32)
    tri = np.zeros((p, 2, p), np.float16)
    tri[:, 0, :] = np.triu(np.ones((p, p)))
    tri[:, 1, :] = 1.0
    cols = np.zeros((p, 16), np.float32)
    cols[:, 0:3], cols[:, 3:6], cols[:, 6:9], cols[:, 9:12] = 1e-5, -0.5, 0.5, -1.0
    cols[:, 12] = np.arange(p)
    nt = tokens // p + experts
    tabs = np.concatenate([np.arange(16) * float(p), np.tril(np.ones((experts, experts))).reshape(-1), [0.0]])
    basee = np.stack([np.arange(experts) * float(tokens) - 1.0, np.arange(experts)])
    places = experts * tokens // p + nt
    empty = np.full((p, places), 2 * tokens, np.int32)
    return {"rope_cos": np.ascontiguousarray(cos), "rope_sin": np.ascontiguousarray(sin),
            "ident": np.eye(p, dtype=np.float32), "tri": tri, "cols": cols,
            "tabs": tabs.astype(np.float32), "basee": basee.astype(np.float32),
            "ids": np.arange(p, dtype=np.int32)[:, None], "empty": empty}


def kernel(**inputs):
    import numpy as _np
    import concourse.bacc as _bacc
    from concourse import mybir as _mybir
    from concourse.bass_utils import run_bass_kernel_spmd as _run

    nc = _bacc.Bacc("TRN2", target_bir_lowering=False, num_devices=1)
    arrays, args = {}, []
    shape = inputs['x'].shape
    given = [(n, _np.ascontiguousarray(inputs[n])) for n in _INS]
    given += list(_constants(shape[0] * shape[1], inputs['L0_ffn_w1'].shape[0]).items())
    for name, a in given:
        arrays[f"in_{name}_dram"] = a
        args.append(nc.dram_tensor(f"in_{name}_dram", a.shape, _mybir.dt.from_np(a.dtype), kind="ExternalInput").ap())
    args.append(nc.dram_tensor("out_0_dram", shape, _mybir.dt.float32, kind="ExternalOutput").ap())
    xattn_moe_kernel(nc, *args)
    r = _run(nc, [arrays], core_ids=[0])
    return r.results[0]["out_0_dram"]
```

```python
from contextlib import ExitStack

import concourse.bass as bass
from concourse import mybir

F32 = mybir.dt.float32
F16 = mybir.dt.float16
I32 = mybir.dt.int32
U32 = mybir.dt.uint32
ALU = mybir.AluOpType
ACT = mybir.ActivationFunctionType
AX_X = mybir.AxisListType.X

P = 128
EPS = 1e-5
W_SCALE = 64.0
W_INV = 1.0 / W_SCALE


class Step:

    def __init__(self, s, batches, it=None, base=None):
        self.s, self.batches, self.it = s, batches, it
        self.base = base or self

    def ahead(self):
        return Step(self.s + 1, self.batches, self.it, self)

    def behind(self):
        return Step(self.s - 1, self.batches, self.it, self)

    def has(self, lag):
        return self.it is not None or 0 <= self.s - lag < self.batches

    def first(self, lag):
        return self.it is None and self.s == lag

    def par(self, lag):
        return (self.s - lag) % 2

    def batch(self, lag):
        b = self.s - lag
        return b if self.it is None else b + self.it * 2

    def n(self, lag, per=1, k=None, ring=1):
        v = per * ((self.s - lag) // ring) + (per if k is None else k)
        return v if self.it is None else v + self.it * (2 // ring * per)


def xattn_moe_kernel(nc, x, ctx_in, gamma_x, beta_x, gamma_l, beta_l, wq, wkv, wo, cent, ln_g, ln_b,
                     w1, b1, w2, b2, rope_cos, rope_sin, ident_c, tri_c, cols_c, tabs_c, basee_c, ids_c, empty_c, out):
    B, T, D = x.shape
    INNER = wq.shape[1]
    DH = 64
    H = INNER // DH
    E, _, FF = w1.shape
    KD = D // P
    NB = INNER // P
    FB = FF // P
    TOK = B * T
    TILES = TOK // P + E - 1
    NT = TILES + 1
    REGION = TOK
    TABLE = (E * REGION // P + NT) * P
    REC = 2 * D + 4
    ALPHA, INV2 = 2 * D, 2 * D + 1
    OOB = 2 * TOK
    assert T == P and KD == 2 and NB == 4 and H == 8 and FB == 8 and B == 2 * E

    L, PJ, AT, WR, RT, SC = -1, 0, 1, 2, 3, 4
    LOOP_FROM, LOOP_TO = 5, 13
    T_FROM, T_TO = 6, TILES - 1
    assert (T_TO - T_FROM) % 4 == 0

    xf = x.rearrange("b t d -> (b t) d")
    cf = ctx_in.rearrange("b t d -> (b t) d")
    outf = out.rearrange("b t d -> (b t) d")
    x_b = xf.rearrange("(b p) d -> b p d", p=P)
    c_b = cf.rearrange("(b p) d -> b p d", p=P)
    w1_g = w1.rearrange("e (k p) f -> (e k) p f", p=P)
    w2_g = w2.rearrange("e (h f p) d -> (e h) p f d", h=2, p=P)
    GRP = FF

    with ExitStack() as es:
        def sb(name, shape, dt):
            return es.enter_context(nc.sbuf_tensor(name, shape, dt))

        def pb(name):
            return es.enter_context(nc.psum_tensor(name, [P, 512], F32))

        def sem(name):
            return es.enter_context(nc.semaphore(name))

        rec_dram = nc.dram_tensor("rec_dram", [TOK, REC], F32).ap()
        ids_dram = nc.dram_tensor("ids_dram", [TABLE, 1], I32).ap()
        rec_b = rec_dram.rearrange("(b p) r -> b p r", p=P)

        w1h = sb("w1h", [P, E, KD * FF], F16)
        w1l = sb("w1l", [P, E, KD * FF], F16)
        w2h = sb("w2h", [P, E, FB * D], F16)
        w2l = sb("w2l", [P, E, FB * D], F16)
        KV = 2 * INNER
        AW = KD * INNER + KD * KV + KD * INNER + NB * D
        aw = [sb("awh", [P, AW], F16), sb("awl", [P, AW], F16)]
        o_q, o_kv, o_rot, o_wo = 0, KD * INNER, KD * (INNER + KV), KD * (INNER + KV + INNER)
        wq_s = [a[:, o_q:o_kv].rearrange("p (k n) -> p k n", k=KD) for a in aw]
        wkv_s = [a[:, o_kv:o_rot].rearrange("p (k n) -> p k n", k=KD) for a in aw]
        rot_s = [a[:, o_rot:o_wo].rearrange("p (k n) -> p k n", k=KD) for a in aw]
        wo_s = [a[:, o_wo:AW].rearrange("p (k n) -> p k n", k=NB) for a in aw]
        stage = [sb(f"stage{i}", [P, GRP], F32) for i in range(2)]
        xc = [sb(f"xc{i}", [P, 2, D], F32) for i in range(2)]
        lnT = [sb(f"lnT{h}", [P, KD, 2 * P], F16) for h in "hl"]
        qT = [sb(f"qT{h}", [P, NB, P], F16) for h in "hl"]
        kT_all = sb("kT", [P, 4, NB * 2 * P], F16)
        kT = [[kT_all[:, 2 * h + i, :].rearrange("p (n s t) -> p n s t", n=NB, s=2) for i in range(2)]
              for h in range(2)]
        v = [[sb(f"v{h}{i}", [P, 2, INNER], F16) for i in range(2)] for h in "hl"]
        k_cos = sb("k_cos", [P, NB, P], F32)
        k_sin = sb("k_sin", [P, NB, P], F32)
        lnT32 = k_sin[:, :, :].rearrange("p b t -> p (b t)")
        cos_t = sb("cos_t", [P, P], F32)
        sin_t = sb("sin_t", [P, P], F32)
        probs = [sb(f"probs{i}", [P, 2, 2 * P], F32) for i in range(2)]
        pT = [[sb(f"pT{h}{i}", [P, 4 * P], F16) for i in range(2)] for h in "hl"]
        attn = sb("attn", [P, INNER], F32)
        aT = [sb(f"aT{h}", [P, NB, P], F16) for h in "hl"]
        rec = [sb(f"rec{i}", [P, REC], F32) for i in range(2)]
        x1 = [r[:, D:2 * D] for r in rec]
        fT = sb("fT", [P, D], F32)
        ident = sb("ident", [P, P], F32)
        tri = sb("tri", [P, 2, P], F16)
        cols = sb("cols", [P, 16], F32)
        tabs = stage[1][:, 0:16 + E * E + 1]
        b1_r = stage[0][0:E, 0:FF]
        lngb_r = stage[1][0:E, 128:128 + 2 * D]
        b2_r = stage[1][0:E, 128 + 2 * D:128 + 3 * D]
        basee = sb("basee", [P, 2, E], F32)
        rowt = attn[0:8 + E * KD, 0:P]
        colt = sb("colt", [P, 8 + E * KD], F32)
        small = sb("small", [P, 120], F32)
        at = [0]

        def few(n):
            a = small[:, at[0]:at[0] + n]
            at[0] += n
            return a

        nmax = [few(2) for _ in range(2)]
        rsum = [few(H) for _ in range(2)]
        rinv = few(H)
        lst = few(12).rearrange("p (a b) -> p a b", a=2)
        mv = few(6).rearrange("p (a b) -> p a b", a=3)
        norms = few(24)
        fst, top8, eidf = few(6), few(8), few(1)
        place, placef, ealpha = few(2 * E).rearrange("p (a e) -> p a e", a=2), few(1), few(2)
        nmean, r1, r2, s2 = norms[:, 0:3], norms[:, 3:6], norms[:, 6:9], norms[:, 9:12]
        nv, nu, ninv2 = norms[:, 12:15], norms[:, 15:18], norms[:, 18:19]
        idx8 = sb("idx8", [P, 8], U32)
        oneh = sb("oneh", [P, E], F16)
        ohcum = [sb(f"ohcum{i}", [P, E], F16) for i in range(2)]
        placei = sb("placei", [P, 1], I32)
        tokid = sb("tokid", [P, 1], I32)
        oob = attn[:, P:P + TABLE // P].bitcast(I32)
        tile_e = sb("tile_e", [1, P], I32)
        tile_r = sb("tile_r", [P, 1], I32)
        idt = sb("idt", [P, NT], I32)

        def over(t, lo, n):
            return t[:, lo:lo + n].bitcast(F32)
        W1 = KD * FF
        w1c = [[kT_all[:, 0:2, :].rearrange("p a n -> p (a n)"), kT_all[:, 2:4, :].rearrange("p a n -> p (a n)")],
               [aw[0][:, 0:W1], aw[1][:, 0:W1]]]
        g_rec = [over(aw[i // 2], W1 + (i % 2) * 2 * REC, 2 * REC) for i in range(4)]
        yout = [over(aw[i], W1 + 4 * REC, 2 * D) for i in range(2)]
        xg = attn[:, 0:D]
        ybase = rec
        hid32 = [k_cos, k_sin]
        xgT = [lnT[i][:, 0, :].rearrange("p (k t) -> p k t", k=KD) for i in range(2)]
        hid = [[v[i][j][:, :, :].rearrange("p a (c t) -> p (a c) t", t=P) for j in range(2)] for i in range(2)]
        NCOL = 2 * KD + FB
        tile_c = probs[0][:, :, :].rearrange("p a b -> p (a b)")[:, 0:NCOL * NT].rearrange("p (c t) -> p c t", c=NCOL)
        oh_t = probs[1][:, 0, 0:E]
        oh_e = probs[1][0:E, 0, 128:256]
        oh_eh = pT[0][0][0:E, 0:P]
        ef_t = probs[1][:, 0, 16:17]
        ids_t = probs[1][0:NT, 1, 0:P].bitcast(I32)
        ids_f = probs[1][0:NT, 1, P:2 * P]
        b2_s = [pT[1][i][0:E, 0:D] for i in range(2)]
        rt = attn[:, :]

        ps_s = es.enter_context(nc.psum_tensor("ps_s", [P, 2, 512], F32))
        ps_t = [pb(f"ps_t{i}") for i in range(2)]
        ps_u = [pb(f"ps_u{i}") for i in range(3)]
        ps_o = pb("ps_o")
        ps_h = [[ps_s[:, i, :] for i in range(2)], [t[:, :] for t in ps_t]]

        consts_in = sem("consts_in")
        first_in = sem("first_in")
        xc_in = [sem(f"xc_in{i}") for i in range(2)]
        x1_in = [sem(f"x1_in{i}") for i in range(2)]
        stage_in = [sem(f"stage_in{i}") for i in range(2)]
        rowt_in = sem("rowt_in")
        table_init = sem("table_init")
        rec_stored = sem("rec_stored")
        ids_scattered = sem("ids_scattered")
        aw_high = sem("aw_high")
        aw_split = sem("aw_split")
        rot_made = sem("rot_made")
        w_high = sem("w_high")
        w_scaled = sem("w_scaled")
        w_split = sem("w_split")
        setup_dve = sem("setup_dve")
        colt_ps = sem("colt_ps")
        colt_ready = sem("colt_ready")
        in_bn = sem("in_bn")
        in_stats = sem("in_stats")
        norm_seq = sem("norm_seq")
        xn_ready = sem("xn_ready")
        lnT_ready = sem("lnT_ready")
        lnT_affine = sem("lnT_affine")
        lnT_high = sem("lnT_high")
        lnT_split = sem("lnT_split")
        kx_ready, kx_cos = sem("kx_ready"), sem("kx_cos")
        rot_ready, rot_sin = sem("rot_ready"), sem("rot_sin")
        kx_sum, kx_high, kx_split = sem("kx_sum"), sem("kx_high"), sem("kx_split")
        kl_ready, kl_high, kl_split = sem("kl_ready"), sem("kl_high"), sem("kl_split")
        vx_ready, vx_high, vx_split = sem("vx_ready"), sem("vx_high"), sem("vx_split")
        vl_ready, vl_high, vl_split = sem("vl_ready"), sem("vl_high"), sem("vl_split")
        q_ready, q_high, q_split = sem("q_ready"), sem("q_high"), sem("q_split")
        scores_ready = sem("scores_ready")
        nmax_ready = sem("nmax_ready")
        probs_ready = sem("probs_ready")
        pT_ready, pT_high, pT_split = sem("pT_ready"), sem("pT_high"), sem("pT_split")
        pv_done = sem("pv_done")
        rinv_ready = sem("rinv_ready")
        attn_ready = sem("attn_ready")
        aT_ready, aT_high, aT_split = sem("aT_ready"), sem("aT_high"), sem("aT_split")
        y_ready = sem("y_ready")
        x1_ready, x1_bn, x1_stats = sem("x1_ready"), sem("x1_bn"), sem("x1_stats")
        f2_ready = sem("f2_ready")
        fT_ready, fT_copied = sem("fT_ready"), sem("fT_copied")
        aff_ready = sem("aff_ready")
        route_seq = sem("route_seq")
        ninv2_ready = sem("ninv2_ready")
        ealpha_ready = sem("ealpha_ready")
        alpha_seq = sem("alpha_seq")
        pref_ready = sem("pref_ready")
        place_seq = sem("place_seq")
        counts_ps = sem("counts_ps")
        tabs_in = sem("tabs_in")
        tile_seq = sem("tile_seq")
        tiles_ready = sem("tiles_ready")
        turned_ps = sem("turned_ps")
        turned = sem("turned")
        ids_in = sem("ids_in")
        idf_ready = sem("idf_ready")
        idt_ps = sem("idt_ps")
        idt_ready = sem("idt_ready")
        cols_ps = sem("cols_ps")
        cols_ready = sem("cols_ready")
        b2_high = sem("b2_high")
        b2_split = sem("b2_split")
        buffers_clear = sem("buffers_clear")
        w1c_in = [sem(f"w1c_in{i}") for i in range(2)]
        g_in = [sem(f"g_in{i}") for i in range(4)]
        xgT_ps, xg_ready, xgT_high, xgT_split = sem("xgT_ps"), sem("xg_ready"), sem("xgT_high"), sem("xgT_split")
        hid_ps, hid_biased, hid_high, hid_split = sem("hid_ps"), sem("hid_biased"), sem("hid_high"), sem("hid_split")
        y2_ps, y2_base, y2_out = sem("y2_ps"), sem("y2_base"), sem("y2_out")
        out_stored = [sem(f"out_stored{i}") for i in range(4)]

        NO_N, RO_N, PL_N, AL_N = 8, 6, 5, 2
        N_FIRST, N_CONST = 16 * 2, 16 * 6

        UNITS = [
            ("kx", PJ, kx_cos, 1, 1),
            ("kl", PJ, kl_split, 1, 1),
            ("rot", PJ, rot_sin, 1, 1),
            ("vx", PJ, vx_split, 1, 1),
            ("pref", RT + 1, place_seq, PL_N, 1),
            ("vl", PJ, vl_split, 1, 1),
            ("aT", WR, aT_split, 1, 1),
            ("lnT", L, lnT_affine, 1, 1),
            ("fT", RT, fT_copied, 1, 1),
            ("q", PJ, q_split, 1, 1),
            ("y", WR, x1_ready, 1, 1),
            ("aff", RT, route_seq, RO_N, 3),
        ]
        LAST_PROJECTION = q_ready
        ORDER = [u[0] for u in UNITS]

        def bank(name):
            return ps_u[ORDER.index(name) % 3]

        def wait_alone(eng, s, n):
            eng.wait_ge(s, n)
            eng.nop(nofuse=True)

        def pipeline(eng, step):
            for s in range(-2, LOOP_FROM):
                step(Step(s, B))
            with eng.Fori(0, (LOOP_TO - LOOP_FROM) // 2) as it:
                for u in range(2):
                    step(Step(LOOP_FROM + u, B, it))
            for s in range(LOOP_TO, B + SC + 1):
                step(Step(s, B))

        block = es.enter_context(nc.Block())

        @block.sync
        def _(sp):
            def load_xc(b, par):
                sp.dma_start(xc[par][:, 0, :], c_b[b]).then_inc(xc_in[par], 16)
                sp.dma_start(xc[par][:, 1, :], x_b[b]).then_inc(xc_in[par], 16)

            load_xc(0, 0)
            sp.dma_start(cols[:, :], cols_c).then_inc(first_in, 16)
            sp.dma_start(ident[:, :], ident_c).then_inc(first_in, 16)
            for i, g in enumerate((gamma_x, gamma_l, beta_x, beta_l)):
                sp.dma_start(rowt[2 * i:2 * i + 2, :], g.rearrange("(k p) -> k p", p=P)).then_inc(rowt_in, 16)
            sp.dma_start(rowt[8:8 + E * KD, :], cent.rearrange("e (k p) -> (e k) p", p=P)).then_inc(rowt_in, 16)
            for k in range(KD):
                sp.dma_start(stage[k][:, :], wkv[k * P:(k + 1) * P, :]).then_inc(stage_in[k], 16)
            sp.dma_start(cos_t[:, :], rope_cos).then_inc(consts_in, 16)
            sp.dma_start(sin_t[:, :], rope_sin).then_inc(consts_in, 16)
            sp.dma_start(tri[:, :, :], tri_c).then_inc(consts_in, 16)
            sp.dma_start(basee[:, :, :], basee_c.partition_broadcast(P)).then_inc(consts_in, 16)
            sp.dma_start(tokid[:, :], ids_c).then_inc(consts_in, 16)
            sp.dma_start(oob[:, :], empty_c).then_inc(consts_in, 16)
            for i, src in enumerate((wq, wo)):
                src = src.rearrange("(k p) n -> p k n", p=P)
                sp.wait_ge(aw_split, i + 1)
                sp.dma_start(stage[i][:, :].rearrange("p (k n) -> p k n", k=src.shape[1]), src)\
                    .then_inc(stage_in[i], 16)
            sp.wait_ge(consts_in, N_CONST)
            sp.dma_start(ids_dram.rearrange("(p c) o -> p (c o)", p=P), oob[:, :]).then_inc(table_init, 16)

            def store_record(st):
                if st.has(RT):
                    wait_alone(sp, f2_ready, st.n(RT))
                    wait_alone(sp, alpha_seq, st.n(RT, AL_N))
                    sp.dma_start(rec_b[st.batch(RT)], rec[st.par(RT)][:, :]).then_inc(rec_stored, 16)

            def load_weights(st):
                if st.has(PJ):
                    g = st.batch(PJ)
                    if st.has(PJ + 1):
                        wait_alone(sp, w_split, st.n(PJ + 1, 2, 1))
                    else:
                        wait_alone(sp, aw_split, 3)
                    sp.dma_start(stage[0][:, :], w1_g[g]).then_inc(stage_in[0], 16)
                    if st.has(PJ + 1):
                        wait_alone(sp, w_split, st.n(PJ + 1, 2, 2))
                    else:
                        wait_alone(sp, aw_split, 4)
                    sp.dma_start(stage[1][:, :].rearrange("p (f d) -> p f d", d=D), w2_g[g]).then_inc(stage_in[1], 16)

            def step(st):
                if st.s < -1:
                    return
                store_record(st.behind())
                if st.has(L - 1):
                    if st.has(PJ):
                        wait_alone(sp, lnT_ready, st.n(PJ))
                    load_xc(st.batch(L - 1), st.par(L - 1))
                if st.has(WR):
                    if st.has(WR + 2):
                        wait_alone(sp, rec_stored, st.n(WR + 2, 16))
                    sp.dma_start(x1[st.par(WR)], x_b[st.batch(WR)]).then_inc(x1_in[st.par(WR)], 16)
                load_weights(st.ahead())

            pipeline(sp, step)

            sp.wait_ge(w_split, 2 * B)
            sp.dma_start(tabs, tabs_c.partition_broadcast(P)).then_inc(tabs_in, 16)
            sp.dma_start(b1_r, b1).then_inc(tabs_in, 16)
            sp.dma_start(lngb_r[:, 0:D], ln_g).then_inc(tabs_in, 16)
            sp.dma_start(lngb_r[:, D:2 * D], ln_b).then_inc(tabs_in, 16)
            sp.dma_start(b2_r, b2).then_inc(tabs_in, 16)

            sp.wait_ge(tiles_ready, 1)

            def copy_w1(t, par, free):
                e = sp.value_load(tile_e[0:1, bass.ds(t, 1)], min_val=0, max_val=E - 1)
                if free is not None:
                    wait_alone(sp, hid_ps, free)
                for i, w in enumerate((w1h, w1l)):
                    sp.dma_start(w1c[par][i], w[:, bass.ds(e, 1), :].rearrange("p a n -> p (a n)"))\
                        .then_inc(w1c_in[par], 16)

            for t in range(3):
                copy_w1(t, t % 2, 2 * (t - 1) if t >= 2 else None)
            with sp.Fori(0, (TILES - 3) // 2) as it:
                for t in (3, 4):
                    copy_w1(it * 2 + t, t % 2, it * 4 + 2 * (t - 1))
            for ring in range(4):
                sp.wait_ge(out_stored[ring], 16 * len(range(ring, TILES, 4)))

        @block.scalar
        def _(act):
            dsts = [wkv_s[0][:, 0, :], wkv_s[0][:, 1, :], wq_s[0], wo_s[0]]
            for i, dst in enumerate(dsts):
                act.wait_ge(stage_in[i % 2], 16 * (i // 2 + 1))
                src = stage[i % 2][:, :]
                if i >= 2:
                    src = src.rearrange("p (k n) -> p k n", k=dst.shape[1])
                act.activation(dst, src, ACT.Copy, scale=W_SCALE).then_inc(aw_high, 1)

            def high(ready, n, dst, src, scale, done):
                act.wait_ge(ready, n)
                act.activation(dst, src, ACT.Copy, scale=scale).then_inc(done, 1)

            def exp_pair(st, j):
                if st.has(AT):
                    act.wait_ge(nmax_ready, st.n(AT, 4, j + 1))
                    for i in range(2):
                        h = 2 * j + i
                        ins = act.activation(probs[j % 2][:, i, :], ps_s[:, i, 0:2 * P], ACT.Exp,
                                             bias=nmax[j % 2][:, i:i + 1],
                                             accum_out=rsum[st.par(AT)][:, h:h + 1])
                    ins.then_inc(probs_ready, 1)

            def probs_high(st, j):
                if st.has(AT):
                    high(pT_ready, st.n(AT, 4, j + 1), pT[0][j % 2][:, :], ps_t[j % 2][:, :], 1.0, pT_high)

            def k_latent_high(st):
                if st.has(PJ):
                    high(kl_ready, st.n(PJ), kT[0][st.par(PJ)][:, :, 1, :],
                         bank("kl")[:, :].rearrange("p (b t) -> p b t", b=NB), W_INV, kl_high)

            def q_high_half(st):
                if st.has(PJ):
                    high(q_ready, st.n(PJ), qT[0][:, :, :], bank("q")[:, :].rearrange("p (b t) -> p b t", b=NB),
                         W_INV * DH ** -0.5, q_high)

            def v_high(st, i):
                if st.has(PJ):
                    high((vx_ready, vl_ready)[i], st.n(PJ), v[0][st.par(PJ)][:, i, :],
                         bank(("vx", "vl")[i])[:, :], W_INV, (vx_high, vl_high)[i])

            def f_copy(st):
                if st.has(RT):
                    high(fT_ready, st.n(RT), fT[:, :], bank("fT")[:, 0:D], 1.0, fT_copied)

            def attn_high(st):
                if st.has(WR):
                    high(aT_ready, st.n(WR), aT[0][:, :, :],
                         bank("aT")[:, :].rearrange("p (b t) -> p b t", b=NB), 1.0, aT_high)

            def norm_affine(st):
                if st.has(L):
                    if st.has(L + 1):
                        act.wait_ge(kx_sum, st.n(L + 1))
                        act.wait_ge(lnT_split, st.n(L + 1))
                    else:
                        act.wait_ge(colt_ready, 1)
                    act.wait_ge(lnT_ready, st.n(L))
                    for c in range(2 * KD):
                        k, src = c // 2, c % 2
                        g, b = colt[:, 2 * src + k:2 * src + k + 1], colt[:, 4 + 2 * src + k:4 + 2 * src + k + 1]
                        ins = act.activation(lnT32[:, c * P:(c + 1) * P], bank("lnT")[:, c * P:(c + 1) * P],
                                             ACT.Identity, bias=b, scale=g)
                    ins.then_inc(lnT_affine, 1)

            def norm_high(st):
                if st.has(L):
                    if st.has(L + 1):
                        act.wait_ge(LAST_PROJECTION, st.n(L + 1))
                    high(lnT_affine, st.n(L), lnT[0][:, :, :], lnT32.rearrange("p (k t) -> p k t", k=KD), 1.0, lnT_high)

            def alpha_exp(st):
                if st.has(RT):
                    act.wait_ge(route_seq, st.n(RT, RO_N, 2))
                    act.wait_ge(ninv2_ready, st.n(RT))
                    act.activation(ealpha[:, 0:1], top8[:, 0:1], ACT.Exp, scale=ninv2).then_inc(ealpha_ready, 1)

            def w_group(st, i):
                if st.has(PJ):
                    g = st.batch(PJ)
                    wait_alone(act, stage_in[i], st.n(PJ, 16) + 32)
                    w = (w1h, w2h)[i][:, :, :].rearrange("p e (h n) -> p (e h) n", h=2)
                    act.activation(w[:, g, :], stage[i][:, :], ACT.Copy, scale=W_SCALE).then_inc(w_high, 1)

            def step(st):
                before = st.behind()
                probs_high(before, 3)
                exp_pair(st, 0)
                w_group(st, 0)
                k_latent_high(st)
                probs_high(st, 0)
                exp_pair(st, 1)
                w_group(st, 1)
                v_high(st, 0)
                exp_pair(st, 2)
                v_high(st, 1)
                attn_high(st)
                norm_affine(st)
                probs_high(st, 1)
                f_copy(st)
                exp_pair(st, 3)
                q_high_half(st)
                norm_high(st)
                probs_high(st, 2)
                alpha_exp(st)

            pipeline(act, step)

            act.wait_ge(tabs_in, 80)
            act.activation(b2_s[0], b2_r, ACT.Copy, scale=W_SCALE).then_inc(b2_high, 1)

            def x_high(n):
                if not (isinstance(n, int) and n == 1):
                    act.wait_ge(hid_ps, n * 2 - 2)
                act.wait_ge(xg_ready, n)
                act.activation(xgT[0], xg.rearrange("p (k t) -> p k t", k=KD), ACT.Copy).then_inc(xgT_high, 1)

            def h_high(n, par, hf):
                act.wait_ge(hid_biased, n + hf)
                act.activation(hid[0][par][:, 4 * hf:4 * hf + 4, :], hid32[hf][:, :, :], ACT.Relu).then_inc(hid_high, 1)

            def tile_step(t, it=None):
                r = 0 if it is None else it
                h_high(r * 8 + (2 * t + 1), t % 2, 0)
                if t + 1 < TILES:
                    x_high(r * 4 + (t + 2))
                h_high(r * 8 + (2 * t + 1), t % 2, 1)

            x_high(1)
            for t in range(T_FROM):
                tile_step(t)
            with act.Fori(0, (T_TO - T_FROM) // 4) as it:
                for t in range(T_FROM, T_FROM + 4):
                    tile_step(t, it)
            for t in range(T_TO, TILES):
                tile_step(t)

        @block.gpsimd
        def _(pool):
            pool.wait_ge(first_in, N_FIRST)
            eps, mhalf, half, mone = (cols[:, i:i + 3] for i in (0, 3, 6, 9))

            def norm_scales(st):
                if not (st.has(L) or st.has(RT)):
                    return
                k = [0]

                def done(ins):
                    k[0] += 1
                    ins.then_inc(norm_seq, 1)

                def former():
                    pool.wait_ge(norm_seq, st.n(L, NO_N, k[0]))

                if st.has(L):
                    pool.wait_ge(in_stats, st.n(L, 2))
                if st.has(RT):
                    pool.wait_ge(x1_stats, st.n(RT))
                done(pool.tensor_tensor(nv, mv[:, :, 1], eps, ALU.add))
                done(pool.tensor_tensor(nmean, mv[:, :, 0], mone, ALU.mult))
                former()
                done(pool.tensor_tensor(r1, nv, mhalf, ALU.pow))
                former()
                done(pool.tensor_tensor(nu[:, 1:3], mv[:, 1:3, 1], r1[:, 1:3], ALU.mult))
                former()
                done(pool.tensor_tensor(nv[:, 1:3], nu[:, 1:3], r1[:, 1:3], ALU.mult))
                former()
                done(pool.tensor_tensor(nu[:, 1:3], nv[:, 1:3], eps[:, 1:3], ALU.add))
                former()
                done(pool.tensor_tensor(r2[:, 1:3], nu[:, 1:3], mhalf[:, 1:3], ALU.pow))
                former()
                done(pool.tensor_tensor(s2[:, 1:3], r1[:, 1:3], r2[:, 1:3], ALU.mult))
                assert k[0] == NO_N

            def f2(st):
                if st.has(RT):
                    r = rec[st.par(RT)]
                    pool.tensor_tensor(r[:, INV2:INV2 + 1], nu[:, 2:3], half[:, 2:3], ALU.pow)
                    wait_alone(pool, norm_seq, st.n(L, NO_N))
                    pool.tensor_scalar(r[:, 0:D], x1[st.par(RT)], nmean[:, 2:3], s2[:, 2:3], ALU.add, ALU.mult)\
                        .then_inc(f2_ready, 1)
                    if st.has(RT + 1):
                        pool.wait_ge(ealpha_ready, st.n(RT + 1))
                    pool.wait_ge(f2_ready, st.n(RT))
                    pool.tensor_tensor(ninv2, r[:, INV2:INV2 + 1], mone[:, 0:1], ALU.mult).then_inc(ninv2_ready, 1)

            def rope(st):
                if st.has(PJ):
                    pool.wait_ge(kx_cos, st.n(PJ))
                    pool.wait_ge(rot_sin, st.n(PJ))
                    pool.tensor_tensor(k_cos[:, :, :], k_cos[:, :, :], k_sin[:, :, :], ALU.add).then_inc(kx_sum, 1)

            def k_context_high(st):
                if st.has(PJ):
                    wait_alone(pool, kx_sum, st.n(PJ))
                    pool.tensor_scalar(kT[0][st.par(PJ)][:, :, 0, :], k_cos[:, :, :], 1.0, 0.0, ALU.mult, ALU.add)\
                        .then_inc(kx_high, 1)

            def norm_inputs(st):
                if st.has(L):
                    c = xc[st.par(L)]
                    wait_alone(pool, norm_seq, st.n(L, NO_N))
                    pool.tensor_scalar(c[:, 0, :], c[:, 0, :], nmean[:, 0:1], r1[:, 0:1], ALU.add, ALU.mult)
                    pool.tensor_scalar(c[:, 1, :], c[:, 1, :], nmean[:, 1:2], s2[:, 1:2], ALU.add, ALU.mult)\
                        .then_inc(xn_ready, 1)

            def w_scale(st, i):
                if st.has(PJ):
                    wait_alone(pool, w_high, st.n(PJ, 2, i + 1))
                    pool.tensor_scalar(stage[i][:, :], stage[i][:, :], W_SCALE, 0.0, ALU.mult, ALU.add)\
                        .then_inc(w_scaled, 1)

            def w_low(st, i):
                if st.has(PJ):
                    g = st.batch(PJ)
                    wh = (w1h, w2h)[i][:, :, :].rearrange("p e (h n) -> p (e h) n", h=2)
                    wl = (w1l, w2l)[i][:, :, :].rearrange("p e (h n) -> p (e h) n", h=2)
                    wait_alone(pool, w_scaled, st.n(PJ, 2, i + 1))
                    pool.tensor_tensor(wl[:, g, :], stage[i][:, :], wh[:, g, :], ALU.subtract).then_inc(w_split, 1)

            def scatter_ids(st):
                if not st.has(SC):
                    return
                if st.it is None and st.s - SC == 0:
                    pool.wait_ge(table_init, 16)
                wait_alone(pool, place_seq, st.n(SC, PL_N))
                pool.indirect_dma_start(ids_dram, bass.IndirectOffsetOnAxis(ap=placei[:, 0:1], axis=0),
                                        tokid[:, :], None).then_inc(ids_scattered, 16)

            def step(st):
                after = st.ahead()
                w_scale(st, 0)
                norm_inputs(st)
                w_low(st, 0)
                rope(st)
                f2(st)
                k_context_high(st)
                scatter_ids(st)
                w_scale(st, 1)
                w_low(st, 1)
                norm_scales(after)

            pipeline(pool, step)

            pool.wait_ge(tiles_ready, 1)
            pool.wait_ge(ids_scattered, 16 * B)
            pool.indirect_dma_start(ids_t, None, ids_dram.rearrange("(r c) o -> r (c o)", c=P),
                                    bass.IndirectOffsetOnAxis(ap=tile_r[0:NT, 0:1], axis=0)).then_inc(ids_in, 16)

            pool.wait_ge(idt_ready, 1)
            pool.wait_ge(buffers_clear, 1)
            pool.wait_ge(rec_stored, 16 * B)

            def gather(t):
                pool.indirect_dma_start(g_rec[t % 4], None, rec_dram,
                                        bass.IndirectOffsetOnAxis(ap=idt[:, t:t + 1], axis=0),
                                        bounds_check=TOK - 1, oob_is_err=False).then_inc(g_in[t % 4], 16)

            def scatter(t):
                pool.wait_ge(y2_out, t + 1)
                pool.indirect_dma_start(outf, bass.IndirectOffsetOnAxis(ap=idt[:, t:t + 1], axis=0),
                                        yout[t % 2], None,
                                        bounds_check=TOK - 1, oob_is_err=False).then_inc(out_stored[t % 4], 16)

            for t in range(4):
                gather(t)
            for t in range(TILES + 1):
                if t + 4 < TILES:
                    pool.wait_ge(y2_base, t + 1)
                    gather(t + 4)
                if t >= 1:
                    scatter(t - 1)

        @block.vector
        def _(dve):
            dve.memset(mv, 1.0).then_inc(setup_dve, 1)
            dve.memset(ohcum[0][:, :], 0.0).then_inc(setup_dve, 1)
            for r in rec:
                ins = dve.memset(r[:, 2 * D:REC], 0.0)
            ins.then_inc(setup_dve, 1)

            def low(ready, n, dst, src, scale, high, done):
                dve.wait_ge(ready, n)
                dve.scalar_tensor_tensor(dst, src, scale, high, ALU.mult, ALU.subtract).then_inc(done, 1)

            srcs = [wkv_s, wkv_s, wq_s, wo_s]

            def aw_low(i):
                d = srcs[i]
                hi, lo = (d[0][:, i, :], d[1][:, i, :]) if i < 2 else (d[0], d[1])
                src = stage[i % 2][:, :]
                if i >= 2:
                    src = src.rearrange("p (k n) -> p k n", k=hi.shape[1])
                low(aw_high, i + 1, lo, src, W_SCALE, hi, aw_split)

            def input_stats(st):
                if st.has(L - 1):
                    par = st.par(L - 1)
                    dve.wait_ge(xc_in[par], st.n(L - 1, 32, ring=2))
                    for i in range(2):
                        ins = dve.bn_stats(lst[:, i, :], xc[par][:, i, :])
                    ins.then_inc(in_bn, 1)

            def input_moments(st):
                if st.has(L - 1):
                    if st.has(L):
                        dve.wait_ge(xn_ready, st.n(L))
                    wait_alone(dve, in_bn, st.n(L - 1))
                    for i in range(2):
                        dve.bn_aggr(mv[:, i, :], lst[:, i, :]).then_inc(in_stats, 1)

            def row_max(st, j):
                if st.has(AT):
                    dve.wait_ge(scores_ready, st.n(AT, 4, j + 1))
                    dve.tensor_reduce(nmax[j % 2][:, :], ps_s[:, :, 0:2 * P],
                                      AX_X, ALU.max, negate=True).then_inc(nmax_ready, 1)

            def probs_low(st, j):
                if st.has(AT):
                    low(pT_high, st.n(AT, 4, j + 1), pT[1][j % 2][:, :], ps_t[j % 2][:, :], 1.0,
                        pT[0][j % 2][:, :], pT_split)

            def blocks(t):
                return t[:, :].rearrange("p (b t) -> p b t", b=NB)

            def k_cosine(st):
                if st.has(PJ):
                    if st.has(PJ + 1):
                        dve.wait_ge(kx_split, st.n(PJ + 1))
                    else:
                        dve.wait_ge(consts_in, N_CONST)
                    dve.wait_ge(kx_ready, st.n(PJ))
                    dve.tensor_tensor(k_cos[:, :, :], blocks(bank("kx")),
                                      cos_t[:, :].unsqueeze(1).broadcast_to([P, NB, P]), ALU.mult).then_inc(kx_cos, 1)

            def k_sine(st):
                if st.has(PJ):
                    if st.has(PJ + 1):
                        dve.wait_ge(kx_sum, st.n(PJ + 1))
                    else:
                        dve.wait_ge(consts_in, N_CONST)
                    dve.wait_ge(rot_ready, st.n(PJ))
                    dve.tensor_tensor(k_sin[:, :, :], blocks(bank("rot")),
                                      sin_t[:, :].unsqueeze(1).broadcast_to([P, NB, P]), ALU.mult).then_inc(rot_sin, 1)

            def k_context_low(st):
                if st.has(PJ):
                    dve.wait_ge(kx_high, st.n(PJ))
                    dve.tensor_tensor(kT[1][st.par(PJ)][:, :, 0, :], k_cos[:, :, :], kT[0][st.par(PJ)][:, :, 0, :],
                                      ALU.subtract).then_inc(kx_split, 1)

            def k_latent_low(st):
                if st.has(PJ):
                    low(kl_high, st.n(PJ), kT[1][st.par(PJ)][:, :, 1, :], blocks(bank("kl")), W_INV,
                        kT[0][st.par(PJ)][:, :, 1, :], kl_split)

            def v_low(st, i):
                if st.has(PJ):
                    low((vx_high, vl_high)[i], st.n(PJ), v[1][st.par(PJ)][:, i, :], bank(("vx", "vl")[i])[:, :], W_INV,
                        v[0][st.par(PJ)][:, i, :], (vx_split, vl_split)[i])

            def q_low(st):
                if st.has(PJ):
                    low(q_high, st.n(PJ), qT[1][:, :, :], blocks(bank("q")), W_INV * DH ** -0.5, qT[0][:, :, :], q_split)

            def norm_low(st):
                if st.has(L):
                    low(lnT_high, st.n(L), lnT[1][:, :, :], lnT32.rearrange("p (k t) -> p k t", k=KD), 1.0,
                        lnT[0][:, :, :], lnT_split)

            def row_sums(st):
                if st.has(WR):
                    dve.wait_ge(probs_ready, st.n(WR, 4))
                    dve.reciprocal(rinv[:, :], rsum[st.par(WR)][:, :]).then_inc(rinv_ready, 1)

            def attn_norm(st):
                if st.has(WR):
                    if st.first(WR):
                        dve.wait_ge(table_init, 16)
                    if st.has(WR + 1):
                        dve.wait_ge(aT_ready, st.n(WR + 1))
                    dve.wait_ge(pv_done, st.n(WR, 4))
                    dve.wait_ge(rinv_ready, st.n(WR))
                    dve.tensor_tensor(attn[:, :].rearrange("p (h d) -> p h d", h=H),
                                      ps_o[:, :].rearrange("p (h d) -> p h d", h=H),
                                      rinv[:, :].unsqueeze(2).broadcast_to([P, H, DH]), ALU.mult).then_inc(attn_ready, 1)

            def attn_low(st):
                if st.has(WR):
                    low(aT_high, st.n(WR), aT[1][:, :, :], blocks(bank("aT")), 1.0, aT[0][:, :, :], aT_split)

            def residual(st):
                if st.has(WR):
                    xt = x1[st.par(WR)]
                    dve.wait_ge(x1_in[st.par(WR)], st.n(WR, 16, ring=2))
                    dve.wait_ge(y_ready, st.n(WR))
                    dve.scalar_tensor_tensor(xt, bank("y")[:, 0:D], W_INV, xt, ALU.mult, ALU.add).then_inc(x1_ready, 1)

            def x1_stats_of(st):
                if st.has(WR):
                    dve.wait_ge(x1_ready, st.n(WR))
                    dve.bn_stats(fst[:, :], x1[st.par(WR)]).then_inc(x1_bn, 1)

            def x1_moments(st):
                if st.has(WR):
                    if st.has(WR + 1):
                        dve.wait_ge(f2_ready, st.n(WR + 1))
                    wait_alone(dve, x1_bn, st.n(WR))
                    dve.bn_aggr(mv[:, 2, :], fst[:, :]).then_inc(x1_stats, 1)

            def route_max(st):
                if st.has(RT):
                    dve.wait_ge(aff_ready, st.n(RT))
                    dve.max(top8[:, :], bank("aff")[:, 0:E]).then_inc(route_seq, 2)

            def route_index(st):
                if st.has(RT):
                    wait_alone(dve, route_seq, st.n(RT, RO_N, 2))
                    dve.max_index(idx8[:, :], top8[:, :], bank("aff")[:, 0:E]).then_inc(route_seq, 1)

            def route_float(st):
                if st.has(RT):
                    dve.wait_ge(route_seq, st.n(RT, RO_N, 3))
                    dve.tensor_copy(eidf[:, :], idx8[:, 0:1]).then_inc(route_seq, 1)

            def route_count(st):
                if st.has(RT):
                    par = st.par(RT)
                    dve.wait_ge(route_seq, st.n(RT, RO_N, 4))
                    dve.tensor_scalar(oneh[:, :], basee[:, 1, :], eidf[:, 0:1], None, ALU.is_equal).then_inc(route_seq, 1)
                    dve.wait_ge(route_seq, st.n(RT, RO_N, 5))
                    dve.tensor_tensor(ohcum[1 - par][:, :], ohcum[par][:, :], oneh[:, :], ALU.add).then_inc(route_seq, 1)

            def alpha(st):
                if st.has(RT):
                    dve.wait_ge(ealpha_ready, st.n(RT))
                    dve.tensor_scalar(ealpha[:, 1:2], ealpha[:, 0:1], 1.0, W_SCALE, ALU.add, ALU.mult)\
                        .then_inc(alpha_seq, 1)
                    dve.wait_ge(alpha_seq, st.n(RT, AL_N, 1))
                    dve.reciprocal(rec[st.par(RT)][:, ALPHA:ALPHA + 1], ealpha[:, 1:2]).then_inc(alpha_seq, 1)

            def place_ranks(st):
                if st.has(RT):
                    dve.wait_ge(pref_ready, st.n(RT))
                    dve.tensor_tensor(place[:, 0, :], bank("pref")[:, 0:E], basee[:, 0, :], ALU.add).then_inc(place_seq, 1)

            def place_mask(st):
                if st.has(RT):
                    dve.wait_ge(place_seq, st.n(RT, PL_N, 1))
                    dve.tensor_tensor(place[:, 1, :], place[:, 0, :], oneh[:, :], ALU.mult).then_inc(place_seq, 1)

            def place_sum(st):
                if st.has(RT):
                    dve.wait_ge(place_seq, st.n(RT, PL_N, 2))
                    dve.tensor_reduce(placef[:, :], place[:, 1, :], AX_X, ALU.add)\
                        .then_inc(place_seq, 1 if st.has(RT + 1) else 2)
                    if st.has(RT + 1):
                        dve.wait_ge(ids_scattered, st.n(RT + 1, 16))
                        dve.tensor_scalar(tokid[:, :], tokid[:, :], float(P), None, ALU.add).then_inc(place_seq, 1)

            def place_number(st):
                if st.has(RT):
                    dve.wait_ge(place_seq, st.n(RT, PL_N, 4))
                    dve.tensor_copy(placei[:, :], placef[:, :]).then_inc(place_seq, 1)

            def first_weights():
                dve.wait_ge(colt_ps, 1)
                dve.tensor_copy(colt[:, :], ps_o[:, 0:8 + E * KD]).then_inc(colt_ready, 1)
                for i in range(2):
                    aw_low(i)
                dve.wait_ge(aw_split, 2)
                for hl, k in ((0, 0), (0, 1), (1, 0), (1, 1)):
                    k4 = wkv_s[hl][:, k, 0:INNER].rearrange("p (h a d) -> p h a d", a=2, d=DH // 2)
                    r4 = rot_s[hl][:, k, :].rearrange("p (h a d) -> p h a d", a=2, d=DH // 2)
                    dve.tensor_scalar(r4[:, :, 0, :], k4[:, :, 1, :], -1.0, None, ALU.mult).then_inc(rot_made, 1)
                    dve.tensor_copy(r4[:, :, 1, :], k4[:, :, 0, :]).then_inc(rot_made, 1)

            def step(st):
                if st.s == -1:
                    first_weights()
                if st.s == 0:
                    aw_low(2)
                    aw_low(3)
                before, after = st.behind(), st.ahead()
                probs_low(before, 3)
                k_cosine(st)
                row_max(st, 1)
                row_sums(st)
                k_latent_low(st)
                probs_low(st, 0)
                k_sine(st)
                attn_norm(st)
                row_max(st, 2)
                place_ranks(before)
                v_low(st, 0)
                input_stats(st)
                place_mask(before)
                input_moments(st)
                place_sum(before)
                v_low(st, 1)
                attn_low(st)
                place_number(before)
                row_max(st, 3)
                k_context_low(st)
                probs_low(st, 1)
                q_low(st)
                residual(st)
                norm_low(st)
                route_max(st)
                x1_stats_of(st)
                route_index(st)
                row_max(after, 0)
                x1_moments(st)
                route_float(st)
                probs_low(st, 2)
                route_count(st)
                alpha(st)

            pipeline(dve, step)

            pos = [0]

            def piece(n):
                a = rt[:, pos[0]:pos[0] + n]
                pos[0] += n
                return a

            seq = [0]

            def link(ins):
                seq[0] += 1
                ins.then_inc(tile_seq, 1)
                dve.wait_ge(tile_seq, seq[0])

            cnt, ntile, cum, past, gone = (piece(E) for _ in range(5))
            more = piece(16 * E).rearrange("p (e k) -> p e k", e=E)
            upto = piece(E * E).rearrange("p (a b) -> p a b", a=E)
            n_e, n_gone, rest, rowf = (piece(1) for _ in range(4))
            thr = tabs[:, 0:16].unsqueeze(1).broadcast_to([P, E, 16])
            mask = tabs[:, 16:16 + E * E].rearrange("p (a b) -> p a b", a=E)
            tcol = cols[:, 12:13]
            dve.wait_ge(tabs_in, 80)
            dve.wait_ge(counts_ps, 1)
            link(dve.tensor_copy(cnt, ps_o[:, 0:E]))
            link(dve.tensor_tensor(more, cnt.unsqueeze(2).broadcast_to([P, E, 16]), thr, ALU.is_gt))
            link(dve.tensor_reduce(ntile, more, AX_X, ALU.add))
            link(dve.tensor_tensor(upto, mask, ntile.unsqueeze(1).broadcast_to([P, E, E]), ALU.mult))
            link(dve.tensor_reduce(cum, upto, AX_X, ALU.add))
            link(dve.tensor_scalar(past, cum, tcol, None, ALU.is_le))
            link(dve.tensor_tensor(gone, past, ntile, ALU.mult))
            dve.tensor_reduce(n_e, past, AX_X, ALU.add)
            link(dve.tensor_reduce(n_gone, gone, AX_X, ALU.add))
            dve.tensor_scalar(ef_t, n_e, float(E - 1), None, ALU.min)
            link(dve.tensor_tensor(rest, tcol, n_gone, ALU.subtract))
            dve.tensor_scalar(oh_t, basee[:, 1, :], ef_t, None, ALU.is_equal).then_inc(tile_seq, 1)
            dve.scalar_tensor_tensor(rowf, n_e, float(REGION // P), rest, ALU.mult, ALU.add).then_inc(tile_seq, 1)
            dve.wait_ge(tile_seq, seq[0] + 2)
            dve.tensor_copy(tile_r[:, :], rowf).then_inc(tile_seq, 1)
            dve.wait_ge(turned_ps, 1)
            dve.tensor_copy(tile_e[:, :], ps_o[0:1, 0:P])
            dve.tensor_copy(oh_e, ps_t[0][0:E, 0:P])
            dve.tensor_copy(oh_eh, ps_t[0][0:E, 0:P]).then_inc(tiles_ready, 1)
            for g in g_rec:
                ins = dve.memset(g, 0.0)
            ins.then_inc(buffers_clear, 1)
            low(b2_high, 1, b2_s[1], b2_r, W_SCALE, b2_s[0], b2_split)
            dve.wait_ge(cols_ps, 1)
            dve.tensor_copy(tile_c, ps_s[:, 0, 0:NCOL * NT].rearrange("p (c t) -> p c t", c=NCOL)).then_inc(cols_ready, 1)
            dve.wait_ge(ids_in, 16)
            dve.tensor_copy(ids_f, ids_t).then_inc(idf_ready, 1)
            dve.wait_ge(idt_ps, 1)
            dve.tensor_copy(idt[:, :], ps_t[1][:, 0:NT]).then_inc(idt_ready, 1)
            dve.wait_ge(cols_ready, 1)

            def column(c, t):
                return tile_c[:, c, bass.ds(t, 1)]

            def x_affine(t, n):
                if not (isinstance(n, int) and n == 1):
                    dve.wait_ge(xgT_split, n - 1)
                dve.wait_ge(xgT_ps, n)
                for k in range(KD):
                    ins = dve.tensor_scalar(xg[:, k * P:(k + 1) * P], ps_u[2][:, k * P:(k + 1) * P],
                                            column(k, t), column(KD + k, t), ALU.mult, ALU.add)
                ins.then_inc(xg_ready, 1)

            def x_low(n):
                dve.wait_ge(xgT_high, n)
                dve.tensor_tensor(xgT[1], xg.rearrange("p (k t) -> p k t", k=KD), xgT[0], ALU.subtract)\
                    .then_inc(xgT_split, 1)

            def h_bias(t, n, par, hf):
                if not (isinstance(n, int) and n == 1):
                    dve.wait_ge(hid_split, n + hf - 2)
                dve.wait_ge(hid_ps, n + hf)
                c = 2 * KD + 4 * hf
                bias = tile_c[:, c:c + 4, bass.ds(t, 1)]
                dve.scalar_tensor_tensor(hid32[hf][:, :, :], ps_h[par][hf].rearrange("p (f t) -> p f t", t=P), W_INV,
                                         bias.broadcast_to([P, 4, P]), ALU.mult, ALU.add).then_inc(hid_biased, 1)

            def h_low(n, par, hf):
                dve.wait_ge(hid_high, n + hf)
                dve.scalar_tensor_tensor(hid[1][par][:, 4 * hf:4 * hf + 4, :], hid32[hf][:, :, :], 0.0,
                                         hid[0][par][:, 4 * hf:4 * hf + 4, :], ALU.max, ALU.subtract)\
                    .then_inc(hid_split, 1)

            def y_base(n, par, ring):
                r = g_rec[ring]
                if not isinstance(n, int) or n > 2:
                    dve.wait_ge(y2_out, n - 2)
                dve.tensor_copy(ybase[par][:, ALPHA:ALPHA + 1], r[:, ALPHA:ALPHA + 1])
                dve.scalar_tensor_tensor(ybase[par][:, 0:D], r[:, 0:D], r[:, INV2:INV2 + 1], r[:, D:2 * D],
                                         ALU.mult, ALU.add).then_inc(y2_base, 1)

            def y_out(n, par, ring, free, first):
                if not first:
                    dve.wait_ge(out_stored[(ring + 2) % 4], free)
                dve.wait_ge(y2_base, n)
                dve.wait_ge(y2_ps, n)
                dve.scalar_tensor_tensor(yout[par], ps_u[par][:, 0:D], ybase[par][:, ALPHA:ALPHA + 1],
                                         ybase[par][:, 0:D], ALU.mult, ALU.add).then_inc(y2_out, 1)

            def tile_step(t, it=None):
                r = 0 if it is None else it
                if t + 1 < TILES:
                    x_affine(r * 4 + (t + 1), r * 4 + (t + 2))
                if t >= 2:
                    y_out(r * 4 + (t - 1), t % 2, (t - 2) % 4, r * 16 + 16 * ((t - 4) // 4 + 1), t < 4)
                n = r * 8 + (2 * t + 1)
                if t < TILES:
                    h_bias(r * 4 + t, n, t % 2, 0)
                    h_bias(r * 4 + t, n, t % 2, 1)
                    h_low(n, t % 2, 0)
                if t + 1 < TILES:
                    x_low(r * 4 + (t + 2))
                if t < TILES:
                    h_low(n, t % 2, 1)
                    y_base(r * 4 + (t + 1), t % 2, t % 4)

            x_affine(0, 1)
            x_low(1)
            for t in range(T_FROM):
                tile_step(t)
            with dve.Fori(0, (T_TO - T_FROM) // 4) as it:
                for t in range(T_FROM, T_FROM + 4):
                    tile_step(t, it)
            for t in range(T_TO, TILES + 2):
                tile_step(t)

        @block.tensor
        def _(pe):
            PAIRS = ((0, 0), (0, 1), (1, 0))

            def split_mm(out, lhs, rhs):
                n = len(lhs) * len(PAIRS)
                c = 0
                for k in range(len(lhs)):
                    for a, b in PAIRS:
                        ins = pe.matmul(out, lhs[k][a], rhs[k][b], start=(c == 0), stop=(c == n - 1))
                        c += 1
                return ins

            def unit(st, name):
                k = ORDER.index(name)
                for m in range(k - 3, -36, -3):
                    i, off = m % 12, -(m // 12)
                    _, lag, evac, per, last = UNITS[i]
                    if st.base.has(lag + off):
                        pe.wait_ge(evac, st.base.n(lag + off, per, last))
                        break
                return bank(name)

            def scores(st, j):
                if not st.has(AT):
                    return
                if j == 0:
                    pe.wait_ge(q_split, st.n(AT))
                    pe.wait_ge(kx_split, st.n(AT))
                    pe.wait_ge(kl_split, st.n(AT))
                    if st.has(AT + 1):
                        pe.wait_ge(probs_ready, st.n(AT + 1, 4))
                else:
                    pe.wait_ge(probs_ready, st.n(AT, 4, j))
                par = st.par(AT)
                for c, (a, b) in enumerate(PAIRS):
                    for i in range(2):
                        r = slice(64 * i, 64 * i + 64)
                        ins = pe.matmul(ps_s[:, i, 0:2 * P], qT[a][r, j, :],
                                        kT[b][par][r, j, :, :].rearrange("p s t -> p (s t)"),
                                        start=(c == 0), stop=(c == 2))
                ins.then_inc(scores_ready, 1)

            def turn_probs(st, j):
                if st.has(AT):
                    pe.wait_ge(probs_ready, st.n(AT, 4, j + 1))
                    for c in range(4):
                        ins = pe.transpose(ps_t[j % 2][:, c * P:(c + 1) * P],
                                           probs[j % 2][:, c // 2, (c % 2) * P:(c % 2 + 1) * P], ident[:, :])
                    ins.then_inc(pT_ready, 1)

            def values(st, j):
                if not st.has(AT):
                    return
                if j == 0:
                    pe.wait_ge(vx_split, st.n(AT))
                    pe.wait_ge(vl_split, st.n(AT))
                    if st.has(AT + 1):
                        pe.wait_ge(attn_ready, st.n(AT + 1))
                pe.wait_ge(pT_split, st.n(AT, 4, j + 1))
                par = st.par(AT)
                for i in range(2):
                    h = 2 * j + i
                    ins = split_mm(ps_o[:, h * DH:(h + 1) * DH],
                                   [[pT[a][j % 2][:, (2 * i + c) * P:(2 * i + c + 1) * P] for a in range(2)]
                                    for c in range(2)],
                                   [[v[a][par][:, c, h * DH:(h + 1) * DH] for a in range(2)] for c in range(2)])
                ins.then_inc(pv_done, 1)

            def inputs_ready(st, name):
                pe.wait_ge(lnT_split, st.n(PJ))
                if st.first(PJ):
                    pe.wait_ge(aw_split, 3 if name == "q" else 2)
                    if name == "rot":
                        pe.wait_ge(rot_made, 8)

            def project_T(st, name, w, col0, src, ready):
                if not st.has(PJ):
                    return
                inputs_ready(st, name)
                bk = unit(st, name)
                for n in range(NB):
                    ins = split_mm(bk[:, n * P:(n + 1) * P],
                                   [[w[a][:, k, col0 + n * P:col0 + (n + 1) * P] for a in range(2)] for k in range(KD)],
                                   [[lnT[a][:, k, src * P:(src + 1) * P] for a in range(2)] for k in range(KD)])
                ins.then_inc(ready, 1)

            def project_v(st, name, src, ready):
                if not st.has(PJ):
                    return
                inputs_ready(st, name)
                bk = unit(st, name)
                split_mm(bk[:, :],
                         [[lnT[a][:, k, src * P:(src + 1) * P] for a in range(2)] for k in range(KD)],
                         [[wkv_s[a][:, k, INNER:2 * INNER] for a in range(2)] for k in range(KD)]).then_inc(ready, 1)

            def turn_f2(st):
                if st.has(RT):
                    bk = unit(st, "fT")
                    pe.wait_ge(f2_ready, st.n(RT))
                    for k in range(KD):
                        ins = pe.transpose(bk[:, k * P:(k + 1) * P], rec[st.par(RT)][:, k * P:(k + 1) * P], ident[:, :])
                    ins.then_inc(fT_ready, 1)

            def affinities(st):
                if st.has(RT):
                    bk = unit(st, "aff")
                    pe.wait_ge(fT_copied, st.n(RT))
                    ck = colt[:, 8:8 + E * KD].rearrange("p (e k) -> p k e", k=KD)
                    for k in range(KD):
                        ins = pe.matmul(bk[:, 0:E], fT[:, k * P:(k + 1) * P], ck[:, k, :], start=(k == 0), stop=(k == KD - 1))
                    ins.then_inc(aff_ready, 1)

            def turn_attn(st):
                if st.has(WR):
                    bk = unit(st, "aT")
                    pe.wait_ge(attn_ready, st.n(WR))
                    for n in range(NB):
                        ins = pe.transpose(bk[:, n * P:(n + 1) * P], attn[:, n * P:(n + 1) * P], ident[:, :])
                    ins.then_inc(aT_ready, 1)

            def turn_inputs(st):
                if st.has(L):
                    bk = unit(st, "lnT")
                    pe.wait_ge(xn_ready, st.n(L))
                    for k in range(KD):
                        for s in range(2):
                            c = 2 * k + s
                            ins = pe.transpose(bk[:, c * P:(c + 1) * P], xc[st.par(L)][:, s, k * P:(k + 1) * P],
                                               ident[:, :])
                    ins.then_inc(lnT_ready, 1)

            def project_attn(st):
                if st.has(WR):
                    bk = unit(st, "y")
                    pe.wait_ge(aT_split, st.n(WR))
                    if st.first(WR):
                        pe.wait_ge(aw_split, 4)
                    split_mm(bk[:, 0:D], [[aT[a][:, n, :] for a in range(2)] for n in range(NB)],
                             [[wo_s[a][:, n, :] for a in range(2)] for n in range(NB)]).then_inc(y_ready, 1)

            def ranks(st):
                if st.has(RT):
                    bk = unit(st, "pref")
                    pe.wait_ge(route_seq, st.n(RT, RO_N))
                    pe.matmul(bk[:, 0:E], tri[:, 0, :], oneh[:, :], start=True, stop=False)
                    pe.matmul(bk[:, 0:E], tri[:, 1, :], ohcum[st.par(RT)][:, :], start=False, stop=True)\
                        .then_inc(pref_ready, 1)

            def step(st):
                before = st.behind()
                turn_probs(before, 3)
                scores(st, 0)
                project_T(st, "kx", wkv_s, 0, 0, kx_ready)
                project_T(st, "kl", wkv_s, 0, 1, kl_ready)
                values(before, 2)
                scores(st, 1)
                turn_probs(st, 0)
                project_T(st, "rot", rot_s, 0, 0, rot_ready)
                values(before, 3)
                project_v(st, "vx", 0, vx_ready)
                scores(st, 2)
                ranks(before)
                project_v(st, "vl", 1, vl_ready)
                turn_probs(st, 1)
                turn_attn(st)
                turn_inputs(st)
                values(st, 0)
                scores(st, 3)
                turn_f2(st)
                turn_probs(st, 2)
                project_T(st, "q", wq_s, 0, 1, q_ready)
                project_attn(st)
                affinities(st)
                values(st, 1)

            pe.wait_ge(first_in, N_FIRST)
            pe.wait_ge(rowt_in, 80)
            n = 8 + E * KD
            pe.transpose(ps_o[:, 0:n], rowt, ident[0:n, 0:n]).then_inc(colt_ps, 1)
            pipeline(pe, step)

            pe.wait_ge(route_seq, RO_N * B)
            pe.matmul(ps_o[:, 0:E], tri[:, 1, :], ohcum[0][:, :], start=True, stop=True).then_inc(counts_ps, 1)
            pe.wait_ge(tile_seq, 12)
            pe.matmul(ps_o[0:1, 0:P], ef_t, ident[:, :], start=True, stop=True)
            pe.transpose(ps_t[0][0:E, 0:P], oh_t, ident[:, :]).then_inc(turned_ps, 1)
            pe.wait_ge(tiles_ready, 1)
            srcs = [lngb_r[:, k * P:(k + 1) * P] for k in range(2 * KD)] + [b1_r[:, f * P:(f + 1) * P] for f in range(FB)]
            for c, src in enumerate(srcs):
                ins = pe.matmul(ps_s[:, 0, c * NT:(c + 1) * NT], src, oh_e[:, 0:NT], start=True, stop=True)
            ins.then_inc(cols_ps, 1)
            pe.wait_ge(idf_ready, 1)
            pe.transpose(ps_t[1][:, 0:NT], ids_f, ident[0:NT, 0:NT]).then_inc(idt_ps, 1)
            pe.wait_ge(b2_split, 1)
            pe.wait_ge(cols_ready, 1)
            pe.wait_ge(idt_ready, 1)

            pe.wait_ge(w_split, 2 * B)

            def expert(t):
                return pe.value_load(tile_e[0:1, bass.ds(t, 1)], min_val=0, max_val=E - 1)

            def x_turn(ring, n, n_rec):
                pe.wait_ge(g_in[ring], n_rec)
                if not (isinstance(n, int) and n == 0):
                    pe.wait_ge(xg_ready, n)
                for k in range(KD):
                    ins = pe.transpose(ps_u[2][:, k * P:(k + 1) * P], g_rec[ring][:, k * P:(k + 1) * P], ident[:, :])
                ins.then_inc(xgT_ps, 1)

            def hidden(n, n_w1, par):
                pe.wait_ge(w1c_in[par], n_w1)
                pe.wait_ge(xgT_split, n)
                for f in range(FB):
                    ins = split_mm(ps_h[par][f // 4][:, (f % 4) * P:(f % 4 + 1) * P],
                                   [[w[:, k * FF + f * P:k * FF + (f + 1) * P] for w in w1c[par]] for k in range(KD)],
                                   [[xgT[a][:, k, :] for a in range(2)] for k in range(KD)])
                    if f % 4 == 3:
                        ins.then_inc(hid_ps, 1)

            def project_out(t, n, par, free):
                e = expert(t)
                if free is not None:
                    pe.wait_ge(y2_out, free)
                pe.wait_ge(hid_split, n)
                oh = oh_eh[:, bass.ds(t, 1)].broadcast_to([E, P])
                for i in range(2):
                    pe.matmul(ps_u[par][:, 0:D], oh, b2_s[i], start=(i == 0), stop=False)
                split = [(f, a, b) for f in range(FB) for a, b in PAIRS]
                for f, a, b in split:
                    ins = pe.matmul(ps_u[par][:, 0:D], hid[a][par][:, f, :], (w2h, w2l)[b][:, e, f * D:(f + 1) * D],
                                    start=False, stop=((f, a, b) == split[-1]))
                ins.then_inc(y2_ps, 1)

            def tile_step(t, it=None):
                r = 0 if it is None else it
                if t + 1 < TILES:
                    x_turn((t + 1) % 4, r * 4 + (t + 1), r * 16 + 16 * ((t + 1) // 4 + 1))
                if t < TILES:
                    hidden(r * 4 + (t + 1), r * 64 + 32 * (t // 2 + 1), t % 2)
                if t >= 1:
                    project_out(r * 4 + (t - 1), r * 8 + 2 * t, (t - 1) % 2, r * 4 + (t - 2) if t > 2 else None)

            x_turn(0, 0, 16)
            for t in range(T_FROM):
                tile_step(t)
            with pe.Fori(0, (T_TO - T_FROM) // 4) as it:
                for t in range(T_FROM, T_FROM + 4):
                    tile_step(t, it)
            for t in range(T_TO, TILES + 1):
                tile_step(t)


_INS = ['x', 'ctx_1024', 'L0_xattn_gamma_x', 'L0_xattn_beta_x', 'L0_xattn_gamma_l', 'L0_xattn_beta_l',
        'L0_xattn_Wq', 'L0_xattn_Wkv', 'L0_xattn_Wo', 'L0_ffn_centroids', 'L0_ffn_ln_g', 'L0_ffn_ln_b',
        'L0_ffn_w1', 'L0_ffn_b1', 'L0_ffn_w2', 'L0_ffn_b2']


def _constants(tokens, experts):
    import numpy as np
    p = 128
    dh, base = 64, 10000.0
    inv = (np.float32(1.0) / np.float32(base) ** (np.arange(0, dh, 2, dtype=np.float32) / np.float32(dh)))
    ang = np.arange(p, dtype=np.float32)[:, None] * inv[None, :].astype(np.float32)
    ang = np.concatenate([ang, ang, ang, ang], axis=1)
    cos = (np.cos(ang).T / 64.0).astype(np.float32)
    sin = (np.sin(ang).T / 64.0).astype(np.float32)
    tri = np.zeros((p, 2, p), np.float16)
    tri[:, 0, :] = np.triu(np.ones((p, p)))
    tri[:, 1, :] = 1.0
    cols = np.zeros((p, 16), np.float32)
    cols[:, 0:3], cols[:, 3:6], cols[:, 6:9], cols[:, 9:12] = 1e-5, -0.5, 0.5, -1.0
    cols[:, 12] = np.arange(p)
    nt = tokens // p + experts
    tabs = np.concatenate([np.arange(16) * float(p), np.tril(np.ones((experts, experts))).reshape(-1), [0.0]])
    basee = np.stack([np.arange(experts) * float(tokens) - 1.0, np.arange(experts)])
    places = experts * tokens // p + nt
    empty = np.full((p, places), 2 * tokens, np.int32)
    return {"rope_cos": np.ascontiguousarray(cos), "rope_sin": np.ascontiguousarray(sin),
            "ident": np.eye(p, dtype=np.float32), "tri": tri, "cols": cols,
            "tabs": tabs.astype(np.float32), "basee": basee.astype(np.float32),
            "ids": np.arange(p, dtype=np.int32)[:, None], "empty": empty}


def kernel(**inputs):
    import numpy as _np
    import concourse.bacc as _bacc
    from concourse import mybir as _mybir
    from concourse.bass_utils import run_bass_kernel_spmd as _run

    nc = _bacc.Bacc("TRN2", target_bir_lowering=False, num_devices=1)
    arrays, args = {}, []
    shape = inputs['x'].shape
    given = [(n, _np.ascontiguousarray(inputs[n])) for n in _INS]
    given += list(_constants(shape[0] * shape[1], inputs['L0_ffn_w1'].shape[0]).items())
    for name, a in given:
        arrays[f"in_{name}_dram"] = a
        args.append(nc.dram_tensor(f"in_{name}_dram", a.shape, _mybir.dt.from_np(a.dtype), kind="ExternalInput").ap())
    args.append(nc.dram_tensor("out_0_dram", shape, _mybir.dt.float32, kind="ExternalOutput").ap())
    xattn_moe_kernel(nc, *args)
    r = _run(nc, [arrays], core_ids=[0])
    return r.results[0]["out_0_dram"]
```

```python
from contextlib import ExitStack

import concourse.bass as bass
from concourse import mybir

F32 = mybir.dt.float32
F16 = mybir.dt.float16
I32 = mybir.dt.int32
U32 = mybir.dt.uint32
ALU = mybir.AluOpType
ACT = mybir.ActivationFunctionType
AX_X = mybir.AxisListType.X

P = 128
EPS = 1e-5
W_SCALE = 64.0
W_INV = 1.0 / W_SCALE


class Step:

    def __init__(self, s, batches, it=None, base=None):
        self.s, self.batches, self.it = s, batches, it
        self.base = base or self

    def ahead(self):
        return Step(self.s + 1, self.batches, self.it, self)

    def behind(self):
        return Step(self.s - 1, self.batches, self.it, self)

    def has(self, lag):
        return self.it is not None or 0 <= self.s - lag < self.batches

    def first(self, lag):
        return self.it is None and self.s == lag

    def par(self, lag):
        return (self.s - lag) % 2

    def batch(self, lag):
        b = self.s - lag
        return b if self.it is None else b + self.it * 2

    def n(self, lag, per=1, k=None, ring=1):
        v = per * ((self.s - lag) // ring) + (per if k is None else k)
        return v if self.it is None else v + self.it * (2 // ring * per)


def xattn_moe_kernel(nc, x, ctx_in, gamma_x, beta_x, gamma_l, beta_l, wq, wkv, wo, cent, ln_g, ln_b,
                     w1, b1, w2, b2, rope_cos, rope_sin, ident_c, tri_c, cols_c, tabs_c, basee_c, ids_c, empty_c, out):
    B, T, D = x.shape
    INNER = wq.shape[1]
    DH = 64
    H = INNER // DH
    E, _, FF = w1.shape
    KD = D // P
    NB = INNER // P
    FB = FF // P
    TOK = B * T
    TILES = TOK // P + E - 1
    NT = TILES + 1
    REGION = TOK
    TABLE = (E * REGION // P + NT) * P
    REC = 2 * D + 4
    ALPHA, INV2 = 2 * D, 2 * D + 1
    OOB = 2 * TOK
    assert T == P and KD == 2 and NB == 4 and H == 8 and FB == 8 and B == 2 * E

    L, PJ, AT, WR, RT, SC = -1, 0, 1, 2, 3, 4
    LOOP_FROM, LOOP_TO = 5, 13
    T_FROM, T_TO = 6, TILES - 1
    assert (T_TO - T_FROM) % 4 == 0

    xf = x.rearrange("b t d -> (b t) d")
    cf = ctx_in.rearrange("b t d -> (b t) d")
    outf = out.rearrange("b t d -> (b t) d")
    x_b = xf.rearrange("(b p) d -> b p d", p=P)
    c_b = cf.rearrange("(b p) d -> b p d", p=P)
    w1_g = w1.rearrange("e (k p) f -> (e k) p f", p=P)
    w2_g = w2.rearrange("e (h f p) d -> (e h) p f d", h=2, p=P)

    with ExitStack() as es:
        def sb(name, shape, dt):
            return es.enter_context(nc.sbuf_tensor(name, shape, dt))

        def pb(name):
            return es.enter_context(nc.psum_tensor(name, [P, 512], F32))

        def sem(name):
            return es.enter_context(nc.semaphore(name))

        rec_dram = nc.dram_tensor("rec_dram", [TOK, REC], F32).ap()
        ids_dram = nc.dram_tensor("ids_dram", [TABLE, 1], I32).ap()
        rec_b = rec_dram.rearrange("(b p) r -> b p r", p=P)

        w1h = sb("w1h", [P, E, KD * FF], F16)
        w1l = sb("w1l", [P, E, KD * FF], F16)
        w2h = sb("w2h", [P, E, FB * D], F16)
        w2l = sb("w2l", [P, E, FB * D], F16)
        KV = 2 * INNER
        AW = KD * INNER + KD * KV + NB * D + 2 * INNER
        aw = [sb("awh", [P, AW], F16), sb("awl", [P, AW], F16)]
        o_q, o_kv, o_wo, o_raw = 0, KD * INNER, KD * (INNER + KV), KD * (INNER + KV) + NB * D
        wq_s = [a[:, o_q:o_kv].rearrange("p (k n) -> p k n", k=KD) for a in aw]
        wkv_s = [a[:, o_kv:o_wo].rearrange("p (k n) -> p k n", k=KD) for a in aw]
        wo_s = [a[:, o_wo:o_raw].rearrange("p (k n) -> p k n", k=NB) for a in aw]
        k_raw, k_swap = (a[:, o_raw:AW].bitcast(F32).rearrange("p (b t) -> p b t", b=NB) for a in aw)
        stage = [sb(f"stage{i}", [P, FF], F32) for i in range(2)]
        aw_stage = [stage[0][:, :], stage[1][:, :]] + [w[:, E - 1, :].bitcast(F32) for w in (w1h, w2h)]
        xc = [sb(f"xc{i}", [P, 2, D], F32) for i in range(2)]
        lnT = [sb(f"lnT{h}", [P, KD, 2 * P], F16) for h in "hl"]
        qT = [sb(f"qT{h}", [P, NB, P], F16) for h in "hl"]
        kT_all = sb("kT", [P, 4, NB * 2 * P], F16)
        kT = [[kT_all[:, 2 * h + i, :].rearrange("p (n s t) -> p n s t", n=NB, s=2) for i in range(2)]
              for h in range(2)]
        v = [[sb(f"v{h}{i}", [P, 2, INNER], F16) for i in range(2)] for h in "hl"]
        k_cos = sb("k_cos", [P, NB, P], F32)
        lnT32 = sb("lnT32", [P, 2 * KD * P], F32)
        cos_t = sb("cos_t", [P, P], F32)
        sin_t = sb("sin_t", [P, P], F32)
        probs = [sb(f"probs{i}", [P, 2, 2 * P], F32) for i in range(2)]
        pT = [[sb(f"pT{h}{i}", [P, 4 * P], F16) for i in range(2)] for h in "hl"]
        attn = sb("attn", [P, INNER], F32)
        aT = [sb(f"aT{h}", [P, NB, P], F16) for h in "hl"]
        rec = [sb(f"rec{i}", [P, REC], F32) for i in range(2)]
        x1 = [r[:, D:2 * D] for r in rec]
        fT = sb("fT", [P, D], F32)
        ident = sb("ident", [P, P], F32)
        tri = sb("tri", [P, 2, P], F16)
        cols = sb("cols", [P, 16], F32)
        tabs = stage[1][:, 0:16 + E * E + 1]
        b1_r = stage[0][0:E, 0:FF]
        lngb_r = stage[1][0:E, 128:128 + 2 * D]
        b2_r = stage[1][:, 128 + 2 * D:128 + 3 * D]
        basee = sb("basee", [P, 2, E], F32)
        rowt = attn[0:8 + E * KD, 0:P]
        colt = sb("colt", [P, 8 + E * KD], F32)
        small = sb("small", [P, 120], F32)
        at = [0]

        def few(n):
            a = small[:, at[0]:at[0] + n]
            at[0] += n
            return a

        nmax = [few(2) for _ in range(2)]
        rsum = [few(H) for _ in range(2)]
        rinv = few(H)
        lst = few(12).rearrange("p (a b) -> p a b", a=2)
        mv = few(6).rearrange("p (a b) -> p a b", a=3)
        norms = few(24)
        fst, top8, eidf = few(6), few(8), few(1)
        place, placef, ealpha = few(2 * E).rearrange("p (a e) -> p a e", a=2), few(1), few(2)
        nmean, r1, r2, s2 = norms[:, 0:3], norms[:, 3:6], norms[:, 6:9], norms[:, 9:12]
        nv, nu, ninv2 = norms[:, 12:15], norms[:, 15:18], norms[:, 18:19]
        idx8 = sb("idx8", [P, 8], U32)
        oneh = sb("oneh", [P, E], F16)
        ohcum = [sb(f"ohcum{i}", [P, E], F16) for i in range(2)]
        placei = sb("placei", [P, 1], I32)
        tokid = sb("tokid", [P, 1], I32)
        oob = attn[:, P:P + TABLE // P].bitcast(I32)
        tile_e = sb("tile_e", [1, P], I32)
        tile_r = sb("tile_r", [P, 1], I32)
        idt = sb("idt", [P, NT], I32)

        def over(t, lo, n):
            return t[:, lo:lo + n].bitcast(F32)
        W1 = KD * FF
        w1c = [[kT_all[:, 0:2, :].rearrange("p a n -> p (a n)"), kT_all[:, 2:4, :].rearrange("p a n -> p (a n)")],
               [aw[0][:, 0:W1], aw[1][:, 0:W1]]]
        g_rec = [over(aw[i // 2], W1 + (i % 2) * 2 * REC, 2 * REC) for i in range(4)]
        yout = [over(aw[i], W1 + 4 * REC, 2 * D) for i in range(2)]
        xg = attn[:, 0:D]
        ybase = rec
        hid32 = [k_cos[:, :, :], lnT32[:, :].rearrange("p (f t) -> p f t", t=P)]
        xgT = [lnT[i][:, 0, :].rearrange("p (k t) -> p k t", k=KD) for i in range(2)]
        hid = [[v[i][j][:, :, :].rearrange("p a (c t) -> p (a c) t", t=P) for j in range(2)] for i in range(2)]
        NCOL = 2 * KD + FB
        tile_c = probs[0][:, :, :].rearrange("p a b -> p (a b)")[:, 0:NCOL * NT].rearrange("p (c t) -> p c t", c=NCOL)
        LOW = 32
        oh_t = probs[1][:, 0, 0:2 * LOW]
        oh_e = probs[1][0:E, 0, 128:256]
        oh_eh = pT[0][0][0:LOW + E, 0:P]
        ef_t = probs[1][:, 0, 2 * LOW:2 * LOW + 1]
        ids_t = probs[1][0:NT, 1, 0:P].bitcast(I32)
        ids_f = probs[1][0:NT, 1, P:2 * P]
        b2_s = pT[1][0][0:LOW + E, 0:D]
        b2_high_too = pT[1][1][LOW:LOW + E, 0:D]
        rt = attn[:, :]

        ps_s = es.enter_context(nc.psum_tensor("ps_s", [P, 2, 512], F32))
        ps_t = [pb(f"ps_t{i}") for i in range(2)]
        ps_u = [pb(f"ps_u{i}") for i in range(3)]
        ps_o = pb("ps_o")
        ps_h = [[ps_s[:, i, :] for i in range(2)], [t[:, :] for t in ps_t]]

        consts_in = sem("consts_in")
        first_in = sem("first_in")
        xc_in = [sem(f"xc_in{i}") for i in range(2)]
        x1_in = [sem(f"x1_in{i}") for i in range(2)]
        stage_in = [sem(f"stage_in{i}") for i in range(2)]
        rowt_in = sem("rowt_in")
        table_init = sem("table_init")
        rec_stored = sem("rec_stored")
        ids_scattered = sem("ids_scattered")
        aw_in = [sem(f"aw_in{i}") for i in range(4)]
        aw_high = sem("aw_high")
        aw_split = sem("aw_split")
        w_high = sem("w_high")
        w_scaled = sem("w_scaled")
        w_split = sem("w_split")
        setup_dve = sem("setup_dve")
        colt_ps = sem("colt_ps")
        colt_ready = sem("colt_ready")
        in_bn = sem("in_bn")
        in_stats = sem("in_stats")
        norm_seq = sem("norm_seq")
        xn_ready = sem("xn_ready")
        lnT_ready = sem("lnT_ready")
        lnT_affine = sem("lnT_affine")
        lnT_high = sem("lnT_high")
        lnT_split = sem("lnT_split")
        kx_ready, kx_copied, kx_cos = sem("kx_ready"), sem("kx_copied"), sem("kx_cos")
        kx_swapped, kx_sin = sem("kx_swapped"), sem("kx_sin")
        kx_sum, kx_high, kx_split = sem("kx_sum"), sem("kx_high"), sem("kx_split")
        kl_ready, kl_high, kl_split = sem("kl_ready"), sem("kl_high"), sem("kl_split")
        vx_ready, vx_high, vx_split = sem("vx_ready"), sem("vx_high"), sem("vx_split")
        vl_ready, vl_high, vl_split = sem("vl_ready"), sem("vl_high"), sem("vl_split")
        q_ready, q_high, q_split = sem("q_ready"), sem("q_high"), sem("q_split")
        scores_ready = sem("scores_ready")
        nmax_ready = sem("nmax_ready")
        probs_ready = sem("probs_ready")
        pT_ready, pT_high, pT_split = sem("pT_ready"), sem("pT_high"), sem("pT_split")
        pv_done = sem("pv_done")
        rinv_ready = sem("rinv_ready")
        attn_ready = sem("attn_ready")
        aT_ready, aT_high, aT_split = sem("aT_ready"), sem("aT_high"), sem("aT_split")
        y_ready = sem("y_ready")
        x1_ready, x1_bn, x1_stats = sem("x1_ready"), sem("x1_bn"), sem("x1_stats")
        f2_ready = sem("f2_ready")
        fT_ready, fT_copied = sem("fT_ready"), sem("fT_copied")
        aff_ready = sem("aff_ready")
        route_seq = sem("route_seq")
        ninv2_ready = sem("ninv2_ready")
        ealpha_ready = sem("ealpha_ready")
        alpha_seq = sem("alpha_seq")
        pref_ready = sem("pref_ready")
        place_seq = sem("place_seq")
        counts_ps = sem("counts_ps")
        tabs_in = sem("tabs_in")
        tile_seq = sem("tile_seq")
        tile_clear = sem("tile_clear")
        tiles_ready = sem("tiles_ready")
        turned_ps = sem("turned_ps")
        turned = sem("turned")
        ids_in = sem("ids_in")
        idf_ready = sem("idf_ready")
        idt_ps = sem("idt_ps")
        idt_ready = sem("idt_ready")
        cols_ps = sem("cols_ps")
        cols_ready = sem("cols_ready")
        b2_high = sem("b2_high")
        b2_split = sem("b2_split")
        buffers_clear = sem("buffers_clear")
        w1c_in = [sem(f"w1c_in{i}") for i in range(2)]
        g_in = [sem(f"g_in{i}") for i in range(4)]
        xgT_ps, xg_ready, xgT_high, xgT_split = sem("xgT_ps"), sem("xg_ready"), sem("xgT_high"), sem("xgT_split")
        hid_ps, hid_biased, hid_high, hid_split = sem("hid_ps"), sem("hid_biased"), sem("hid_high"), sem("hid_split")
        y2_ps, y2_base, y2_out = sem("y2_ps"), sem("y2_base"), sem("y2_out")
        out_stored = [sem(f"out_stored{i}") for i in range(4)]

        NO_N, RO_N, PL_N, AL_N = 8, 6, 5, 2
        TILE_N = 12
        N_FIRST, N_CONST = 16 * 2, 16 * 6

        UNITS = [
            ("kx", 0, PJ, kx_copied, 1, 1),
            ("kl", 1, PJ, kl_split, 1, 1),
            ("pref", 0, RT + 1, place_seq, PL_N, 1),
            ("vx", 2, PJ, vx_split, 1, 1),
            ("vl", 1, PJ, vl_split, 1, 1),
            ("aT", 0, WR, aT_split, 1, 1),
            ("lnT", 2, L, lnT_affine, 1, 1),
            ("q", 1, PJ, q_split, 1, 1),
            ("fT", 2, RT, fT_copied, 1, 1),
            ("y", 0, WR, x1_ready, 1, 1),
            ("aff", 2, RT, route_seq, RO_N, 3),
        ]
        LAST_PROJECTION = q_ready
        ORDER = [u[0] for u in UNITS]

        def bank(name):
            return ps_u[UNITS[ORDER.index(name)][1]]

        def wait_alone(eng, s, n):
            eng.wait_ge(s, n)
            eng.nop(nofuse=True)

        def pipeline(eng, step):
            for s in range(-2, LOOP_FROM):
                step(Step(s, B))
            with eng.Fori(0, (LOOP_TO - LOOP_FROM) // 2) as it:
                for u in range(2):
                    step(Step(LOOP_FROM + u, B, it))
            for s in range(LOOP_TO, B + SC + 1):
                step(Step(s, B))

        def wait_pair(eng, s, st, j):
            if j >= 2:
                eng.wait_ge(s, st.n(AT, 4, j - 1))
            elif st.has(AT + 1):
                eng.wait_ge(s, st.n(AT + 1, 4, j + 3))

        block = es.enter_context(nc.Block())

        @block.sync
        def _(sp):
            def load_xc(b, par):
                sp.dma_start(xc[par][:, 0, :], c_b[b]).then_inc(xc_in[par], 16)
                sp.dma_start(xc[par][:, 1, :], x_b[b]).then_inc(xc_in[par], 16)

            load_xc(0, 0)
            sp.dma_start(cols[:, :], cols_c).then_inc(first_in, 16)
            for k in range(KD):
                sp.dma_start(aw_stage[k], wkv[k * P:(k + 1) * P, :]).then_inc(aw_in[k], 16)
            load_xc(1, 1)
            for i, src in enumerate((wq, wo)):
                src = src.rearrange("(k p) n -> p k n", p=P)
                sp.dma_start(aw_stage[2 + i].rearrange("p (k n) -> p k n", k=src.shape[1]), src)\
                    .then_inc(aw_in[2 + i], 16)
            sp.dma_start(cos_t[:, :], rope_cos).then_inc(consts_in, 16)
            sp.dma_start(sin_t[:, :], rope_sin).then_inc(consts_in, 16)
            sp.dma_start(tri[:, :, :], tri_c).then_inc(consts_in, 16)
            sp.dma_start(basee[:, :, :], basee_c.partition_broadcast(P)).then_inc(consts_in, 16)
            sp.dma_start(tokid[:, :], ids_c).then_inc(consts_in, 16)
            sp.dma_start(oob[:, :], empty_c).then_inc(consts_in, 16)
            sp.wait_ge(consts_in, N_CONST)
            sp.dma_start(ids_dram.rearrange("(p c) o -> p (c o)", p=P), oob[:, :]).then_inc(table_init, 16)

            def swap_keys(st):
                if st.has(PJ):
                    if st.has(PJ + 1):
                        wait_alone(sp, kx_sum, st.n(PJ + 1))
                    wait_alone(sp, kx_copied, st.n(PJ))
                    for lo in range(0, P, DH):
                        for a, b in ((lo, lo + DH // 2), (lo + DH // 2, lo)):
                            sp.dma_start(k_swap[a:a + DH // 2], k_raw[b:b + DH // 2]).then_inc(kx_swapped, 16)

            def store_record(st):
                if st.has(RT):
                    wait_alone(sp, f2_ready, st.n(RT))
                    wait_alone(sp, alpha_seq, st.n(RT, AL_N))
                    sp.dma_start(rec_b[st.batch(RT)], rec[st.par(RT)][:, :]).then_inc(rec_stored, 16)

            def load_weights(st, i):
                if st.has(PJ):
                    g = st.batch(PJ)
                    if st.has(PJ + 1):
                        wait_alone(sp, w_split, st.n(PJ + 1, 2, i + 1))
                    else:
                        wait_alone(sp, aw_split, 1 + i)
                    if i == 0:
                        sp.dma_start(stage[0][:, :], w1_g[g]).then_inc(stage_in[0], 16)
                    else:
                        sp.dma_start(stage[1][:, :].rearrange("p (f d) -> p f d", d=D), w2_g[g])\
                            .then_inc(stage_in[1], 16)

            def load_inputs(st):
                if st.has(L - 1) and not (st.it is None and st.s < 0):
                    wait_alone(sp, lnT_ready, st.n(PJ))
                    load_xc(st.batch(L - 1), st.par(L - 1))

            def load_x1(st):
                if st.has(WR):
                    if st.has(WR + 2):
                        wait_alone(sp, rec_stored, st.n(WR + 2, 16))
                    sp.dma_start(x1[st.par(WR)], x_b[st.batch(WR)]).then_inc(x1_in[st.par(WR)], 16)

            def load_tile_constants():
                sp.wait_ge(w_split, 2 * B)
                sp.dma_start(tabs, tabs_c.partition_broadcast(P)).then_inc(tabs_in, 16)
                sp.dma_start(b1_r, b1).then_inc(tabs_in, 16)
                sp.dma_start(lngb_r[:, 0:D], ln_g).then_inc(tabs_in, 16)
                sp.dma_start(lngb_r[:, D:2 * D], ln_b).then_inc(tabs_in, 16)
                for lo in (0, LOW):
                    sp.dma_start(b2_r[lo:lo + E, :], b2).then_inc(tabs_in, 16)

            def step(st):
                if st.s == B + 1:
                    load_tile_constants()
                before = st.behind()
                store_record(before)
                swap_keys(st)
                load_inputs(st)
                load_x1(st)
                load_weights(st, 0)
                load_weights(st, 1)

            pipeline(sp, step)

            sp.wait_ge(tiles_ready, 1)

            def copy_w1(t, par, free):
                e = sp.value_load(tile_e[0:1, bass.ds(t, 1)], min_val=0, max_val=E - 1)
                if free is not None:
                    wait_alone(sp, hid_ps, free)
                for i, w in enumerate((w1h, w1l)):
                    sp.dma_start(w1c[par][i], w[:, bass.ds(e, 1), :].rearrange("p a n -> p (a n)"))\
                        .then_inc(w1c_in[par], 16)

            for t in range(3):
                if t == 1:
                    sp.wait_ge(g_in[0], 16)
                copy_w1(t, t % 2, 2 * (t - 1) if t >= 2 else None)
            with sp.Fori(0, (TILES - 3) // 2) as it:
                for t in (3, 4):
                    copy_w1(it * 2 + t, t % 2, it * 4 + 2 * (t - 1))
            for ring in range(4):
                sp.wait_ge(out_stored[ring], 16 * len(range(ring, TILES, 4)))

        @block.scalar
        def _(act):
            act.dma_start(ident[:, :], ident_c).then_inc(first_in, 16)
            for i, g in enumerate((gamma_x, gamma_l, beta_x, beta_l)):
                act.dma_start(rowt[2 * i:2 * i + 2, :], g.rearrange("(k p) -> k p", p=P)).then_inc(rowt_in, 16)
            act.dma_start(rowt[8:8 + E * KD, :], cent.rearrange("e (k p) -> (e k) p", p=P)).then_inc(rowt_in, 16)

            dsts = [wkv_s[0][:, 0, :], wkv_s[0][:, 1, :], wq_s[0], wo_s[0]]

            def aw_high_half(i):
                dst, src = dsts[i], aw_stage[i]
                act.wait_ge(aw_in[i], 16)
                if i >= 2:
                    src = src.rearrange("p (k n) -> p k n", k=dst.shape[1])
                act.activation(dst, src, ACT.Copy, scale=W_SCALE).then_inc(aw_high, 1)

            aw_high_half(0)
            aw_high_half(1)

            def high(ready, n, dst, src, scale, done):
                act.wait_ge(ready, n)
                act.activation(dst, src, ACT.Copy, scale=scale).then_inc(done, 1)

            def exp_pair(st, j):
                if st.has(AT):
                    wait_pair(act, pT_ready, st, j)
                    act.wait_ge(nmax_ready, st.n(AT, 4, j + 1))
                    for i in range(2):
                        h = 2 * j + i
                        ins = act.activation(probs[j % 2][:, i, :], ps_s[:, i, 0:2 * P], ACT.Exp,
                                             bias=nmax[j % 2][:, i:i + 1],
                                             accum_out=rsum[st.par(AT)][:, h:h + 1])
                    ins.then_inc(probs_ready, 1)

            def probs_high(st, j):
                if st.has(AT):
                    wait_pair(act, pv_done, st, j)
                    high(pT_ready, st.n(AT, 4, j + 1), pT[0][j % 2][:, :], ps_t[j % 2][:, :], 1.0, pT_high)

            def k_copy(st):
                if st.has(PJ):
                    if st.has(PJ + 1):
                        act.wait_ge(kx_cos, st.n(PJ + 1))
                        act.wait_ge(kx_swapped, st.n(PJ + 1, 64))
                    high(kx_ready, st.n(PJ), k_raw, bank("kx")[:, :].rearrange("p (b t) -> p b t", b=NB), 1.0, kx_copied)

            def k_latent_high(st):
                if st.has(PJ):
                    high(kl_ready, st.n(PJ), kT[0][st.par(PJ)][:, :, 1, :],
                         bank("kl")[:, :].rearrange("p (b t) -> p b t", b=NB), W_INV, kl_high)

            def q_high_half(st):
                if st.has(PJ):
                    high(q_ready, st.n(PJ), qT[0][:, :, :], bank("q")[:, :].rearrange("p (b t) -> p b t", b=NB),
                         W_INV * DH ** -0.5, q_high)

            def v_high(st, i):
                if st.has(PJ):
                    if st.has(PJ + 2):
                        act.wait_ge(pv_done, st.n(PJ + 2, 4))
                    high((vx_ready, vl_ready)[i], st.n(PJ), v[0][st.par(PJ)][:, i, :],
                         bank(("vx", "vl")[i])[:, :], W_INV, (vx_high, vl_high)[i])

            def f_copy(st):
                if st.has(RT):
                    high(fT_ready, st.n(RT), fT[:, :], bank("fT")[:, 0:D], 1.0, fT_copied)

            def attn_high(st):
                if st.has(WR):
                    high(aT_ready, st.n(WR), aT[0][:, :, :],
                         bank("aT")[:, :].rearrange("p (b t) -> p b t", b=NB), 1.0, aT_high)

            def norm_affine(st):
                if st.has(L):
                    if st.has(L + 1):
                        act.wait_ge(lnT_split, st.n(L + 1))
                    else:
                        act.wait_ge(colt_ready, 1)
                    act.wait_ge(lnT_ready, st.n(L))
                    for c in range(2 * KD):
                        k, src = c // 2, c % 2
                        g, b = colt[:, 2 * src + k:2 * src + k + 1], colt[:, 4 + 2 * src + k:4 + 2 * src + k + 1]
                        ins = act.activation(lnT32[:, c * P:(c + 1) * P], bank("lnT")[:, c * P:(c + 1) * P],
                                             ACT.Identity, bias=b, scale=g)
                    ins.then_inc(lnT_affine, 1)

            def norm_high(st):
                if st.has(L):
                    if st.has(L + 1):
                        act.wait_ge(LAST_PROJECTION, st.n(L + 1))
                    high(lnT_affine, st.n(L), lnT[0][:, :, :], lnT32[:, :].rearrange("p (k t) -> p k t", k=KD), 1.0, lnT_high)

            def alpha_exp(st):
                if st.has(RT):
                    act.wait_ge(route_seq, st.n(RT, RO_N, 2))
                    act.wait_ge(ninv2_ready, st.n(RT))
                    act.activation(ealpha[:, 0:1], top8[:, 0:1], ACT.Exp, scale=ninv2).then_inc(ealpha_ready, 1)

            def w_group(st, i):
                if st.has(PJ):
                    g = st.batch(PJ)
                    wait_alone(act, stage_in[i], st.n(PJ, 16))
                    w = (w1h, w2h)[i][:, :, :].rearrange("p e (h n) -> p (e h) n", h=2)
                    act.activation(w[:, g, :], stage[i][:, :], ACT.Copy, scale=W_SCALE).then_inc(w_high, 1)

            def step(st):
                if st.s == 0:
                    aw_high_half(2)
                    aw_high_half(3)
                before = st.behind()
                exp_pair(st, 0)
                k_copy(st)
                k_latent_high(st)
                probs_high(before, 3)
                exp_pair(st, 1)
                v_high(st, 0)
                w_group(before, 1)
                exp_pair(st, 2)
                v_high(st, 1)
                attn_high(st)
                probs_high(st, 0)
                norm_affine(st)
                probs_high(st, 1)
                q_high_half(st)
                f_copy(st)
                exp_pair(st, 3)
                norm_high(st)
                w_group(st, 0)
                alpha_exp(st)
                probs_high(st, 2)

            pipeline(act, step)

            act.wait_ge(tabs_in, 96)
            act.wait_ge(tile_clear, 1)
            act.activation(b2_s[0:E, :], b2_r[0:E, :], ACT.Copy, scale=W_SCALE).then_inc(b2_high, 1)
            act.activation(b2_high_too, b2_r[LOW:LOW + E, :], ACT.Copy, scale=W_SCALE).then_inc(b2_high, 1)

            def x_high(n):
                if not (isinstance(n, int) and n == 1):
                    act.wait_ge(hid_ps, n * 2 - 2)
                act.wait_ge(xg_ready, n)
                act.activation(xgT[0], xg.rearrange("p (k t) -> p k t", k=KD), ACT.Copy).then_inc(xgT_high, 1)

            def h_high(n, par, hf):
                act.wait_ge(hid_biased, n + hf)
                act.activation(hid[0][par][:, 4 * hf:4 * hf + 4, :], hid32[hf], ACT.Relu).then_inc(hid_high, 1)

            def tile_step(t, it=None):
                r = 0 if it is None else it
                h_high(r * 8 + (2 * t + 1), t % 2, 0)
                if t + 1 < TILES:
                    x_high(r * 4 + (t + 2))
                h_high(r * 8 + (2 * t + 1), t % 2, 1)

            x_high(1)
            for t in range(T_FROM):
                tile_step(t)
            with act.Fori(0, (T_TO - T_FROM) // 4) as it:
                for t in range(T_FROM, T_FROM + 4):
                    tile_step(t, it)
            for t in range(T_TO, TILES):
                tile_step(t)

        @block.gpsimd
        def _(pool):
            pool.wait_ge(first_in, N_FIRST)
            eps, mhalf, half, mone = (cols[:, i:i + 3] for i in (0, 3, 6, 9))

            def norm_scales(st):
                if not (st.has(L) or st.has(RT)):
                    return
                k = [0]

                def done(ins):
                    k[0] += 1
                    ins.then_inc(norm_seq, 1)

                def former():
                    pool.wait_ge(norm_seq, st.n(L, NO_N, k[0]))

                if st.has(L):
                    pool.wait_ge(in_stats, st.n(L, 2))
                if st.has(RT):
                    pool.wait_ge(x1_stats, st.n(RT))
                done(pool.tensor_tensor(nv, mv[:, :, 1], eps, ALU.add))
                done(pool.tensor_tensor(nmean, mv[:, :, 0], mone, ALU.mult))
                former()
                done(pool.tensor_tensor(r1, nv, mhalf, ALU.pow))
                former()
                done(pool.tensor_tensor(nu[:, 1:3], mv[:, 1:3, 1], r1[:, 1:3], ALU.mult))
                former()
                done(pool.tensor_tensor(nv[:, 1:3], nu[:, 1:3], r1[:, 1:3], ALU.mult))
                former()
                done(pool.tensor_tensor(nu[:, 1:3], nv[:, 1:3], eps[:, 1:3], ALU.add))
                former()
                done(pool.tensor_tensor(r2[:, 1:3], nu[:, 1:3], mhalf[:, 1:3], ALU.pow))
                former()
                done(pool.tensor_tensor(s2[:, 1:3], r1[:, 1:3], r2[:, 1:3], ALU.mult))
                assert k[0] == NO_N

            def f2(st):
                if st.has(RT):
                    r = rec[st.par(RT)]
                    pool.tensor_tensor(r[:, INV2:INV2 + 1], nu[:, 2:3], half[:, 2:3], ALU.pow)
                    wait_alone(pool, norm_seq, st.n(L, NO_N))
                    pool.tensor_scalar(r[:, 0:D], x1[st.par(RT)], nmean[:, 2:3], s2[:, 2:3], ALU.add, ALU.mult)\
                        .then_inc(f2_ready, 1)
                    if st.has(RT + 1):
                        pool.wait_ge(ealpha_ready, st.n(RT + 1))
                    pool.wait_ge(f2_ready, st.n(RT))
                    pool.tensor_tensor(ninv2, r[:, INV2:INV2 + 1], mone[:, 0:1], ALU.mult).then_inc(ninv2_ready, 1)

            def rope(st):
                if st.has(PJ):
                    pool.wait_ge(kx_cos, st.n(PJ))
                    pool.wait_ge(kx_sin, st.n(PJ))
                    pool.tensor_tensor(k_cos[:, :, :], k_cos[:, :, :], k_swap, ALU.add).then_inc(kx_sum, 1)

            def k_context_high(st):
                if st.has(PJ):
                    wait_alone(pool, kx_sum, st.n(PJ))
                    pool.tensor_scalar(kT[0][st.par(PJ)][:, :, 0, :], k_cos[:, :, :], 1.0, 0.0, ALU.mult, ALU.add)\
                        .then_inc(kx_high, 1)

            def norm_inputs(st):
                if st.has(L):
                    c = xc[st.par(L)]
                    wait_alone(pool, norm_seq, st.n(L, NO_N))
                    pool.tensor_scalar(c[:, 0, :], c[:, 0, :], nmean[:, 0:1], r1[:, 0:1], ALU.add, ALU.mult)
                    pool.tensor_scalar(c[:, 1, :], c[:, 1, :], nmean[:, 1:2], s2[:, 1:2], ALU.add, ALU.mult)\
                        .then_inc(xn_ready, 1)

            def w_scale(st, i):
                if st.has(PJ):
                    wait_alone(pool, w_high, st.n(PJ, 2, i + 1))
                    pool.tensor_scalar(stage[i][:, :], stage[i][:, :], W_SCALE, 0.0, ALU.mult, ALU.add)\
                        .then_inc(w_scaled, 1)

            def w_low(st, i):
                if st.has(PJ):
                    g = st.batch(PJ)
                    wh = (w1h, w2h)[i][:, :, :].rearrange("p e (h n) -> p (e h) n", h=2)
                    wl = (w1l, w2l)[i][:, :, :].rearrange("p e (h n) -> p (e h) n", h=2)
                    wait_alone(pool, w_scaled, st.n(PJ, 2, i + 1))
                    pool.tensor_tensor(wl[:, g, :], stage[i][:, :], wh[:, g, :], ALU.subtract).then_inc(w_split, 1)

            def scatter_ids(st):
                if not st.has(SC):
                    return
                if st.it is None and st.s - SC == 0:
                    pool.wait_ge(table_init, 16)
                wait_alone(pool, place_seq, st.n(SC, PL_N))
                pool.indirect_dma_start(ids_dram, bass.IndirectOffsetOnAxis(ap=placei[:, 0:1], axis=0),
                                        tokid[:, :], None).then_inc(ids_scattered, 16)

            def clear_records():
                pool.wait_ge(y_ready, B)
                pool.wait_ge(kx_split, B)
                for g in g_rec:
                    ins = pool.memset(g, 0.0)
                ins.then_inc(buffers_clear, 1)

            def step(st):
                if st.s == B + SC:
                    clear_records()
                before, after = st.behind(), st.ahead()
                norm_inputs(st)
                f2(st)
                rope(st)
                k_context_high(st)
                w_scale(before, 1)
                scatter_ids(st)
                w_low(before, 1)
                w_scale(st, 0)
                norm_scales(after)
                w_low(st, 0)

            pipeline(pool, step)

            pool.wait_ge(tile_seq, TILE_N)
            pool.wait_ge(ids_scattered, 16 * B)
            pool.indirect_dma_start(ids_t, None, ids_dram.rearrange("(r c) o -> r (c o)", c=P),
                                    bass.IndirectOffsetOnAxis(ap=tile_r[0:NT, 0:1], axis=0)).then_inc(ids_in, 16)

            pool.wait_ge(idt_ready, 1)
            pool.wait_ge(buffers_clear, 1)
            pool.wait_ge(rec_stored, 16 * B)

            def gather(t):
                pool.indirect_dma_start(g_rec[t % 4], None, rec_dram,
                                        bass.IndirectOffsetOnAxis(ap=idt[:, t:t + 1], axis=0),
                                        bounds_check=TOK - 1, oob_is_err=False).then_inc(g_in[t % 4], 16)

            def scatter(t):
                pool.wait_ge(y2_out, t + 1)
                pool.indirect_dma_start(outf, bass.IndirectOffsetOnAxis(ap=idt[:, t:t + 1], axis=0),
                                        yout[t % 2], None,
                                        bounds_check=TOK - 1, oob_is_err=False).then_inc(out_stored[t % 4], 16)

            for t in range(4):
                gather(t)
            for t in range(TILES + 1):
                if t + 4 < TILES:
                    pool.wait_ge(y2_base, t + 1)
                    gather(t + 4)
                if t >= 1:
                    scatter(t - 1)

        @block.vector
        def _(dve):
            dve.memset(mv, 1.0).then_inc(setup_dve, 1)
            dve.memset(pT[0][0][:, :], 0.0).then_inc(setup_dve, 1)
            dve.memset(ohcum[0][:, :], 0.0).then_inc(setup_dve, 1)
            for r in rec:
                ins = dve.memset(r[:, 2 * D:REC], 0.0)
            ins.then_inc(setup_dve, 1)

            def low(ready, n, dst, src, scale, high, done):
                dve.wait_ge(ready, n)
                dve.scalar_tensor_tensor(dst, src, scale, high, ALU.mult, ALU.subtract).then_inc(done, 1)

            srcs = [wkv_s, wkv_s, wq_s, wo_s]

            def aw_low(i):
                d = srcs[i]
                hi, lo = (d[0][:, i, :], d[1][:, i, :]) if i < 2 else (d[0], d[1])
                src = aw_stage[i]
                if i >= 2:
                    src = src.rearrange("p (k n) -> p k n", k=hi.shape[1])
                low(aw_high, i + 1, lo, src, W_SCALE, hi, aw_split)

            def input_stats(st):
                if st.has(L - 1):
                    par = st.par(L - 1)
                    if st.has(L):
                        dve.wait_ge(in_stats, st.n(L, 2))
                    dve.wait_ge(xc_in[par], st.n(L - 1, 32, ring=2))
                    for i in range(2):
                        ins = dve.bn_stats(lst[:, i, :], xc[par][:, i, :])
                    ins.then_inc(in_bn, 1)

            def input_moments(st):
                if st.has(L - 1):
                    if st.has(L):
                        dve.wait_ge(xn_ready, st.n(L))
                    wait_alone(dve, in_bn, st.n(L - 1))
                    for i in range(2):
                        dve.bn_aggr(mv[:, i, :], lst[:, i, :]).then_inc(in_stats, 1)

            def row_max(st, j):
                if st.has(AT):
                    dve.wait_ge(scores_ready, st.n(AT, 4, j + 1))
                    dve.tensor_reduce(nmax[j % 2][:, :], ps_s[:, :, 0:2 * P],
                                      AX_X, ALU.max, negate=True).then_inc(nmax_ready, 1)

            def probs_low(st, j):
                if st.has(AT):
                    low(pT_high, st.n(AT, 4, j + 1), pT[1][j % 2][:, :], ps_t[j % 2][:, :], 1.0,
                        pT[0][j % 2][:, :], pT_split)

            def blocks(t):
                return t[:, :].rearrange("p (b t) -> p b t", b=NB)

            def k_cosine(st):
                if st.has(PJ):
                    if st.has(PJ + 1):
                        dve.wait_ge(kx_split, st.n(PJ + 1))
                    else:
                        dve.wait_ge(consts_in, N_CONST)
                    dve.wait_ge(kx_copied, st.n(PJ))
                    dve.tensor_tensor(k_cos[:, :, :], k_raw, cos_t[:, :].unsqueeze(1).broadcast_to([P, NB, P]), ALU.mult)\
                        .then_inc(kx_cos, 1)

            def k_sine(st):
                if st.has(PJ):
                    dve.wait_ge(kx_swapped, st.n(PJ, 64))
                    dve.tensor_tensor(k_swap, k_swap, sin_t[:, :].unsqueeze(1).broadcast_to([P, NB, P]), ALU.mult)\
                        .then_inc(kx_sin, 1)

            def k_context_low(st):
                if st.has(PJ):
                    dve.wait_ge(kx_high, st.n(PJ))
                    dve.tensor_tensor(kT[1][st.par(PJ)][:, :, 0, :], k_cos[:, :, :], kT[0][st.par(PJ)][:, :, 0, :],
                                      ALU.subtract).then_inc(kx_split, 1)

            def k_latent_low(st):
                if st.has(PJ):
                    low(kl_high, st.n(PJ), kT[1][st.par(PJ)][:, :, 1, :], blocks(bank("kl")), W_INV,
                        kT[0][st.par(PJ)][:, :, 1, :], kl_split)

            def v_low(st, i):
                if st.has(PJ):
                    low((vx_high, vl_high)[i], st.n(PJ), v[1][st.par(PJ)][:, i, :], bank(("vx", "vl")[i])[:, :], W_INV,
                        v[0][st.par(PJ)][:, i, :], (vx_split, vl_split)[i])

            def q_low(st):
                if st.has(PJ):
                    low(q_high, st.n(PJ), qT[1][:, :, :], blocks(bank("q")), W_INV * DH ** -0.5, qT[0][:, :, :], q_split)

            def norm_low(st):
                if st.has(L):
                    low(lnT_high, st.n(L), lnT[1][:, :, :], lnT32[:, :].rearrange("p (k t) -> p k t", k=KD), 1.0,
                        lnT[0][:, :, :], lnT_split)

            def row_sums(st):
                if st.has(WR):
                    dve.wait_ge(probs_ready, st.n(WR, 4))
                    dve.reciprocal(rinv[:, :], rsum[st.par(WR)][:, :]).then_inc(rinv_ready, 1)

            def attn_norm(st):
                if st.has(WR):
                    if st.first(WR):
                        dve.wait_ge(table_init, 16)
                    if st.has(WR + 1):
                        dve.wait_ge(aT_ready, st.n(WR + 1))
                    dve.wait_ge(pv_done, st.n(WR, 4))
                    dve.wait_ge(rinv_ready, st.n(WR))
                    dve.tensor_tensor(attn[:, :].rearrange("p (h d) -> p h d", h=H),
                                      ps_o[:, :].rearrange("p (h d) -> p h d", h=H),
                                      rinv[:, :].unsqueeze(2).broadcast_to([P, H, DH]), ALU.mult).then_inc(attn_ready, 1)

            def attn_low(st):
                if st.has(WR):
                    low(aT_high, st.n(WR), aT[1][:, :, :], blocks(bank("aT")), 1.0, aT[0][:, :, :], aT_split)

            def residual(st):
                if st.has(WR):
                    xt = x1[st.par(WR)]
                    dve.wait_ge(x1_in[st.par(WR)], st.n(WR, 16, ring=2))
                    dve.wait_ge(y_ready, st.n(WR))
                    dve.scalar_tensor_tensor(xt, bank("y")[:, 0:D], W_INV, xt, ALU.mult, ALU.add).then_inc(x1_ready, 1)

            def x1_stats_of(st):
                if st.has(WR):
                    dve.wait_ge(x1_ready, st.n(WR))
                    dve.bn_stats(fst[:, :], x1[st.par(WR)]).then_inc(x1_bn, 1)

            def x1_moments(st):
                if st.has(WR):
                    if st.has(WR + 1):
                        dve.wait_ge(f2_ready, st.n(WR + 1))
                    wait_alone(dve, x1_bn, st.n(WR))
                    dve.bn_aggr(mv[:, 2, :], fst[:, :]).then_inc(x1_stats, 1)

            def route_max(st):
                if st.has(RT):
                    dve.wait_ge(aff_ready, st.n(RT))
                    dve.max(top8[:, :], bank("aff")[:, 0:E]).then_inc(route_seq, 2)

            def route_index(st):
                if st.has(RT):
                    wait_alone(dve, route_seq, st.n(RT, RO_N, 2))
                    dve.max_index(idx8[:, :], top8[:, :], bank("aff")[:, 0:E]).then_inc(route_seq, 1)

            def route_float(st):
                if st.has(RT):
                    dve.wait_ge(route_seq, st.n(RT, RO_N, 3))
                    dve.tensor_copy(eidf[:, :], idx8[:, 0:1]).then_inc(route_seq, 1)

            def route_count(st):
                if st.has(RT):
                    par = st.par(RT)
                    dve.wait_ge(route_seq, st.n(RT, RO_N, 4))
                    dve.tensor_scalar(oneh[:, :], basee[:, 1, :], eidf[:, 0:1], None, ALU.is_equal).then_inc(route_seq, 1)
                    dve.wait_ge(route_seq, st.n(RT, RO_N, 5))
                    dve.tensor_tensor(ohcum[1 - par][:, :], ohcum[par][:, :], oneh[:, :], ALU.add).then_inc(route_seq, 1)

            def alpha(st):
                if st.has(RT):
                    dve.wait_ge(ealpha_ready, st.n(RT))
                    dve.tensor_scalar(ealpha[:, 1:2], ealpha[:, 0:1], 1.0, W_SCALE, ALU.add, ALU.mult)\
                        .then_inc(alpha_seq, 1)
                    dve.wait_ge(alpha_seq, st.n(RT, AL_N, 1))
                    dve.reciprocal(rec[st.par(RT)][:, ALPHA:ALPHA + 1], ealpha[:, 1:2]).then_inc(alpha_seq, 1)

            def place_ranks(st):
                if st.has(RT):
                    dve.wait_ge(pref_ready, st.n(RT))
                    dve.tensor_tensor(place[:, 0, :], bank("pref")[:, 0:E], basee[:, 0, :], ALU.add).then_inc(place_seq, 1)

            def place_mask(st):
                if st.has(RT):
                    dve.wait_ge(place_seq, st.n(RT, PL_N, 1))
                    dve.tensor_tensor(place[:, 1, :], place[:, 0, :], oneh[:, :], ALU.mult).then_inc(place_seq, 1)

            def place_sum(st):
                if st.has(RT):
                    dve.wait_ge(place_seq, st.n(RT, PL_N, 2))
                    dve.tensor_reduce(placef[:, :], place[:, 1, :], AX_X, ALU.add)\
                        .then_inc(place_seq, 1 if st.has(RT + 1) else 2)
                    if st.has(RT + 1):
                        dve.wait_ge(ids_scattered, st.n(RT + 1, 16))
                        dve.tensor_scalar(tokid[:, :], tokid[:, :], float(P), None, ALU.add).then_inc(place_seq, 1)

            def place_number(st):
                if st.has(RT):
                    dve.wait_ge(place_seq, st.n(RT, PL_N, 4))
                    dve.tensor_copy(placei[:, :], placef[:, :]).then_inc(place_seq, 1)

            def first_weights():
                dve.wait_ge(colt_ps, 1)
                dve.tensor_copy(colt[:, :], ps_o[:, 0:8 + E * KD]).then_inc(colt_ready, 1)
                for i in range(2):
                    aw_low(i)

            def step(st):
                if st.s == -1:
                    first_weights()
                if st.s == 0:
                    aw_low(2)
                    aw_low(3)
                before, after = st.behind(), st.ahead()
                k_cosine(st)
                row_max(st, 1)
                probs_low(before, 3)
                row_sums(st)
                place_ranks(before)
                k_latent_low(st)
                attn_norm(st)
                row_max(st, 2)
                v_low(st, 0)
                k_sine(st)
                place_mask(before)
                place_sum(before)
                v_low(st, 1)
                place_number(before)
                attn_low(st)
                input_stats(st)
                probs_low(st, 0)
                row_max(st, 3)
                k_context_low(st)
                q_low(st)
                probs_low(st, 1)
                residual(st)
                norm_low(st)
                route_max(st)
                route_index(st)
                x1_stats_of(st)
                input_moments(st)
                x1_moments(st)
                row_max(after, 0)
                route_float(st)
                alpha(st)
                probs_low(st, 2)
                route_count(st)

            pipeline(dve, step)

            pos = [0]

            def piece(n):
                a = rt[:, pos[0]:pos[0] + n]
                pos[0] += n
                return a

            seq = [0]

            def link(ins):
                seq[0] += 1
                ins.then_inc(tile_seq, 1)
                dve.wait_ge(tile_seq, seq[0])

            cnt, ntile, cum, past, gone = (piece(E) for _ in range(5))
            more = piece(16 * E).rearrange("p (e k) -> p e k", e=E)
            upto = piece(E * E).rearrange("p (a b) -> p a b", a=E)
            n_e, n_gone, rest, rowf = (piece(1) for _ in range(4))
            thr = tabs[:, 0:16].unsqueeze(1).broadcast_to([P, E, 16])
            mask = tabs[:, 16:16 + E * E].rearrange("p (a b) -> p a b", a=E)
            tcol = cols[:, 12:13]
            dve.memset(oh_t, 0.0)
            dve.memset(b2_s, 0.0).then_inc(tile_clear, 1)
            dve.wait_ge(tile_clear, 1)
            dve.wait_ge(tabs_in, 96)
            dve.wait_ge(counts_ps, 1)
            link(dve.tensor_copy(cnt, ps_o[:, 0:E]))
            link(dve.tensor_tensor(more, cnt.unsqueeze(2).broadcast_to([P, E, 16]), thr, ALU.is_gt))
            link(dve.tensor_reduce(ntile, more, AX_X, ALU.add))
            link(dve.tensor_tensor(upto, mask, ntile.unsqueeze(1).broadcast_to([P, E, E]), ALU.mult))
            link(dve.tensor_reduce(cum, upto, AX_X, ALU.add))
            link(dve.tensor_scalar(past, cum, tcol, None, ALU.is_le))
            link(dve.tensor_tensor(gone, past, ntile, ALU.mult))
            dve.tensor_reduce(n_e, past, AX_X, ALU.add)
            link(dve.tensor_reduce(n_gone, gone, AX_X, ALU.add))
            dve.tensor_scalar(ef_t, n_e, float(E - 1), None, ALU.min)
            link(dve.tensor_tensor(rest, tcol, n_gone, ALU.subtract))
            dve.tensor_scalar(oh_t.rearrange("p (a e) -> p a e", a=2)[:, :, 0:E],
                              basee[:, 1, :].unsqueeze(1).broadcast_to([P, 2, E]), ef_t, None, ALU.is_equal)\
                .then_inc(tile_seq, 1)
            dve.scalar_tensor_tensor(rowf, n_e, float(REGION // P), rest, ALU.mult, ALU.add).then_inc(tile_seq, 1)
            dve.wait_ge(tile_seq, seq[0] + 2)
            dve.tensor_copy(tile_r[:, :], rowf).then_inc(tile_seq, 1)
            dve.wait_ge(turned_ps, 1)
            dve.tensor_copy(tile_e[:, :], ps_o[0:1, 0:P])
            dve.tensor_copy(oh_e, ps_t[0][0:E, 0:P])
            dve.tensor_copy(oh_eh, ps_t[0][0:LOW + E, 0:P]).then_inc(tiles_ready, 1)
            low(b2_high, 2, b2_s[LOW:LOW + E, :], b2_r[LOW:LOW + E, :], W_SCALE, b2_high_too, b2_split)
            dve.wait_ge(ids_in, 16)
            dve.tensor_copy(ids_f, ids_t).then_inc(idf_ready, 1)
            dve.wait_ge(idt_ps, 1)
            dve.tensor_copy(idt[:, :], ps_t[1][:, 0:NT]).then_inc(idt_ready, 1)
            dve.wait_ge(cols_ps, 1)
            dve.tensor_copy(tile_c, ps_s[:, 0, 0:NCOL * NT].rearrange("p (c t) -> p c t", c=NCOL)).then_inc(cols_ready, 1)
            dve.wait_ge(cols_ready, 1)

            def column(c, t):
                return tile_c[:, c, bass.ds(t, 1)]

            def x_affine(t, n):
                if not (isinstance(n, int) and n == 1):
                    dve.wait_ge(xgT_split, n - 1)
                dve.wait_ge(xgT_ps, n)
                for k in range(KD):
                    ins = dve.tensor_scalar(xg[:, k * P:(k + 1) * P], ps_u[2][:, k * P:(k + 1) * P],
                                            column(k, t), column(KD + k, t), ALU.mult, ALU.add)
                ins.then_inc(xg_ready, 1)

            def x_low(n):
                dve.wait_ge(xgT_high, n)
                dve.tensor_tensor(xgT[1], xg.rearrange("p (k t) -> p k t", k=KD), xgT[0], ALU.subtract)\
                    .then_inc(xgT_split, 1)

            def h_bias(t, n, par, hf):
                if not (isinstance(n, int) and n == 1):
                    dve.wait_ge(hid_split, n + hf - 2)
                dve.wait_ge(hid_ps, n + hf)
                c = 2 * KD + 4 * hf
                bias = tile_c[:, c:c + 4, bass.ds(t, 1)]
                dve.scalar_tensor_tensor(hid32[hf], ps_h[par][hf].rearrange("p (f t) -> p f t", t=P), W_INV,
                                         bias.broadcast_to([P, 4, P]), ALU.mult, ALU.add).then_inc(hid_biased, 1)

            def h_low(n, par, hf):
                dve.wait_ge(hid_high, n + hf)
                dve.scalar_tensor_tensor(hid[1][par][:, 4 * hf:4 * hf + 4, :], hid32[hf], 0.0,
                                         hid[0][par][:, 4 * hf:4 * hf + 4, :], ALU.max, ALU.subtract)\
                    .then_inc(hid_split, 1)

            def y_base(n, par, ring):
                r = g_rec[ring]
                if not isinstance(n, int) or n > 2:
                    dve.wait_ge(y2_out, n - 2)
                dve.tensor_copy(ybase[par][:, ALPHA:ALPHA + 1], r[:, ALPHA:ALPHA + 1])
                dve.scalar_tensor_tensor(ybase[par][:, 0:D], r[:, 0:D], r[:, INV2:INV2 + 1], r[:, D:2 * D],
                                         ALU.mult, ALU.add).then_inc(y2_base, 1)

            def y_out(n, par, ring, free, first):
                if not first:
                    dve.wait_ge(out_stored[(ring + 2) % 4], free)
                dve.wait_ge(y2_base, n)
                dve.wait_ge(y2_ps, n)
                dve.scalar_tensor_tensor(yout[par], ps_u[par][:, 0:D], ybase[par][:, ALPHA:ALPHA + 1],
                                         ybase[par][:, 0:D], ALU.mult, ALU.add).then_inc(y2_out, 1)

            def tile_step(t, it=None):
                r = 0 if it is None else it
                if t + 1 < TILES:
                    x_affine(r * 4 + (t + 1), r * 4 + (t + 2))
                if t >= 2:
                    y_out(r * 4 + (t - 1), t % 2, (t - 2) % 4, r * 16 + 16 * ((t - 4) // 4 + 1), t < 4)
                n = r * 8 + (2 * t + 1)
                if t < TILES:
                    h_bias(r * 4 + t, n, t % 2, 0)
                    h_bias(r * 4 + t, n, t % 2, 1)
                    h_low(n, t % 2, 0)
                if t + 1 < TILES:
                    x_low(r * 4 + (t + 2))
                if t < TILES:
                    h_low(n, t % 2, 1)
                    y_base(r * 4 + (t + 1), t % 2, t % 4)

            x_affine(0, 1)
            x_low(1)
            for t in range(T_FROM):
                tile_step(t)
            with dve.Fori(0, (T_TO - T_FROM) // 4) as it:
                for t in range(T_FROM, T_FROM + 4):
                    tile_step(t, it)
            for t in range(T_TO, TILES + 2):
                tile_step(t)

        @block.tensor
        def _(pe):
            PAIRS = ((0, 0), (0, 1), (1, 0))

            def split_mm(out, lhs, rhs):
                n = len(lhs) * len(PAIRS)
                c = 0
                for k in range(len(lhs)):
                    for a, b in PAIRS:
                        ins = pe.matmul(out, lhs[k][a], rhs[k][b], start=(c == 0), stop=(c == n - 1))
                        c += 1
                return ins

            def keep_warm(n, src, bk):
                for _ in range(n):
                    pe.matmul(bk[:, :], src[:, 0:P], src[:, 0:4 * P], start=True, stop=True)

            def unit(st, name):
                k = ORDER.index(name)
                for m in range(k - 1, -3 * len(UNITS), -1):
                    i, off = m % len(UNITS), -(m // len(UNITS))
                    _, bk, lag, evac, per, last = UNITS[i]
                    if bk == UNITS[k][1] and st.base.has(lag + off):
                        pe.wait_ge(evac, st.base.n(lag + off, per, last))
                        break
                return bank(name)

            def scores(st, j):
                if not st.has(AT):
                    return
                if j == 0:
                    pe.wait_ge(q_split, st.n(AT))
                    pe.wait_ge(kx_split, st.n(AT))
                    pe.wait_ge(kl_split, st.n(AT))
                    if st.has(AT + 1):
                        pe.wait_ge(probs_ready, st.n(AT + 1, 4))
                else:
                    pe.wait_ge(probs_ready, st.n(AT, 4, j))
                par = st.par(AT)
                for c, (a, b) in enumerate(PAIRS):
                    for i in range(2):
                        r = slice(64 * i, 64 * i + 64)
                        ins = pe.matmul(ps_s[:, i, 0:2 * P], qT[a][r, j, :],
                                        kT[b][par][r, j, :, :].rearrange("p s t -> p (s t)"),
                                        start=(c == 0), stop=(c == 2))
                ins.then_inc(scores_ready, 1)

            def turn_probs(st, j):
                if st.has(AT):
                    wait_pair(pe, pT_split, st, j)
                    pe.wait_ge(probs_ready, st.n(AT, 4, j + 1))
                    for c in range(4):
                        ins = pe.transpose(ps_t[j % 2][:, c * P:(c + 1) * P],
                                           probs[j % 2][:, c // 2, (c % 2) * P:(c % 2 + 1) * P], ident[:, :])
                    ins.then_inc(pT_ready, 1)

            def values(st, j):
                if not st.has(AT):
                    return
                if j == 0:
                    pe.wait_ge(vx_split, st.n(AT))
                    pe.wait_ge(vl_split, st.n(AT))
                    if st.has(AT + 1):
                        pe.wait_ge(attn_ready, st.n(AT + 1))
                pe.wait_ge(pT_split, st.n(AT, 4, j + 1))
                par = st.par(AT)
                for i in range(2):
                    h = 2 * j + i
                    ins = split_mm(ps_o[:, h * DH:(h + 1) * DH],
                                   [[pT[a][j % 2][:, (2 * i + c) * P:(2 * i + c + 1) * P] for a in range(2)]
                                    for c in range(2)],
                                   [[v[a][par][:, c, h * DH:(h + 1) * DH] for a in range(2)] for c in range(2)])
                ins.then_inc(pv_done, 1)

            def inputs_ready(st, name):
                pe.wait_ge(lnT_split, st.n(PJ))
                if st.first(PJ):
                    pe.wait_ge(aw_split, 3 if name == "q" else 2)

            def project_T(st, name, w, col0, src, ready):
                if not st.has(PJ):
                    return
                inputs_ready(st, name)
                bk = unit(st, name)
                for n in range(NB):
                    ins = split_mm(bk[:, n * P:(n + 1) * P],
                                   [[w[a][:, k, col0 + n * P:col0 + (n + 1) * P] for a in range(2)] for k in range(KD)],
                                   [[lnT[a][:, k, src * P:(src + 1) * P] for a in range(2)] for k in range(KD)])
                ins.then_inc(ready, 1)

            def project_v(st, name, src, ready):
                if not st.has(PJ):
                    return
                inputs_ready(st, name)
                bk = unit(st, name)
                split_mm(bk[:, :],
                         [[lnT[a][:, k, src * P:(src + 1) * P] for a in range(2)] for k in range(KD)],
                         [[wkv_s[a][:, k, INNER:2 * INNER] for a in range(2)] for k in range(KD)]).then_inc(ready, 1)

            def turn_f2(st):
                if st.has(RT):
                    bk = unit(st, "fT")
                    pe.wait_ge(f2_ready, st.n(RT))
                    for k in range(KD):
                        ins = pe.transpose(bk[:, k * P:(k + 1) * P], rec[st.par(RT)][:, k * P:(k + 1) * P], ident[:, :])
                    ins.then_inc(fT_ready, 1)

            def affinities(st):
                if st.has(RT):
                    bk = unit(st, "aff")
                    pe.wait_ge(fT_copied, st.n(RT))
                    ck = colt[:, 8:8 + E * KD].rearrange("p (e k) -> p k e", k=KD)
                    for k in range(KD):
                        ins = pe.matmul(bk[:, 0:E], fT[:, k * P:(k + 1) * P], ck[:, k, :], start=(k == 0), stop=(k == KD - 1))
                    ins.then_inc(aff_ready, 1)

            def turn_attn(st):
                if st.has(WR):
                    bk = unit(st, "aT")
                    pe.wait_ge(attn_ready, st.n(WR))
                    for n in range(NB):
                        ins = pe.transpose(bk[:, n * P:(n + 1) * P], attn[:, n * P:(n + 1) * P], ident[:, :])
                    ins.then_inc(aT_ready, 1)

            def turn_inputs(st):
                if st.has(L):
                    bk = unit(st, "lnT")
                    pe.wait_ge(xn_ready, st.n(L))
                    for k in range(KD):
                        for s in range(2):
                            c = 2 * k + s
                            ins = pe.transpose(bk[:, c * P:(c + 1) * P], xc[st.par(L)][:, s, k * P:(k + 1) * P],
                                               ident[:, :])
                    ins.then_inc(lnT_ready, 1)

            def project_attn(st):
                if st.has(WR):
                    bk = unit(st, "y")
                    pe.wait_ge(aT_split, st.n(WR))
                    if st.first(WR):
                        pe.wait_ge(aw_split, 4)
                    split_mm(bk[:, 0:D], [[aT[a][:, n, :] for a in range(2)] for n in range(NB)],
                             [[wo_s[a][:, n, :] for a in range(2)] for n in range(NB)]).then_inc(y_ready, 1)

            def ranks(st):
                if st.has(RT):
                    bk = unit(st, "pref")
                    pe.wait_ge(route_seq, st.n(RT, RO_N))
                    pe.matmul(bk[:, 0:E], tri[:, 0, :], oneh[:, :], start=True, stop=False)
                    pe.matmul(bk[:, 0:E], tri[:, 1, :], ohcum[st.par(RT)][:, :], start=False, stop=True)\
                        .then_inc(pref_ready, 1)

            def step(st):
                before, after = st.behind(), st.ahead()
                turn_probs(before, 3)
                project_T(st, "kx", wkv_s, 0, 0, kx_ready)
                project_T(st, "kl", wkv_s, 0, 1, kl_ready)
                scores(st, 1)
                values(before, 2)
                ranks(before)
                project_v(st, "vx", 0, vx_ready)
                values(before, 3)
                scores(st, 2)
                turn_probs(st, 0)
                project_v(st, "vl", 1, vl_ready)
                turn_attn(st)
                turn_probs(st, 1)
                turn_inputs(st)
                scores(st, 3)
                project_T(st, "q", wq_s, 0, 1, q_ready)
                turn_f2(st)
                project_attn(st)
                affinities(st)
                turn_probs(st, 2)
                values(st, 0)
                scores(after, 0)
                values(st, 1)
                if st.s == -1:
                    keep_warm(8, pT[0][0], ps_t[0])

            pe.wait_ge(setup_dve, 4)
            keep_warm(12, pT[0][0], ps_t[0])
            pe.wait_ge(first_in, N_FIRST)
            pe.wait_ge(rowt_in, 80)
            n = 8 + E * KD
            pe.transpose(ps_o[:, 0:n], rowt, ident[0:n, 0:n]).then_inc(colt_ps, 1)
            pipeline(pe, step)

            pe.wait_ge(route_seq, RO_N * B)
            pe.matmul(ps_o[:, 0:E], tri[:, 1, :], ohcum[0][:, :], start=True, stop=True).then_inc(counts_ps, 1)
            pe.wait_ge(tile_seq, TILE_N)
            pe.matmul(ps_o[0:1, 0:P], ef_t, ident[:, :], start=True, stop=True)
            pe.transpose(ps_t[0][0:2 * LOW, 0:P], oh_t, ident[:, :]).then_inc(turned_ps, 1)
            pe.wait_ge(tiles_ready, 1)
            srcs = [lngb_r[:, k * P:(k + 1) * P] for k in range(2 * KD)] + [b1_r[:, f * P:(f + 1) * P] for f in range(FB)]
            for c, src in enumerate(srcs):
                if c == 2 * KD:
                    pe.wait_ge(idf_ready, 1)
                    pe.transpose(ps_t[1][:, 0:NT], ids_f, ident[0:NT, 0:NT]).then_inc(idt_ps, 1)
                ins = pe.matmul(ps_s[:, 0, c * NT:(c + 1) * NT], src, oh_e[:, 0:NT], start=True, stop=True)
            ins.then_inc(cols_ps, 1)
            pe.wait_ge(b2_split, 1)
            pe.wait_ge(cols_ready, 1)
            pe.wait_ge(idt_ready, 1)

            pe.wait_ge(w_split, 2 * B)

            def expert(t):
                return pe.value_load(tile_e[0:1, bass.ds(t, 1)], min_val=0, max_val=E - 1)

            def x_turn(ring, n, n_rec):
                pe.wait_ge(g_in[ring], n_rec)
                if not (isinstance(n, int) and n == 0):
                    pe.wait_ge(xg_ready, n)
                for k in range(KD):
                    ins = pe.transpose(ps_u[2][:, k * P:(k + 1) * P], g_rec[ring][:, k * P:(k + 1) * P], ident[:, :])
                ins.then_inc(xgT_ps, 1)

            def hidden(n, n_w1, par):
                pe.wait_ge(w1c_in[par], n_w1)
                pe.wait_ge(xgT_split, n)
                for f in range(FB):
                    ins = split_mm(ps_h[par][f // 4][:, (f % 4) * P:(f % 4 + 1) * P],
                                   [[w[:, k * FF + f * P:k * FF + (f + 1) * P] for w in w1c[par]] for k in range(KD)],
                                   [[xgT[a][:, k, :] for a in range(2)] for k in range(KD)])
                    if f % 4 == 3:
                        ins.then_inc(hid_ps, 1)

            def project_out(t, n, par, free):
                e = expert(t)
                if free is not None:
                    pe.wait_ge(y2_out, free)
                pe.wait_ge(hid_split, n)
                oh = oh_eh[:, bass.ds(t, 1)].broadcast_to([LOW + E, P])
                pe.matmul(ps_u[par][:, 0:D], oh, b2_s, start=True, stop=False)
                split = [(f, a, b) for f in range(FB) for a, b in PAIRS]
                for f, a, b in split:
                    ins = pe.matmul(ps_u[par][:, 0:D], hid[a][par][:, f, :], (w2h, w2l)[b][:, e, f * D:(f + 1) * D],
                                    start=False, stop=((f, a, b) == split[-1]))
                ins.then_inc(y2_ps, 1)

            def tile_step(t, it=None):
                r = 0 if it is None else it
                if t + 1 < TILES:
                    x_turn((t + 1) % 4, r * 4 + (t + 1), r * 16 + 16 * ((t + 1) // 4 + 1))
                if t < TILES:
                    hidden(r * 4 + (t + 1), r * 64 + 32 * (t // 2 + 1), t % 2)
                if t >= 1:
                    project_out(r * 4 + (t - 1), r * 8 + 2 * t, (t - 1) % 2, r * 4 + (t - 2) if t > 2 else None)

            x_turn(0, 0, 16)
            keep_warm(5, aT[0][:, :, :].rearrange("p n t -> p (n t)"), ps_o)
            for t in range(T_FROM):
                tile_step(t)
            with pe.Fori(0, (T_TO - T_FROM) // 4) as it:
                for t in range(T_FROM, T_FROM + 4):
                    tile_step(t, it)
            for t in range(T_TO, TILES + 1):
                tile_step(t)


_INS = ['x', 'ctx_1024', 'L0_xattn_gamma_x', 'L0_xattn_beta_x', 'L0_xattn_gamma_l', 'L0_xattn_beta_l',
        'L0_xattn_Wq', 'L0_xattn_Wkv', 'L0_xattn_Wo', 'L0_ffn_centroids', 'L0_ffn_ln_g', 'L0_ffn_ln_b',
        'L0_ffn_w1', 'L0_ffn_b1', 'L0_ffn_w2', 'L0_ffn_b2']


def _constants(tokens, experts):
    import numpy as np
    p = 128
    dh, base = 64, 10000.0
    inv = (np.float32(1.0) / np.float32(base) ** (np.arange(0, dh, 2, dtype=np.float32) / np.float32(dh)))
    ang = np.arange(p, dtype=np.float32)[:, None] * inv[None, :].astype(np.float32)
    ang = np.concatenate([ang, ang, ang, ang], axis=1)
    cos = (np.cos(ang).T / 64.0).astype(np.float32)
    sin = (np.sin(ang).T / 64.0).astype(np.float32)
    sin[np.arange(p) % dh < dh // 2] *= -1.0
    tri = np.zeros((p, 2, p), np.float16)
    tri[:, 0, :] = np.triu(np.ones((p, p)))
    tri[:, 1, :] = 1.0
    cols = np.zeros((p, 16), np.float32)
    cols[:, 0:3], cols[:, 3:6], cols[:, 6:9], cols[:, 9:12] = 1e-5, -0.5, 0.5, -1.0
    cols[:, 12] = np.arange(p)
    nt = tokens // p + experts
    tabs = np.concatenate([np.arange(16) * float(p), np.tril(np.ones((experts, experts))).reshape(-1), [0.0]])
    basee = np.stack([np.arange(experts) * float(tokens) - 1.0, np.arange(experts)])
    places = experts * tokens // p + nt
    empty = np.full((p, places), 2 * tokens, np.int32)
    return {"rope_cos": np.ascontiguousarray(cos), "rope_sin": np.ascontiguousarray(sin),
            "ident": np.eye(p, dtype=np.float32), "tri": tri, "cols": cols,
            "tabs": tabs.astype(np.float32), "basee": basee.astype(np.float32),
            "ids": np.arange(p, dtype=np.int32)[:, None], "empty": empty}


def kernel(**inputs):
    import numpy as _np
    import concourse.bacc as _bacc
    from concourse import mybir as _mybir
    from concourse.bass_utils import run_bass_kernel_spmd as _run

    nc = _bacc.Bacc("TRN2", target_bir_lowering=False, num_devices=1)
    arrays, args = {}, []
    shape = inputs['x'].shape
    given = [(n, _np.ascontiguousarray(inputs[n])) for n in _INS]
    given += list(_constants(shape[0] * shape[1], inputs['L0_ffn_w1'].shape[0]).items())
    for name, a in given:
        arrays[f"in_{name}_dram"] = a
        args.append(nc.dram_tensor(f"in_{name}_dram", a.shape, _mybir.dt.from_np(a.dtype), kind="ExternalInput").ap())
    args.append(nc.dram_tensor("out_0_dram", shape, _mybir.dt.float32, kind="ExternalOutput").ap())
    xattn_moe_kernel(nc, *args)
    r = _run(nc, [arrays], core_ids=[0])
    return r.results[0]["out_0_dram"]
```
